# Optimizing a Trainium2 kernel written in Bass

```python
import numpy as np
import jax
import jax.numpy as jnp

def _softmax(x, axis=-1):
    return jax.nn.softmax(x, axis=axis)

def _gelu(x):
    return jax.nn.gelu(x, approximate=True)

def _silu(x):
    return jax.nn.silu(x)

def _sigmoid(x):
    return jax.nn.sigmoid(x)

def _layernorm(x, axis=-1, eps=1e-05):
    m = jnp.mean(x, axis=axis, keepdims=True)
    v = jnp.var(x, axis=axis, keepdims=True)
    return (x - m) / jnp.sqrt(v + eps)

def _scatter_add(tgt, idx, src, axis=0):
    return tgt.at[idx].add(src)

def _segment_sum(src, seg, n):
    return jax.ops.segment_sum(src, seg, n)
kernel_name = 'mk_adaln_d1_jaxref_r4_555c22'

def setup_inputs(seed: int=0):
    np.random.seed(seed)
    _w = jnp.asarray

    def _L0_attn_setup():
        import jax, jax.numpy as jnp
        import numpy as np
        N_HEADS = 16
        D_HEAD = 128
        D_MODEL = 512
        MAXLEN = 512
        key = jax.random.key(seed)
        ks = jax.random.split(key, 9)
        b, t = (2, 512)
        hd = N_HEADS * D_HEAD
        init = 0.02
        return {'x': jax.random.normal(ks[0], (b, t, D_MODEL), dtype=jnp.float32), 'Wq': jax.random.normal(ks[1], (D_MODEL, hd), dtype=jnp.float32) * init, 'bq': jnp.zeros((hd,), dtype=jnp.float32), 'Wk': jax.random.normal(ks[2], (D_MODEL, hd), dtype=jnp.float32) * init, 'bk': jnp.zeros((hd,), dtype=jnp.float32), 'Wv': jax.random.normal(ks[3], (D_MODEL, hd), dtype=jnp.float32) * init, 'bv': jnp.zeros((hd,), dtype=jnp.float32), 'Wo': jax.random.normal(ks[4], (hd, D_MODEL), dtype=jnp.float32) * init, 'bo': jnp.zeros((D_MODEL,), dtype=jnp.float32)}
    _L0_attn_in = _L0_attn_setup()

    def _L0_ffn_setup():
        import jax, jax.numpy as jnp
        import numpy as np
        B, S, H = (2, 256, 512)
        E, K, F = (8, 2, 352)
        N_SHARED = 2
        FS = F * N_SHARED
        ROUTED_SCALE = 1.0

        def _swiglu_mlp(x, wg, wu, wd):
            return jax.nn.silu(x @ wg.T) * (x @ wu.T) @ wd.T
        key = jax.random.key(seed)
        ks = jax.random.split(key, 8)

        def w(k, shape, fan_in):
            return jax.random.normal(k, shape, jnp.float32) * (1.0 / np.sqrt(fan_in))
        return {'hidden_states': jax.random.normal(ks[0], (B, S, H), jnp.float32), 'gate_weight': w(ks[1], (E, H), H), 'w_gate': w(ks[2], (E, F, H), H), 'w_up': w(ks[3], (E, F, H), H), 'w_down': w(ks[4], (E, H, F), F), 'sw_gate': w(ks[5], (FS, H), H), 'sw_up': w(ks[6], (FS, H), H), 'sw_down': w(ks[7], (H, FS), FS)}
    _L0_ffn_in = _L0_ffn_setup()
    _L0_c = _w((lambda *s: np.random.randn(*s).astype(np.float32) * 0.05)(4, 512))
    _L0_wmod = _w((lambda *s: np.random.randn(*s).astype(np.float32) * 0.05)(512, 6 * 512) * 512 ** (-0.5))
    _d = {'L0_attn_x': _L0_attn_in['x'], 'L0_attn_Wq': _L0_attn_in['Wq'], 'L0_attn_bq': _L0_attn_in['bq'], 'L0_attn_Wk': _L0_attn_in['Wk'], 'L0_attn_bk': _L0_attn_in['bk'], 'L0_attn_Wv': _L0_attn_in['Wv'], 'L0_attn_bv': _L0_attn_in['bv'], 'L0_attn_Wo': _L0_attn_in['Wo'], 'L0_attn_bo': _L0_attn_in['bo'], 'L0_ffn_gate_weight': _L0_ffn_in['gate_weight'], 'L0_ffn_w_gate': _L0_ffn_in['w_gate'], 'L0_ffn_w_up': _L0_ffn_in['w_up'], 'L0_ffn_w_down': _L0_ffn_in['w_down'], 'L0_ffn_sw_gate': _L0_ffn_in['sw_gate'], 'L0_ffn_sw_up': _L0_ffn_in['sw_up'], 'L0_ffn_sw_down': _L0_ffn_in['sw_down'], 'L0_c': _L0_c, 'L0_wmod': _L0_wmod}
    _x0 = _d['L0_attn_x']
    _d['L0_attn_x'] = jax.random.normal(jax.random.fold_in(jax.random.key(seed), 1), (4, 512, 512), dtype=_x0.dtype)
    del _x0
    return _d

def reference(L0_attn_x, L0_attn_Wq, L0_attn_bq, L0_attn_Wk, L0_attn_bk, L0_attn_Wv, L0_attn_bv, L0_attn_Wo, L0_attn_bo, L0_ffn_gate_weight, L0_ffn_w_gate, L0_ffn_w_up, L0_ffn_w_down, L0_ffn_sw_gate, L0_ffn_sw_up, L0_ffn_sw_down, L0_c, L0_wmod):

    def _L0_attn_ref(x, Wq, bq, Wk, bk, Wv, bv, Wo, bo):
        import jax, jax.numpy as jnp
        import numpy as np
        N_HEADS = 16
        D_HEAD = 128
        D_MODEL = 512
        MAXLEN = 512
        b, t, _ = x.shape
        h, dh = (N_HEADS, D_HEAD)
        scale = 1.0 / np.sqrt(dh).astype(np.float32)
        q = (x @ Wq + bq).reshape(b, h, t, dh)
        k = (x @ Wk + bk).reshape(b, t, h, dh).transpose(0, 2, 3, 1)
        v = (x @ Wv + bv).reshape(b, t, h, dh).transpose(0, 2, 1, 3)
        logits = jnp.einsum('bhtd,bhds->bhts', q, k) * scale
        mask = jnp.triu(jnp.full((t, t), -jnp.inf, dtype=x.dtype), k=1)
        weights = jax.nn.softmax(logits + mask, axis=-1)
        out = jnp.einsum('bhts,bhsd->bhtd', weights, v)
        out = out.transpose(0, 2, 1, 3).reshape(b, t, h * dh)
        return out @ Wo + bo

    def _L0_ffn_ref(hidden_states, gate_weight, w_gate, w_up, w_down, sw_gate, sw_up, sw_down):
        import jax, jax.numpy as jnp
        import numpy as np
        B, S, H = (2, 256, 512)
        E, K, F = (8, 2, 352)
        N_SHARED = 2
        FS = F * N_SHARED
        ROUTED_SCALE = 1.0

        def _swiglu_mlp(x, wg, wu, wd):
            return jax.nn.silu(x @ wg.T) * (x @ wu.T) @ wd.T
        b, s, h = hidden_states.shape
        x = hidden_states.reshape(-1, h)
        T = x.shape[0]
        logits = x.astype(jnp.float32) @ gate_weight.astype(jnp.float32).T
        scores = jax.nn.softmax(logits, axis=-1)
        topk_w, topk_idx = jax.lax.top_k(scores, K)
        topk_w = topk_w / (jnp.sum(topk_w, axis=-1, keepdims=True) + 1e-20)
        topk_w = topk_w * ROUTED_SCALE
        cw = jnp.zeros((T, E), jnp.float32).at[jnp.arange(T)[:, None], topk_idx].add(topk_w)
        g = jax.nn.silu(jnp.einsum('th,efh->tef', x, w_gate)) * jnp.einsum('th,efh->tef', x, w_up)
        expert_out = jnp.einsum('tef,ehf->teh', g, w_down)
        y = jnp.einsum('te,teh->th', cw, expert_out).reshape(b, s, h)
        y = y + _swiglu_mlp(x, sw_gate, sw_up, sw_down).reshape(b, s, h)
        return y
    x = L0_attn_x
    mod = (_silu(L0_c) @ L0_wmod).reshape(L0_c.shape[0], 6, 1, -1)
    sa, ca, ga, sb, cb, gb = (mod[:, 0], mod[:, 1], mod[:, 2], mod[:, 3], mod[:, 4], mod[:, 5])
    ga = (2 * (ga >= 0) - 1) * jnp.maximum(jnp.abs(ga), 0.25)
    gb = (2 * (gb >= 0) - 1) * jnp.maximum(jnp.abs(gb), 0.25)
    h = _layernorm(x, axis=-1) * (1 + ca) + sa
    x = x + ga * _L0_attn_ref(h, L0_attn_Wq, L0_attn_bq, L0_attn_Wk, L0_attn_bk, L0_attn_Wv, L0_attn_bv, L0_attn_Wo, L0_attn_bo)
    h = _layernorm(x, axis=-1) * (1 + cb) + sb
    x = x + gb * _L0_ffn_ref(h, L0_ffn_gate_weight, L0_ffn_w_gate, L0_ffn_w_up, L0_ffn_w_down, L0_ffn_sw_gate, L0_ffn_sw_up, L0_ffn_sw_down)
    return x

_drawn_inputs = setup_inputs


def setup_inputs(seed=0):
    import zlib

    import numpy as np

    out = dict(_drawn_inputs(seed))
    spreads = {'L0_attn_bq': (0.0, 0.8),
     'L0_attn_bk': (0.0, 0.8),
     'L0_attn_bv': (0.0, 0.309),
     'L0_attn_bo': (0.0, 0.29)}
    factors = {'L0_attn_Wq': 8.0, 'L0_attn_Wk': 8.0, 'L0_attn_Wv': 4.167}
    for name, (base, spread) in spreads.items():
        noise = np.random.default_rng([zlib.crc32(name.encode()), seed]).standard_normal(out[name].shape)
        drawn = base * np.exp(spread * noise) if base else spread * noise
        out[name] = jnp.asarray(drawn.astype(out[name].dtype))
    for name, factor in factors.items():
        out[name] = (out[name] * factor).astype(out[name].dtype)
    return out
```

```python
from contextlib import ExitStack

import numpy as np
import concourse.bass as bass
from concourse import mybir

F32 = mybir.dt.float32
F32R = mybir.dt.float32r
I32 = mybir.dt.int32
U32 = mybir.dt.uint32
ALU = mybir.AluOpType
ACT = mybir.ActivationFunctionType
AX_X = mybir.AxisListType.X

P = 128
D = 512
DC = D // P
B = 4
T = 512
TT = T // P
NT = B * TT
N = B * T
H = 16
HP = H // 2
HD = H * P
NIT = HP * B
TRI = TT * (TT + 1) // 2 * P
E = 8
F = 352
FC = 3
FK = [P, P, F - 2 * P]
NX = E + 2
WG, WU, WD = 0, DC * F, 2 * DC * F
WE = 2 * DC * F + FC * D
NCH = 4 * NIT
CH = NX * WE // NCH
NSLOT = 2 * NT + E
NJ = 2 * NT + NSLOT
SCALE = float(1.0 / np.sqrt(np.float32(P)))
MASKED = -(2.0 ** 100)
EPS = 1e-5
assert CH * NCH == NX * WE and NSLOT % 2 == 0 and F == sum(FK)

ROW_AT = [r * (r + 1) // 2 * P for r in range(TT)]
PT_GROUPS = [[(0, 0)], [(1, 0), (3, (TT - 1) * P)], [(2, 0)]]
PT_AT = [0, T, 2 * T]
PT_LEN = [T, T, 2 * P]


COEFS = [("iota", NT * E), ("keep", E * NT), ("edges", E * NT), ("one_e", E), ("tiles", NSLOT * E),
         ("parity", E), ("even", E), ("odd", E), ("next", E), ("load_0", E), ("load_1", E)]
COEF_AT = {name: sum(w for _, w in COEFS[:i]) for i, (name, _) in enumerate(COEFS)}
COEF_W = sum(w for _, w in COEFS)


def coefficients():
    e, t, j = np.arange(E), np.arange(NT), np.arange(NSLOT)
    rows = {
        "iota": np.tile(e - E, NT),
        "keep": np.tile(t > 0, E),
        "edges": np.tile(P * t, E),
        "one_e": np.ones(E),
        "tiles": np.repeat(j, E),
        "parity": np.where(e == 0, 0, np.where(e % 2 == 1, 1, -1)),
        "even": 32 * ((e % 2 == 0) + (e == 0)),
        "odd": 32 * ((e % 2 == 1) + (e == 0)),
        "next": np.ones(E),
        "load_0": (e < E - 1) & (e % 2 == 1),
        "load_1": (e < E - 1) & (e % 2 == 0),
    }
    flat = np.concatenate([np.asarray(rows[name], np.float32) for name, _ in COEFS])
    return np.ascontiguousarray(np.broadcast_to(flat, (P, COEF_W)))


def adaln_layer(nc, x, wq, bq, wk, bk, wv, bv, wo, bo, gate_t, wexp, c_t, wmod, ident_in, causal_in,
                tri_in, coef_in, out):
    ctx = ExitStack()
    with ctx:
        def sem(name):
            return ctx.enter_context(nc.semaphore(name))

        def sbuf(scope, name, shape, dt=F32):
            return scope.enter_context(nc.sbuf_tensor(name, shape, dt))

        def dram(name, shape, dt=F32):
            return nc.dram_tensor(name, shape, dt, kind="Internal").ap()

        mod_d = dram("mod_rows", (B, 6 * D))
        q_d = dram("q_transposed", (B, H, P, T))
        wx_hi_d = dram("experts_hi", (P, NX * WE))
        wx_lo_d = dram("experts_lo", (P, NX * WE))
        rows_d = dram("ffn_rows", (N + NSLOT * P, D))
        y_d = dram("slot_results", (NSLOT * P, D))

        bank = [ctx.enter_context(nc.psum_tensor(f"bank{i}", [P, T], F32)) for i in range(8)]

        ident = sbuf(ctx, "ident", [P, P])
        ident_r = sbuf(ctx, "ident_r", [P, P], F32R)
        causal = sbuf(ctx, "causal", [P, P])
        causal_r = sbuf(ctx, "causal_r", [P, P], F32R)
        bq_c = sbuf(ctx, "bq_c", [P, H])
        bk_c = sbuf(ctx, "bk_c", [P, H])
        bv_c = sbuf(ctx, "bv_c", [P, H])
        modc = sbuf(ctx, "modc", [P, 2, DC, B])
        zero = sbuf(ctx, "zero", [P, D])
        acc = sbuf(ctx, "acc", [P, NT, D])
        mh = sbuf(ctx, "minus_half", [P, TT])
        stat = sbuf(ctx, "stat", [P, TT, 6])
        mv = sbuf(ctx, "mean_var", [P, TT, 2])
        ve = sbuf(ctx, "var_eps", [P, TT])
        rs0 = sbuf(ctx, "rstd_seed", [P, TT])
        nt1 = sbuf(ctx, "newton1", [P, TT])
        nt2 = sbuf(ctx, "newton2", [P, TT])
        rstd = sbuf(ctx, "rstd", [P, TT])
        acc_cols = acc[:, :, :].rearrange("p t d -> p (t d)")
        stage = [acc_cols[:, s * DC * D:(s + 1) * DC * D].rearrange("p (c n) -> p c n", c=DC) for s in range(3)]
        x_in = acc_cols[:, 3 * DC * D:4 * DC * D].rearrange("p (i n) -> p i n", i=TT)

        s12 = ExitStack()
        h_hi = sbuf(s12, "h_hi", [P, DC, N], F32R)
        h_lo = sbuf(s12, "h_lo", [P, DC, N], F32R)
        wk_raw = sbuf(s12, "wk_raw", [P, DC, 2 * P])
        wv_raw = sbuf(s12, "wv_raw", [P, DC, 2 * P])
        wo_raw = sbuf(s12, "wo_raw", [P, 2, D])

        s1 = ExitStack()
        wq_hi = sbuf(s1, "wq_hi", [P, DC, HD], F32R)
        wq_lo = sbuf(s1, "wq_lo", [P, DC, HD], F32R)
        q_out = sbuf(s1, "q_out", [P, 4, T])
        h_full = sbuf(s1, "h_full", [P, 2, DC, P])
        c_in = sbuf(s1, "c_in", [P, DC, B])
        c_silu = sbuf(s1, "c_silu", [P, DC, B])
        mod_row = sbuf(s1, "mod_row", [B, 2, D])
        mod_a = sbuf(s1, "mod_a", [B, D])
        mod_s = sbuf(s1, "mod_s", [B, D])
        s1.close()

        s2 = ExitStack()
        wk_hi = sbuf(s2, "wk_hi", [P, DC, 2 * P], F32R)
        wk_lo = sbuf(s2, "wk_lo", [P, DC, 2 * P], F32R)
        wv_hi = sbuf(s2, "wv_hi", [P, DC, 2 * P], F32R)
        wv_lo = sbuf(s2, "wv_lo", [P, DC, 2 * P], F32R)
        wo_hi = sbuf(s2, "wo_hi", [P, 2, D], F32R)
        wo_lo = sbuf(s2, "wo_lo", [P, 2, D], F32R)
        k_hi = sbuf(s2, "k_hi", [P, 2, T], F32R)
        k_lo = sbuf(s2, "k_lo", [P, 2, T], F32R)
        v_hi = sbuf(s2, "v_hi", [P, TT, 2 * P], F32R)
        v_lo = sbuf(s2, "v_lo", [P, TT, 2 * P], F32R)
        o_hi = sbuf(s2, "o_hi", [P, 2, T], F32R)
        o_lo = sbuf(s2, "o_lo", [P, 2, T], F32R)
        q_raw = sbuf(s2, "q_raw", [P, H, 64])
        q_hi = sbuf(s2, "q_hi", [P, 2, T], F32R)
        q_lo = sbuf(s2, "q_lo", [P, 2, T], F32R)
        prob = sbuf(s2, "prob", [P, 2, TRI])
        pt_hi = sbuf(s2, "pt_hi", [P, TRI], F32R)
        pt_lo = sbuf(s2, "pt_lo", [P, TRI], F32R)
        row_max = sbuf(s2, "row_max", [P, 2, TT])
        neg_max = sbuf(s2, "neg_max", [P, 2, TT])
        row_sum = sbuf(s2, "row_sum", [P, 2, TT])
        row_inv = sbuf(s2, "row_inv", [P, 2, TT])
        ch_raw = sbuf(s2, "ch_raw", [P, 2, CH])
        ch_hi = sbuf(s2, "ch_hi", [P, 2, CH], F32R)
        ch_lo = sbuf(s2, "ch_lo", [P, 2, CH], F32R)
        s2.close()
        s12.close()

        s3 = ExitStack()
        w_hi = sbuf(s3, "w_hi", [P, 2 * WE], F32R)
        w_lo = sbuf(s3, "w_lo", [P, 2 * WE], F32R)
        ga_b = sbuf(s3, "ga_b", [P, B, D])
        cb_b = sbuf(s3, "cb_b", [P, B, D])
        sb_b = sbuf(s3, "sb_b", [P, B, D])
        gb_b = sbuf(s3, "gb_b", [P, B, D])
        xr = sbuf(s3, "xr", [P, 2, D])
        h2 = sbuf(s3, "h2", [P, 2, D])
        xin = sbuf(s3, "xin", [P, 2, D])
        xt_hi = sbuf(s3, "xt_hi", [P, 2, DC, P], F32R)
        xt_lo = sbuf(s3, "xt_lo", [P, 2, DC, P], F32R)
        gate_s = sbuf(s3, "gate_s", [P, 2, F])
        h_mid = sbuf(s3, "h_mid", [P, 2, F])
        ht_hi = sbuf(s3, "ht_hi", [P, FC, P], F32R)
        ht_lo = sbuf(s3, "ht_lo", [P, FC, P], F32R)
        y_sb = sbuf(s3, "y_sb", [P, 2, D])
        bo_b = sbuf(s3, "bo_b", [P, D])
        g_raw = sbuf(s3, "g_raw", [P, DC, E])
        g_hi = sbuf(s3, "g_hi", [P, DC, E], F32R)
        g_lo = sbuf(s3, "g_lo", [P, DC, E], F32R)
        tri = sbuf(s3, "tri", [P, P])
        ones = sbuf(s3, "ones", [P, P])
        coef = sbuf(s3, "coef", [P, COEF_W])
        lg = sbuf(s3, "lg", [P, NT, E])
        sc = sbuf(s3, "sc", [P, NT, E])
        ra = sbuf(s3, "ra", [P, NT, E])
        rb = sbuf(s3, "rb", [P, NT, E])
        oh1 = sbuf(s3, "oh1", [P, NT, E])
        oh2 = sbuf(s3, "oh2", [P, NT, E])
        hot = sbuf(s3, "hot", [P, NT, E])
        slot_base = sbuf(s3, "slot_base", [P, NT, E])
        cnt_et = sbuf(s3, "cnt_et", [P, E, NT])
        cum_et = sbuf(s3, "cum_et", [P, E, NT])
        over = sbuf(s3, "over", [P, E, NT])
        r1 = sbuf(s3, "r1", [P, 8, NT])
        e1 = sbuf(s3, "e1", [P, 4, E])
        top_w = sbuf(s3, "top_w", [P, 2, NT])
        pos_i = sbuf(s3, "pos_i", [P, 2, NT], U32)
        pos_r = sbuf(s3, "pos_r", [P, 2, NT], U32)
        j_le = sbuf(s3, "j_le", [P, NSLOT, E])
        j_eq = sbuf(s3, "j_eq", [P, NSLOT, E])
        j_t = sbuf(s3, "j_t", [P, NSLOT, E])
        j_f = sbuf(s3, "j_f", [P, 6, NSLOT])
        tab = sbuf(s3, "tab", [P, 6, NSLOT], I32)
        yg = sbuf(s3, "yg", [P, 2, 2, D])
        s3.close()

        def cf(name, width, *dims):
            a = coef[:, COEF_AT[name]:COEF_AT[name] + width]
            return a.rearrange(*dims[0:1], **dims[1]) if dims else a

        const_ld = sem("const_ld")
        stage_ld = [sem(f"stage_ld{s}") for s in range(3)]
        x_ld = sem("x_ld")
        silu_c = sem("silu_c")
        const_r = sem("const_r")
        mod_full = sem("mod_full")
        mod_ev = sem("mod_ev")
        mod_st = [sem("mod_st0"), sem("mod_st1")]
        modt_full = sem("modt_full")
        modc_ok = sem("modc_ok")
        wq_hi_ok = sem("wq_hi_ok")
        wq_ok = sem("wq_ok")
        dchain = sem("dve_chain")
        mh_ok = sem("minus_half_ok")
        split_hi = sem("split_hi")
        ln_chain = sem("ln_chain")
        ln_var = sem("ln_var")
        ln_seed = sem("ln_seed")
        xn_ok = sem("xn_ok")
        tx_full = sem("tx_full")
        hf_ok = sem("h_full_ok")
        hhi_ok = sem("h_hi_ok")
        hlo_ok = sem("h_lo_ok")
        q_full = sem("q_full")
        q_ev = sem("q_ev")
        q_st = [sem(f"q_st{s}") for s in range(4)]
        zero_ok = sem("zero_ok")
        zero_st = sem("zero_st")
        wk_ld = sem("wk_ld")
        wv_ld = sem("wv_ld")
        wo_ld = sem("wo_ld")
        wk_ok = sem("wk_ok")
        wv_ok = sem("wv_ok")
        wo_ok = sem("wo_ok")
        acc_ok = sem("acc_ok")
        q_ld = sem("q_ld")
        q_ok = sem("q_split")
        k_full = sem("k_full")
        k_hi_ok = sem("k_hi_ok")
        k_ok = sem("k_ok")
        v_full = sem("v_full")
        v_hi_ok = sem("v_hi_ok")
        v_ok = sem("v_ok")
        s_full = sem("s_full")
        s_max = sem("s_max")
        s_neg = sem("s_neg")
        s_exp = sem("s_exp")
        inv_ok = sem("inv_ok")
        p_ok = sem("p_ok")
        pt_full = sem("pt_full")
        pt_hi_ok = sem("pt_hi_ok")
        pt_ok = sem("pt_ok")
        o_full = sem("o_full")
        o_hi_ok = sem("o_hi_ok")
        o_ok = sem("o_ok")
        wo_full = sem("wo_full")
        wo_add = sem("wo_add")
        ch_ld = [sem("ch_ld0"), sem("ch_ld1")]
        ch_ok = sem("ch_ok")
        ch_st = [sem("ch_st0"), sem("ch_st1")]
        c3_ld = sem("stage3_constants")
        xr_ld = [sem("xr_ld0"), sem("xr_ld1")]
        x1_ok = sem("x1_ok")
        c_var = sem("c_var")
        c_seed = sem("c_seed")
        c_xn = sem("c_xn")
        c_chain = sem("c_chain")
        h2_scaled = sem("h2_scaled")
        g_hi_ok = sem("g_hi_ok")
        h2_ok = sem("h2_ok")
        h2_st = [sem("h2_st0"), sem("h2_st1")]
        g_ok = sem("g_ok")
        ones_ok = sem("ones_ok")
        w_ld = [sem("w_ld_even"), sem("w_ld_odd")]
        xin_ld = [sem("xin_ld0"), sem("xin_ld1")]
        xt_full = sem("xt_full")
        xt_hi_ok = sem("xt_hi_ok")
        xt_ok = sem("xt_ok")
        gt_full = sem("gate_full")
        up_full = sem("up_full")
        silu_ok = sem("silu_ok")
        mid_ok = sem("mid_ok")
        ht_full = sem("ht_full")
        ht_hi_ok = sem("ht_hi_ok")
        ht_ok = sem("ht_ok")
        y_full = sem("y_full")
        y_gb = sem("y_gb")
        y_add = sem("y_add")
        y_ev = sem("y_ev")
        y_st = [sem("y_st0"), sem("y_st1")]
        lg_full = sem("lg_full")
        lg_ok = sem("lg_ok")
        rt_sub = sem("rt_sub")
        rt_exp = sem("rt_exp")
        rt_hot = sem("rt_hot")
        rt_cnt = sem("rt_cnt")
        pos_ok = sem("pos_ok")
        tab_ok = sem("tab_ok")
        sc_ld = [sem("sc_ld0"), sem("sc_ld1")]
        sc_st = [sem("sc_st0"), sem("sc_st1")]
        g_ld = [sem("g_ld0"), sem("g_ld1")]
        f_w1 = sem("f_w1")
        f_w2 = sem("f_w2")
        f_gb = sem("f_gb")
        f_ok = sem("f_ok")
        out_st = [sem("out_st0"), sem("out_st1")]

        block = ctx.enter_context(nc.Block())

        def wait_apart(eng, *waits):
            waits = [(s, v if isinstance(v, int) else eng.to_reg(v)) for s, v in waits]
            eng.wait_ge(const_ld, 6 * 16)
            for s, v in waits:
                eng.wait_ge(s, v)

        def walk_steps(eng, step):
            step(0, 0, True, False)
            with eng.Fori(0, HP - 1) as p:
                for b in range(1, B):
                    step(p, b, False, False)
                step(p + 1, 0, False, False)
            for b in range(1, B):
                step(HP - 1, b, False, b == B - 1)

        x_t = x.rearrange("(t p) d -> p t d", p=P)
        wq_v = wq.rearrange("(c p) n -> p c n", p=P)
        wk_v = wk.rearrange("(c p) n -> p c n", p=P)
        wv_v = wv.rearrange("(c p) n -> p c n", p=P)
        wo_v = wo.rearrange("(h p) n -> p h n", p=P)
        wmod_v = wmod.rearrange("(c p) n -> p c n", p=P)
        out_t = out.rearrange("(t p) d -> p t d", p=P)
        rows_t = rows_d.rearrange("(t p) d -> p t d", p=P)
        y_t = y_d.rearrange("(t p) d -> p t d", p=P)
        q_v = q_d.rearrange("b j p t -> p b j t")

        loads = [("mod", 0), ("mod", 1)] + [("wq", g) for g in range(4)] + [("mod", m) for m in range(2, 6)]
        load_at = {what: i for i, what in enumerate(loads)}

        def stage1_over(eng):
            eng.wait_ge(q_full, B * H)
            eng.wait_ge(hlo_ok, NT)
            for s in q_st:
                eng.wait_ge(s, 16 * B * H // 4)
            for s in mod_st:
                eng.wait_ge(s, 3 * 16)

        @block.sync
        def _(sp):
            sp.dma_start(c_in[:, :, :], c_t.rearrange("(c p) b -> p c b", p=P)).then_inc(const_ld, 16)
            sp.dma_start(ident[:, :], ident_in).then_inc(const_ld, 16)
            sp.dma_start(causal[:, :], causal_in).then_inc(const_ld, 16)
            sp.dma_start(bq_c[:, :], bq).then_inc(const_ld, 16)
            sp.dma_start(bk_c[:, :], bk).then_inc(const_ld, 16)
            sp.dma_start(bv_c[:, :], bv).then_inc(const_ld, 16)
            sp.dma_start(x_in, x_t[:, 0:TT, :]).then_inc(x_ld, 16)
            for i, (kind, m) in enumerate(loads[:-1]):
                if i >= 3:
                    was, k = loads[i - 3]
                    if was == "mod":
                        sp.wait_ge(mod_full, k + 1)
                    else:
                        sp.wait_ge(wq_ok, k + 1)
                src = (wmod_v if kind == "mod" else wq_v)[:, :, m * D:(m + 1) * D]
                sp.dma_start(stage[i % 3], src).then_inc(stage_ld[i % 3], 16)
                if i == 5:
                    for r in range(2):
                        sp.wait_ge(mod_ev, r + 1)
                        sp.dma_start(mod_d[:, r * D:(r + 1) * D], mod_row[:, r, :]).then_inc(mod_st[r], 16)
            sp.wait_ge(zero_ok, 1)
            slots = rows_d[N:, :].rearrange("(a p) d -> p a d", p=P)
            for a in range(0, NSLOT, 8):
                sp.dma_start(slots[:, a:a + 8, :],
                             zero[:, :].unsqueeze(1).to_broadcast([P, 8, D])).then_inc(zero_st, 16)
            sp.dma_start(wk_raw[:, :, :], wk_v[:, :, 0:2 * P]).then_inc(wk_ld, 16)
            sp.dma_start(wv_raw[:, :, :], wv_v[:, :, 0:2 * P]).then_inc(wv_ld, 16)
            sp.dma_start(wo_raw[:, :, :], wo_v[:, 0:2, :]).then_inc(wo_ld, 16)

            def q_rows(b, more):
                if more:
                    sp.wait_ge(tx_full, b * TT + TT)
                    sp.dma_start(x_in, x_t[:, bass.ds((b + 1) * TT, TT), :]).then_inc(x_ld, 16)
                for j in range(H):
                    sp.wait_ge(q_ev, b * H + (j + 1))
                    sp.dma_start(q_v[:, bass.ds(b, 1), j, :], q_out[:, j % 4, :].unsqueeze(1))\
                      .then_inc(q_st[j % 4], 16)
                    if not more and j == H // 2:
                        store_mod(5)

            def store_mod(m):
                sp.wait_ge(mod_ev, m + 1)
                sp.dma_start(mod_d[:, m * D:(m + 1) * D], mod_row[:, m % 2, :]).then_inc(mod_st[m % 2], 16)

            with sp.Fori(0, B - 1) as b:
                q_rows(b, True)
            sp.wait_ge(mod_full, 3)
            i = len(loads) - 1
            sp.dma_start(stage[i % 3], wmod_v[:, :, 5 * D:6 * D]).then_inc(stage_ld[i % 3], 16)
            for m in range(2, 5):
                store_mod(m)
            q_rows(B - 1, False)

            stage1_over(sp)

            def load_q(p, b):
                sp.dma_start(q_raw[:, :, :], q_v[:, b, :, bass.ds(p * 64, 64)]).then_inc(q_ld, 16)

            load_q(0, 0)
            sp.wait_ge(acc_ok, 1)
            for s in range(2):
                sp.dma_start(ch_raw[:, s, :], wexp[:, s * CH:(s + 1) * CH]).then_inc(ch_ld[s], 16)

            def step(p, b, first, last):
                n = p * B + b
                if not last:
                    sp.wait_ge(q_ok, n * 2 + 2)
                    load_q(p if b < B - 1 else p + 1, (b + 1) % B)
                if b == 1 and not (isinstance(p, int) and p == HP - 1):
                    nxt = (p + 1) * 2 * P
                    sp.wait_ge(wk_ok, p + 1)
                    sp.dma_start(wk_raw[:, :, :], wk_v[:, :, bass.ds(nxt, 2 * P)]).then_inc(wk_ld, 16)
                    sp.wait_ge(wv_ok, p + 1)
                    sp.dma_start(wv_raw[:, :, :], wv_v[:, :, bass.ds(nxt, 2 * P)]).then_inc(wv_ld, 16)
                    sp.wait_ge(wo_ok, p + 1)
                    sp.dma_start(wo_raw[:, :, :], wo_v[:, bass.ds((p + 1) * 2, 2), :]).then_inc(wo_ld, 16)
                for q in range(4):
                    c, s = n * 4 + q, q % 2
                    sp.wait_ge(ch_ok, c + 1)
                    sp.dma_start(wx_hi_d[:, bass.ds(c * CH, CH)], ch_hi[:, s, :].bitcast(F32)).then_inc(ch_st[s], 16)
                    sp.dma_start(wx_lo_d[:, bass.ds(c * CH, CH)], ch_lo[:, s, :].bitcast(F32)).then_inc(ch_st[s], 16)
                    if not (last and q >= 2):
                        sp.dma_start(ch_raw[:, s, :], wexp[:, bass.ds((c + 2) * CH, CH)]).then_inc(ch_ld[s], 16)

            walk_steps(sp, step)

            sp.wait_ge(wo_add, NIT * TT)
            for s in range(2):
                sp.wait_ge(mod_st[s], 3 * 16)
                sp.wait_ge(ch_st[s], 16 * NCH)
            for i, dst in ((2, ga_b), (4, cb_b), (3, sb_b), (5, gb_b)):
                for b in range(B):
                    sp.dma_start(dst[:, b, :], mod_d[b:b + 1, i * D:(i + 1) * D].to_broadcast([P, D]))\
                      .then_inc(c3_ld, 16)
            sp.dma_start(g_raw[:, :, :], gate_t.rearrange("(c p) e -> p c e", p=P)).then_inc(c3_ld, 16)
            sp.dma_start(tri[:, :], tri_in).then_inc(c3_ld, 16)
            sp.dma_start(coef[:, :], coef_in).then_inc(c3_ld, 16)
            sp.dma_start(bo_b[:, :], bo.to_broadcast([P, D])).then_inc(c3_ld, 16)

            def load_xr(t, s):
                sp.dma_start(xr[:, s, :].unsqueeze(1), x_t[:, bass.ds(t, 1), :]).then_inc(xr_ld[s], 16)

            def load_w(e, s):
                sp.dma_start(w_hi[:, s * WE:(s + 1) * WE].bitcast(F32), wx_hi_d[:, e * WE:(e + 1) * WE]).then_inc(w_ld[s], 16)
                sp.dma_start(w_lo[:, s * WE:(s + 1) * WE].bitcast(F32), wx_lo_d[:, e * WE:(e + 1) * WE]).then_inc(w_ld[s], 16)

            load_xr(0, 0)
            load_xr(1, 1)
            load_w(E, 0)
            load_w(E + 1, 1)

            def c_tile(t, i, more):
                s = i % 2
                sp.wait_ge(h2_ok, t + 1)
                sp.dma_start(rows_t[:, bass.ds(t, 1), :], h2[:, s, :].unsqueeze(1)).then_inc(h2_st[s], 16)
                if more:
                    sp.wait_ge(x1_ok, t + 1)
                    load_xr(t + 2, s)

            def load_xin(tile, m, s):
                if not (isinstance(m, int) and m < 2):
                    sp.wait_ge(xt_full, m - 1)
                sp.dma_start(xin[:, s, :].unsqueeze(1), rows_t[:, bass.ds(tile, 1), :]).then_inc(xin_ld[s], 16)

            for t in range(TT):
                c_tile(t, t, True)
            sp.wait_ge(h2_st[0], 16)
            load_xin(0, 0, 0)

            def quad0(b, hidden):
                for i in range(TT):
                    n = b * TT + i
                    if hidden or i < TT - 1:
                        sp.wait_ge(h2_st[(i + 1) % 2], b * 32 + 16 * ((i + 1) // 2 + 1))
                    load_xin(n + 1 if (hidden or i < TT - 1) else 0, n + 1, (i + 1) % 2)
                    if hidden:
                        c_tile(n + TT, i, hidden == 1 or i < 2)

            quad0(0, 1)
            with sp.Fori(1, B - 2) as b:
                quad0(b, 1)
            quad0(B - 2, 2)
            quad0(B - 1, 0)
            def quad1(b, scatter, final):
                for i in range(TT):
                    n = b * TT + (NT + i)
                    if final and i == TT - 1:
                        for s in range(2):
                            sp.wait_ge(sc_st[s], 16 * NT)
                    load_xin(n + 1 - NT, n + 1, (i + 1) % 2)
                    if isinstance(b, int) and b == 0 and i == 0:
                        sp.wait_ge(y_full, NT)
                        load_w(0, 0)
                    if scatter:
                        for k in range(2):
                            t = (b - 1) * 2 * TT + (2 * i + k)
                            if not (isinstance(b, int) and b == 1 and i == 0):
                                sp.wait_ge(sc_st[k], (b - 1) * (TT * 32) + i * 32)
                            sp.dma_start(yg[:, 0, k, :].unsqueeze(1), rows_t[:, bass.ds(t, 1), :])\
                              .then_inc(sc_ld[k], 16)

            quad1(0, False, False)
            quad1(1, True, False)
            quad1(2, True, False)
            quad1(3, False, True)

            sp.wait_ge(tab_ok, 1)

            def routed(j, first, last):
                for k in range(2):
                    r = j * 2 + k
                    n = r + 2 * NT
                    if not (last and k == 1):
                        load_xin(r + (NT + 1), n + 1, (k + 1) % 2)
                    nxt = sp.value_load(tab[0:1, 3, bass.ds(r, 1)], min_val=1, max_val=E)
                    load = [sp.value_load(tab[0:1, 4 + s, bass.ds(r, 1)], min_val=0, max_val=1) for s in range(2)]
                    wait_apart(sp, (y_full, n))
                    for s in range(2):
                        with sp.If(load[s]):
                            sp.dma_start(w_hi[:, s * WE:(s + 1) * WE].bitcast(F32), wx_hi_d[:, bass.ds(nxt * WE, WE)])\
                              .then_inc(w_ld[s], 16)
                            sp.dma_start(w_lo[:, s * WE:(s + 1) * WE].bitcast(F32), wx_lo_d[:, bass.ds(nxt * WE, WE)])\
                              .then_inc(w_ld[s], 16)
                    if not (first and k == 0):
                        store_y(r - 1, (k + 1) % 2)

            def store_y(r, s):
                sp.wait_ge(y_ev, r + 1)
                sp.dma_start(y_t[:, bass.ds(r, 1), :], y_sb[:, s, :].unsqueeze(1)).then_inc(y_st[s], 16)

            routed(0, True, False)
            with sp.Fori(1, NSLOT // 2 - 1) as j:
                routed(j, False, False)
            routed(NSLOT // 2 - 1, False, True)
            store_y(NSLOT - 1, 1)

            for t in range(NT):
                sp.wait_ge(f_ok, t + 1)
                sp.dma_start(out_t[:, t, :], yg[:, 1, t % 2, :]).then_inc(out_st[t % 2], 16)
            for s in range(2):
                sp.wait_ge(out_st[s], 16 * NT // 2)
                sp.wait_ge(y_st[s], 16 * NSLOT // 2)
            sp.wait_ge(zero_st, 16 * (NSLOT // 8))

        @block.gpsimd
        def _(pool):
            pool.memset(zero[:, :], 0.0).then_inc(zero_ok, 1)
            pool.memset(mh[:, :], -0.5).then_inc(mh_ok, 1)
            pool.wait_ge(mh_ok, 1)

            def seed(b):
                pool.wait_ge(ln_var, b + 1)
                pool.tensor_tensor(rs0[:, :], ve[:, :], mh[:, :], ALU.pow).then_inc(ln_seed, 1)

            seed(0)
            with pool.Fori(0, B - 1) as b:
                seed(b + 1)

            stage1_over(pool)
            pool.memset(acc[:, :, :], 0.0).then_inc(acc_ok, 1)

            q_nat_hi = q_hi[:, :, :].rearrange("p h (r j) -> p h r j", j=H)
            q_nat_lo = q_lo[:, :, :].rearrange("p h (r j) -> p h r j", j=H)
            q_in = q_raw[:, :, :].rearrange("p j (h r) -> p h r j", h=2)

            def run(what, base):
                for k, (raw, hi, lo, waits, done) in enumerate(what):
                    wait_apart(pool, *waits)
                    pool.tensor_copy(hi, raw).then_inc(split_hi, 1)
                    pool.wait_ge(split_hi, base + (k + 1))
                    pool.tensor_tensor(lo, raw, hi.bitcast(F32), ALU.subtract).then_inc(done, 1)

            SPB = [7, 6, 7, 7]
            SPP = sum(SPB)

            def base_of(p, b):
                done = 4 + sum(SPB[:b])
                if isinstance(p, int) and p == HP - 1 and b == B - 1:
                    done -= 1
                return p * SPP + done

            run([
                (wk_raw[:, :, :], wk_hi[:, :, :], wk_lo[:, :, :], [(wk_ld, 16)], wk_ok),
                (q_in[:, 0], q_nat_hi[:, 0], q_nat_lo[:, 0], [(q_ld, 16)], q_ok),
                (q_in[:, 1], q_nat_hi[:, 1], q_nat_lo[:, 1], [], q_ok),
                (wv_raw[:, :, :], wv_hi[:, :, :], wv_lo[:, :, :], [(wv_ld, 16)], wv_ok)], 0)

            def step(p, b, first, last):
                n = p * B + b
                base = base_of(p, b)
                k = 0
                for h in range(2):
                    wait_apart(pool, (inv_ok, n * 2 + (h + 1)))
                    for r in range(TT):
                        part = prob[:, h, ROW_AT[r]:ROW_AT[r] + (r + 1) * P]
                        ins = pool.tensor_scalar(part, part, row_inv[:, h, r:r + 1], None, ALU.mult)
                    ins.then_inc(p_ok, 1)
                    if not last:
                        run([(q_in[:, h], q_nat_hi[:, h], q_nat_lo[:, h],
                                    [(q_ld, n * 16 + 32), (s_full, n * 8 + (4 * h + 4))], q_ok)], base + k)
                        k += 1
                for q in range(4):
                    c, s = n * 4 + q, q % 2
                    waits = [(ch_ld[s], n * 32 + (q // 2 + 1) * 16)]
                    if not (first and q < 2):
                        waits.append((ch_st[s], n * 64 + (q // 2) * 32))
                    run([(ch_raw[:, s, :], ch_hi[:, s, :], ch_lo[:, s, :], waits, ch_ok)], base + k)
                    k += 1
                at_end = isinstance(p, int) and p == HP - 1
                if b == 0:
                    waits = [(wo_ld, p * 16 + 16)]
                    if not first:
                        waits.append((wo_full, n * TT))
                    run([(wo_raw[:, :, :], wo_hi[:, :, :], wo_lo[:, :, :], waits, wo_ok)], base + k)
                    k += 1
                if b == 2 and not at_end:
                    run([(wk_raw[:, :, :], wk_hi[:, :, :], wk_lo[:, :, :],
                                [(wk_ld, p * 16 + 32), (k_full, n * 2 + 4)], wk_ok)], base + k)
                    k += 1
                if b == 3 and not at_end:
                    run([(wv_raw[:, :, :], wv_hi[:, :, :], wv_lo[:, :, :],
                                [(wv_ld, p * 16 + 32), (v_full, n * 2 + 2)], wv_ok)], base + k)
                    k += 1
                assert at_end or k == SPB[b]

            walk_steps(pool, step)

            pool.wait_ge(wo_add, NIT * TT)
            pool.memset(ones[:, :], 1.0).then_inc(ones_ok, 1)
            pool.wait_ge(c3_ld, 16 * (4 * B + 4))

            def c_tile(b, i, t):
                s = i % 2
                pool.wait_ge(c_var, t + 1)
                pool.tensor_tensor(rs0[:, s:s + 1], ve[:, s:s + 1], mh[:, s:s + 1], ALU.pow).then_inc(c_seed, 1)
                wait_apart(pool, (c_xn, t + 1))
                pool.tensor_tensor(h2[:, s, :].unsqueeze(1), h2[:, s, :].unsqueeze(1), cb_b[:, bass.ds(b, 1), :], ALU.mult)\
                    .then_inc(h2_scaled, 1)
                wait_apart(pool, (h2_scaled, t + 1))
                pool.tensor_tensor(h2[:, s, :].unsqueeze(1), h2[:, s, :].unsqueeze(1), sb_b[:, bass.ds(b, 1), :], ALU.add)\
                    .then_inc(h2_ok, 1)

            def add_y(t, n, s):
                wait_apart(pool, (y_gb, n + 1))
                pool.tensor_tensor(acc[:, bass.ds(t, 1), :], acc[:, bass.ds(t, 1), :], y_sb[:, s, :].unsqueeze(1),
                                   ALU.add).then_inc(y_add, 1)

            for t in range(TT):
                c_tile(0, t, t)

            def quad0(b, hidden, first):
                for i in range(TT):
                    n = b * TT + i
                    if hidden:
                        c_tile(b + 1, i, n + TT)
                    if not (first and i == 0):
                        add_y(n - 1, n - 1, (i + 1) % 2)

            quad0(0, True, True)
            with pool.Fori(1, B - 1) as b:
                quad0(b, True, False)
            quad0(B - 1, False, False)

            def scatter(t, k, count):
                pool.wait_ge(sc_ld[k], count)
                for c in range(2):
                    pool.indirect_dma_start(
                        out=rows_d, out_offset=bass.IndirectOffsetOnAxis(ap=pos_r[:, c, t:t + 1], axis=0),
                        in_=yg[:, 0, k, :], in_offset=None,
                        bounds_check=N + NSLOT * P - 1, oob_is_err=True).then_inc(sc_st[k], 16)

            for b in range(B):
                for i in range(TT):
                    n = NT + b * TT + i
                    add_y((n - 1) % NT, n - 1, (i + 1) % 2)
                    if b in (1, 2):
                        if b == 1 and i == 0:
                            pool.wait_ge(pos_ok, 1)
                            pool.wait_ge(zero_st, 16 * (NSLOT // 8))
                        for k in range(2):
                            t = (b - 1) * 2 * TT + 2 * i + k
                            scatter(t, k, 16 * (t // 2 + 1))
            add_y(NT - 1, 2 * NT - 1, 1)

            for s in range(2):
                pool.wait_ge(y_st[s], 16 * NSLOT // 2)

            def gather(t):
                s = t % 2
                for c in range(2):
                    pool.indirect_dma_start(
                        out=yg[:, c, s, :], out_offset=None, in_=y_d,
                        in_offset=bass.IndirectOffsetOnAxis(ap=pos_i[:, c, t:t + 1], axis=0),
                        bounds_check=NSLOT * P - 1, oob_is_err=True).then_inc(g_ld[s], 16)

            gather(0)
            gather(1)
            for t in range(NT):
                s = t % 2
                pool.wait_ge(f_gb, t + 1)
                pool.tensor_tensor(yg[:, 1, s, :], yg[:, 1, s, :], acc[:, t, :], ALU.add).then_inc(f_ok, 1)
                if t + 2 < NT:
                    pool.wait_ge(out_st[s], 16 * (t // 2 + 1))
                    gather(t + 2)

        @block.scalar
        def _(act):
            act.wait_ge(const_ld, 6 * 16)
            act.activation(c_silu[:, :, :], c_in[:, :, :], ACT.Silu).then_inc(silu_c, 1)
            for g in range(4):
                i = load_at["wq", g]
                act.wait_ge(stage_ld[i % 3], 16 * (i // 3 + 1))
                act.activation(wq_hi[:, :, g * D:(g + 1) * D], stage[i % 3], ACT.Copy).then_inc(wq_hi_ok, 1)
                if g == 0:
                    for i in range(TT):
                        act.wait_ge(hf_ok, i + 1)
                        act.activation(h_hi[:, :, i * P:(i + 1) * P], h_full[:, i % 2], ACT.Copy)\
                           .then_inc(hhi_ok, 1)

            def q_rows(b, more, first):
                for j in range(H):
                    act.wait_ge(q_full, b * H + (j + 1))
                    if not (first and j < 4):
                        act.wait_ge(q_st[j % 4], b * (16 * H // 4) + 16 * (j // 4))
                    act.activation(q_out[:, j % 4, :], bank[j % 4][:, :], ACT.Identity,
                                   bias=bq_c[:, j:j + 1]).then_inc(q_ev, 1)
                    if more and j >= 11 and j < 15:
                        i = j - 11
                        wait_apart(act, (hf_ok, b * TT + (TT + i + 1)))
                        act.activation(h_hi[:, :, bass.ds((b + 1) * T + i * P, P)], h_full[:, i % 2],
                                       ACT.Copy).then_inc(hhi_ok, 1)

            q_rows(0, True, True)
            with act.Fori(1, B - 1) as b:
                q_rows(b, True, False)
            q_rows(B - 1, False, False)

            stage1_over(act)

            def k_part(p, n, h):
                wait_apart(act, (k_full, n * 2 + (h + 1)))
                act.activation(k_hi[:, h, :], bank[h][:, :], ACT.Identity,
                               bias=bk_c[:, bass.ds(p * 2 + h, 1)]).then_inc(k_hi_ok, 1)

            k_part(0, 0, 0)
            k_part(0, 0, 1)

            def step(p, b, first, last):
                n = p * B + b

                def exps(h):
                    if not first:
                        act.wait_ge(pt_full, n * 6 + (3 * h - 3))
                    for r in range(TT):
                        act.wait_ge(s_neg, n * 8 + (4 * h + r + 1))
                        act.activation(prob[:, h, ROW_AT[r]:ROW_AT[r] + (r + 1) * P],
                                       bank[2 + r % 2][:, 0:(r + 1) * P], ACT.Exp,
                                       bias=neg_max[:, h, r:r + 1], scale=SCALE,
                                       accum_out=row_sum[:, h, r:r + 1]).then_inc(s_exp, 1)

                def v_part(g):
                    if g == 0 and not first:
                        act.wait_ge(o_full, n * 2)
                    act.wait_ge(v_full, n * 2 + (g + 1))
                    act.activation(v_hi[:, 2 * g:2 * g + 2, :], bank[g][:, :].rearrange("p (i n) -> p i n", i=2),
                                   ACT.Copy).then_inc(v_hi_ok, 1)

                def pt_part(h):
                    if not (first and h == 0):
                        act.wait_ge(o_full, n * 2 + h)
                    for g in range(3):
                        act.wait_ge(pt_full, n * 6 + (3 * h + g + 1))
                        act.activation(pt_hi[:, PT_AT[g]:PT_AT[g] + PT_LEN[g]], bank[4 + g % 2][:, 0:PT_LEN[g]],
                                       ACT.Copy).then_inc(pt_hi_ok, 1)

                def o_part(h):
                    free = [(wo_full, n * TT)] if h == 0 and not first else []
                    wait_apart(act, *free, (o_full, n * 2 + (h + 1)))
                    act.activation(o_hi[:, h, :], bank[6 + h][:, :], ACT.Identity,
                                   bias=bv_c[:, bass.ds(p * 2 + h, 1)]).then_inc(o_hi_ok, 1)

                exps(0)
                exps(1)
                v_part(0)
                pt_part(0)
                v_part(1)
                o_part(0)
                pt_part(1)
                if not last:
                    pn = p if b < B - 1 else p + 1
                    k_part(pn, n + 1, 0)
                    k_part(pn, n + 1, 1)
                o_part(1)

            walk_steps(act, step)

            act.wait_ge(wo_add, NIT * TT)

            def xt_part(n, s):
                act.wait_ge(xt_full, n + 1)
                act.activation(xt_hi[:, s], bank[2][:, :].rearrange("p (c n) -> p c n", c=DC), ACT.Copy)\
                   .then_inc(xt_hi_ok, 1)

            def job(n, s, prev, nxt):
                act.wait_ge(gt_full, n + 1)
                act.activation(gate_s[:, s, :], bank[0][:, 0:F], ACT.Silu).then_inc(silu_ok, 1)
                if prev:
                    ht_part(n - 1)
                if nxt:
                    if not (isinstance(n, int) and n == 0):
                        act.wait_ge(up_full, n)
                    xt_part(n + 1, 1 - s)
                if prev == "routed":
                    y_part(n - 1, 1 - s)

            def ht_part(m):
                act.wait_ge(ht_full, m + 1)
                for f in range(FC):
                    ins = act.activation(ht_hi[0:FK[f], f, :], bank[3][0:FK[f], f * P:(f + 1) * P], ACT.Copy)
                ins.then_inc(ht_hi_ok, 1)

            def y_part(m, s):
                act.wait_ge(y_full, m + 1)
                if not (isinstance(m, int) and m < 2 * NT + 2):
                    act.wait_ge(y_st[s], (m - (2 * NT + s)) * 8)
                act.activation(y_sb[:, s, :], bank[4 + s][:, :], ACT.Copy).then_inc(y_ev, 1)

            xt_part(0, 0)
            job(0, 0, None, True)
            job(1, 1, "shared", True)
            with act.Fori(1, NT // 2) as j:
                for k in range(2):
                    job(j * 2 + k, k, "shared", True)
            job(NT, 0, "shared", True)
            act.wait_ge(rt_sub, 1)
            act.activation(sc[:, :, :], ra[:, :, :], ACT.Exp).then_inc(rt_exp, 1)
            job(NT + 1, 1, "shared", True)
            with act.Fori(NT // 2 + 1, NT) as j:
                for k in range(2):
                    job(j * 2 + k, k, "shared", True)
            job(2 * NT, 0, "shared", True)
            act.wait_ge(y_add, 2 * NT)
            job(2 * NT + 1, 1, "routed", True)
            with act.Fori(NT + 1, NJ // 2 - 1) as j:
                for k in range(2):
                    job(j * 2 + k, k, "routed", True)
            job(NJ - 2, 0, "routed", True)
            job(NJ - 1, 1, "routed", False)
            ht_part(NJ - 1)
            y_part(NJ - 1, 1)

            for t in range(NT):
                s = t % 2
                act.wait_ge(g_ld[s], 32 * (t // 2 + 1))
                act.activation(yg[:, 0, s, :], yg[:, 0, s, :], ACT.Copy, scale=top_w[:, 0, t:t + 1])\
                   .then_inc(f_w1, 1)

        @block.tensor
        def _(pe):
            def mm3(dst, terms):
                k, last = 0, 3 * len(terms) - 1
                for sh, sl, mh_, ml in terms:
                    for a, m in ((sh, mh_), (sh, ml), (sl, mh_)):
                        ins = pe.matmul(dst, a, m, start=(k == 0), stop=(k == last))
                        k += 1
                return ins

            pe.wait_ge(const_ld, 6 * 16)
            pe.wait_ge(silu_c, 1)

            def mod_piece(m):
                i = load_at["mod", m]
                pe.wait_ge(stage_ld[i % 3], 16 * (i // 3 + 1))
                if m >= 1:
                    pe.wait_ge(mod_ev, m)
                for c in range(DC):
                    ins = pe.matmul(bank[6][0:B, :], c_silu[:, c, :], stage[i % 3][:, c, :],
                                    start=(c == 0), stop=(c == DC - 1))
                ins.then_inc(mod_full, 1)

            for m in range(2):
                mod_piece(m)
            for m in range(2):
                pe.wait_ge(mod_ev, m + 1)
                for c in range(DC):
                    ins = pe.transpose(bank[7][:, (m * DC + c) * B:(m * DC + c + 1) * B],
                                       mod_row[:, m, c * P:(c + 1) * P], ident[0:B, 0:B])
            ins.then_inc(modt_full, 1)

            def transposes(b, i):
                pe.wait_ge(xn_ok, b * TT + (i + 1))
                if not (isinstance(b, int) and b == 0 and i < 2):
                    pe.wait_ge(hf_ok, b * TT + (i - 1))
                for c in range(DC):
                    ins = pe.transpose(bank[4 + i % 2][:, c * P:(c + 1) * P], x_in[:, i, c * P:(c + 1) * P],
                                       ident[:, :])
                ins.then_inc(tx_full, 1)

            for i in range(TT):
                transposes(0, i)

            def q_rows(b, more, first):
                cols = bass.ds(b * T, T)
                pe.wait_ge(hlo_ok, b * TT + TT)
                for j in range(H):
                    if first and j % 4 == 0:
                        pe.wait_ge(wq_ok, j // 4 + 1)
                    if not (first and j < 4):
                        pe.wait_ge(q_ev, b * H + (j - 3))
                    mm3(bank[j % 4][:, :],
                        [(wq_hi[:, c, j * P:(j + 1) * P], wq_lo[:, c, j * P:(j + 1) * P],
                          h_hi[:, c, cols], h_lo[:, c, cols]) for c in range(DC)]).then_inc(q_full, 1)
                    if more and j >= 10 and j < 14:
                        transposes(b + 1, j - 10)
                    if not more and j == H // 2 - 1:
                        mod_piece(5)

            q_rows(0, True, True)
            with pe.Fori(1, B - 1) as b:
                q_rows(b, True, False)
            for m in range(2, 5):
                mod_piece(m)
            q_rows(B - 1, False, False)

            pe.wait_ge(const_r, 2)
            pe.wait_ge(q_ev, B * H)
            pe.wait_ge(mod_ev, 6)
            pe.wait_ge(hlo_ok, NT)

            def k_rows(n, pair, b):
                pe.wait_ge(wk_ok, pair + 1)
                for h in range(2):
                    if not (isinstance(n, int) and n == 0):
                        pe.wait_ge(v_ok, n * 2 + (h - 1))
                    mm3(bank[h][:, :],
                        [(wk_hi[:, c, h * P:(h + 1) * P], wk_lo[:, c, h * P:(h + 1) * P],
                          h_hi[:, c, b * T:(b + 1) * T], h_lo[:, c, b * T:(b + 1) * T])
                         for c in range(DC)]).then_inc(k_full, 1)

            k_rows(0, 0, 0)

            def out_tile(m, pair, i, after):
                if i == 0:
                    pe.wait_ge(wo_ok, pair + 1)
                    pe.wait_ge(o_ok, m * 2 + 2)
                if after:
                    pe.wait_ge(*after)
                mm3(bank[i % 2][:, :],
                    [(o_hi[:, h, i * P:(i + 1) * P], o_lo[:, h, i * P:(i + 1) * P],
                      wo_hi[:, h, :], wo_lo[:, h, :]) for h in range(2)]).then_inc(wo_full, 1)

            def step(p, b, first, last):
                n = p * B + b

                def scores(h):
                    pe.wait_ge(k_ok, n * 2 + (h + 1))
                    pe.wait_ge(q_ok, n * 2 + (h + 1))
                    for r in range(TT):
                        if not (first and h == 0 and r < 2):
                            pe.wait_ge(s_exp, n * 8 + (4 * h + r - 1))
                        w = (r + 1) * P
                        dst = bank[2 + r % 2]
                        for k, (a, m) in enumerate(((q_hi, k_hi), (q_hi, k_lo), (q_lo, k_hi))):
                            pe.matmul(dst[:, 0:w], a[:, h, r * P:w], m[:, h, 0:w], start=(k == 0), stop=False)
                        pe.matmul(dst[:, r * P:w], ident_r[:, :], causal_r[:, :], start=False, stop=True)\
                          .then_inc(s_full, 1)

                def values(g):
                    pe.wait_ge(wv_ok, p + 1)
                    if not first:
                        pe.wait_ge(wo_add, n * TT + (g - 1))
                    for i in range(2):
                        rows = slice((b * TT + 2 * g + i) * P, (b * TT + 2 * g + i + 1) * P)
                        ins = mm3(bank[g][:, i * 2 * P:(i + 1) * 2 * P],
                                  [(h_hi[:, c, rows], h_lo[:, c, rows], wv_hi[:, c, :], wv_lo[:, c, :])
                                   for c in range(DC)])
                    ins.then_inc(v_full, 1)

                def turn(h):
                    pe.wait_ge(p_ok, n * 2 + (h + 1))
                    for g, blocks in enumerate(PT_GROUPS):
                        if not (first and h == 0 and g < 2):
                            pe.wait_ge(pt_ok, n * 6 + (3 * h + (1 if g == 2 else 0)))
                        for k, at in blocks:
                            for r in range(k, TT):
                                ins = pe.transpose(
                                    bank[4 + g % 2][:, at + (r - k) * P:at + (r - k + 1) * P],
                                    prob[:, h, ROW_AT[r] + k * P:ROW_AT[r] + (k + 1) * P], ident[:, :])
                        ins.then_inc(pt_full, 1)

                def weigh(h):
                    if not first:
                        pe.wait_ge(o_ok, n * 2 + (h - 1))
                    for g, blocks in enumerate(PT_GROUPS):
                        pe.wait_ge(pt_ok, n * 6 + (3 * h + g + 1))
                        pe.wait_ge(v_ok, n * 2 + (1 if g == 0 else 2))
                        for k, at in blocks:
                            w = (TT - k) * P
                            cols = slice(PT_AT[g] + at, PT_AT[g] + at + w)
                            vals = slice(h * P, (h + 1) * P)
                            for q, (a, m) in enumerate(((v_hi, pt_hi), (v_hi, pt_lo), (v_lo, pt_hi))):
                                ins = pe.matmul(bank[6 + h][:, k * P:T], a[:, k, vals], m[:, cols],
                                                start=(k == 0 and q == 0), stop=(g == 2 and q == 2))
                    ins.then_inc(o_full, 1)

                scores(0)
                if not first:
                    pm = p if b > 0 else p - 1
                    out_tile(n - 1, pm, 0, (k_ok, n * 2 + 1))
                    out_tile(n - 1, pm, 1, (k_ok, n * 2 + 2))
                    out_tile(n - 1, pm, 2, (wo_add, n * TT - 3))
                    out_tile(n - 1, pm, 3, (wo_add, n * TT - 2))
                scores(1)
                values(0)
                turn(0)
                values(1)
                weigh(0)
                turn(1)
                if not last:
                    k_rows(n + 1, p if b < B - 1 else p + 1, (b + 1) % B)
                weigh(1)

            walk_steps(pe, step)
            out_tile(NIT - 1, HP - 1, 0, (v_ok, 2 * NIT - 1))
            out_tile(NIT - 1, HP - 1, 1, (v_ok, 2 * NIT))
            out_tile(NIT - 1, HP - 1, 2, (wo_add, NIT * TT - 3))
            out_tile(NIT - 1, HP - 1, 3, (wo_add, NIT * TT - 2))

            pe.wait_ge(wo_add, NIT * TT)
            pe.wait_ge(pt_ok, NIT * 6)
            pe.wait_ge(o_ok, NIT * 2)

            def turn_rows(n, s, count):
                pe.wait_ge(xin_ld[s], count)
                if not (isinstance(n, int) and n == 0):
                    pe.wait_ge(xt_ok, n)
                for c in range(DC):
                    ins = pe.transpose(bank[2][:, c * P:(c + 1) * P], xin[:, s, c * P:(c + 1) * P], ident[:, :])
                ins.then_inc(xt_full, 1)

            def half(n, s, wofs, which):
                if which == 0:
                    pe.wait_ge(xt_ok, n + 1)
                if not (isinstance(n, int) and n == 0):
                    pe.wait_ge((silu_ok, mid_ok)[which], n)
                at = (WG, WU)[which]
                mm3(bank[which][:, 0:F],
                    [(xt_hi[:, s, c, :], xt_lo[:, s, c, :], w_hi[:, wcol(wofs, at + c * F, F)],
                      w_lo[:, wcol(wofs, at + c * F, F)]) for c in range(DC)])\
                    .then_inc((gt_full, up_full)[which], 1)

            def wcol(wofs, at, width):
                if isinstance(wofs, int):
                    return slice(wofs + at, wofs + at + width)
                return bass.ds(wofs + at, width)

            def logits(n, s):
                if not (isinstance(n, int) and n == 0):
                    pe.wait_ge(lg_ok, n)
                mm3(bank[6][:, 0:E],
                    [(xt_hi[:, s, c, :], xt_lo[:, s, c, :], g_hi[:, c, :], g_lo[:, c, :])
                     for c in range(DC)]).then_inc(lg_full, 1)

            def turn_mid(m, s):
                pe.wait_ge(mid_ok, m + 1)
                if not (isinstance(m, int) and m == 0):
                    pe.wait_ge(ht_ok, m)
                for f in range(FC):
                    ins = pe.transpose(bank[3][0:FK[f], f * P:(f + 1) * P],
                                       h_mid[:, s, f * P:f * P + FK[f]], ident[:, :])
                ins.then_inc(ht_full, 1)

            def down(m, s, wofs, free):
                pe.wait_ge(ht_ok, m + 1)
                if free:
                    pe.wait_ge(*free)
                mm3(bank[4 + s][:, :],
                    [(ht_hi[0:FK[f], f, :], ht_lo[0:FK[f], f, :], w_hi[0:FK[f], wcol(wofs, WD + f * D, D)],
                      w_lo[0:FK[f], wcol(wofs, WD + f * D, D)]) for f in range(FC)]).then_inc(y_full, 1)

            def job(n, s, wofs, prev_ofs, route=False, prev=True, nxt=True, free=None):
                half(n, s, wofs, 0)
                if prev:
                    turn_mid(n - 1, 1 - s)
                half(n, s, wofs, 1)
                if route:
                    logits(n, s)
                if nxt:
                    turn_rows(n + 1, 1 - s, xcount(n + 1, 1 - s))
                if prev:
                    down(n - 1, 1 - s, prev_ofs, free)

            def xcount(m, s):
                return (m - s) * 8 + 16

            pe.wait_ge(g_ok, 1)
            turn_rows(0, 0, 16)
            pe.wait_ge(w_ld[0], 32)
            job(0, 0, 0, 0, route=True, prev=False)
            job(1, 1, 0, 0, route=True)
            job(2, 0, 0, 0, route=True)
            job(3, 1, 0, 0, route=True, free=(y_gb, 1))
            with pe.Fori(2, NT // 2) as j:
                for k in range(2):
                    job(j * 2 + k, k, 0, 0, route=True, free=(y_gb, j * 2 + (k - 2)))
            pe.wait_ge(w_ld[1], 32)
            job(NT, 0, WE, 0, free=(y_gb, NT - 2))
            job(NT + 1, 1, WE, WE, free=(y_gb, NT - 1))
            pe.wait_ge(rt_hot, 1)
            pe.wait_ge(ones_ok, 1)
            hot_cols = hot[:, :, :].rearrange("p t e -> p (t e)")
            pe.matmul(bank[7][:, 0:NT * E], tri[:, :], hot_cols, start=True, stop=True)
            pe.matmul(bank[7][:, NT * E:2 * NT * E], ones[:, :], hot_cols, start=True, stop=True)\
              .then_inc(rt_cnt, 1)
            with pe.Fori(NT // 2 + 1, NT) as j:
                for k in range(2):
                    job(j * 2 + k, k, WE, WE, free=(y_gb, j * 2 + (k - 2)))

            pe.wait_ge(tab_ok, 1)

            def read(row, r, most):
                return pe.value_load(tab[0:1, row, bass.ds(r, 1)], min_val=0, max_val=most)

            def routed(j, first, last):
                for k in range(2):
                    r = j * 2 + k
                    n = r + 2 * NT
                    par = read(0, r, 1)
                    loads_0, loads_1 = read(1, r, 32 * E), read(2, r, 32 * E)
                    if first and k == 0:
                        free, prev_ofs = (y_gb, n - 2), WE
                    else:
                        prev_ofs = read(0, r - 1, 1) * WE
                        if first:
                            free = (y_gb, 2 * NT - 1)
                        elif k == 0 and isinstance(j, int) and j == 1:
                            free = (y_gb, 2 * NT)
                        else:
                            free = (y_ev, r - 2)
                    pe.wait_ge(w_ld[0], loads_0)
                    pe.wait_ge(w_ld[1], loads_1)
                    job(n, k, par * WE, prev_ofs, nxt=not (last and k == 1), free=free)

            routed(0, True, False)
            routed(1, False, False)
            with pe.Fori(2, NSLOT // 2 - 1) as j:
                routed(j, False, False)
            routed(NSLOT // 2 - 1, False, True)
            turn_mid(NJ - 1, 1)
            down(NJ - 1, 1, read(0, NSLOT - 1, 1) * WE, (y_ev, NSLOT - 2))

        @block.vector
        def _(dve):
            dve.wait_ge(const_ld, 6 * 16)
            dve.tensor_copy(ident_r[:, :], ident[:, :]).then_inc(const_r, 1)
            dve.tensor_copy(causal_r[:, :], causal[:, :]).then_inc(const_r, 1)

            dc = [0]

            def link(ins):
                dc[0] += 1
                ins.then_inc(dchain, 1)
                dve.wait_ge(dchain, dc[0])

            def mod_piece(m):
                dst = mod_row[:, m % 2, :]
                if m >= 2:
                    dve.wait_ge(mod_st[m % 2], 16 * (m // 2))
                dve.wait_ge(mod_full, m + 1)
                src = bank[6][0:B, :]
                if m in (1, 4):
                    dve.tensor_scalar(dst, src, 1.0, None, ALU.add).then_inc(mod_ev, 1)
                elif m in (0, 3):
                    dve.tensor_copy(dst, src).then_inc(mod_ev, 1)
                else:
                    link(dve.tensor_scalar(mod_a[:, :], src, -1.0, None, ALU.mult))
                    link(dve.tensor_tensor(mod_a[:, :], mod_a[:, :], src, ALU.max))
                    link(dve.tensor_scalar(mod_a[:, :], mod_a[:, :], 0.25, None, ALU.max))
                    link(dve.tensor_scalar(mod_s[:, :], src, 0.0, 2.0, ALU.is_ge, ALU.mult))
                    dve.scalar_tensor_tensor(out=dst, in0=mod_s[:, :], scalar=-1.0, in1=mod_a[:, :],
                                             op0=ALU.add, op1=ALU.mult).then_inc(mod_ev, 1)

            def norm_stats(b, base):
                wait_apart(dve, (x_ld, b * 16 + 16))
                k = [0]

                def chain(ins):
                    k[0] += 1
                    ins.then_inc(ln_chain, 1)
                    wait_apart(dve, (ln_chain, base + k[0]))

                for i in range(TT):
                    ins = dve.bn_stats(stat[:, i, :], x_in[:, i, :])
                chain(ins)
                for i in range(TT):
                    ins = dve.bn_aggr(mv[:, i, :], stat[:, i, :])
                chain(ins)
                dve.tensor_scalar(ve[:, :], mv[:, :, 1], EPS, None, ALU.add).then_inc(ln_var, 1)
                dve.wait_ge(ln_seed, b + 1)
                chain(dve.tensor_tensor(nt1[:, :], rs0[:, :], rs0[:, :], ALU.mult))
                chain(dve.tensor_tensor(nt2[:, :], nt1[:, :], ve[:, :], ALU.mult))
                chain(dve.tensor_scalar(nt1[:, :], nt2[:, :], -0.5, 1.5, ALU.mult, ALU.add))
                chain(dve.tensor_tensor(rstd[:, :], nt1[:, :], rs0[:, :], ALU.mult))
                for i in range(TT):
                    dve.tensor_scalar(x_in[:, i, :], x_in[:, i, :], mv[:, i, 0:1], rstd[:, i:i + 1],
                                      ALU.subtract, ALU.mult).then_inc(xn_ok, 1)

            LN_CHAIN = 6

            def modulate(b, i, first):
                dve.wait_ge(tx_full, b * TT + (i + 1))
                if not (first and i < 2):
                    dve.wait_ge(hlo_ok, b * TT + (i - 1))
                for c in range(DC):
                    ins = dve.tensor_scalar(h_full[:, i % 2, c, :], bank[4 + i % 2][:, c * P:(c + 1) * P],
                                            modc[:, 1, c, bass.ds(b, 1)], modc[:, 0, c, bass.ds(b, 1)],
                                            ALU.mult, ALU.add)
                ins.then_inc(hf_ok, 1)

            def h_low(b, i):
                dve.wait_ge(hhi_ok, b * TT + (i + 1))
                cols = bass.ds(b * T + i * P, P)
                dve.tensor_tensor(h_lo[:, :, cols], h_full[:, i % 2], h_hi[:, :, cols].bitcast(F32), ALU.subtract)\
                    .then_inc(hlo_ok, 1)

            norm_stats(0, 0)
            mod_piece(0)
            mod_piece(1)
            dve.wait_ge(modt_full, 1)
            dve.tensor_copy(modc[:, :, :, :].rearrange("p m c b -> p (m c b)"), bank[7][:, 0:2 * DC * B])\
                .then_inc(modc_ok, 1)
            dve.wait_ge(modc_ok, 1)
            def wq_low(g):
                i = load_at["wq", g]
                dve.wait_ge(wq_hi_ok, g + 1)
                dve.tensor_tensor(wq_lo[:, :, g * D:(g + 1) * D], stage[i % 3],
                                  wq_hi[:, :, g * D:(g + 1) * D].bitcast(F32), ALU.subtract).then_inc(wq_ok, 1)

            wq_low(0)
            for i in range(TT):
                modulate(0, i, True)
                if i:
                    h_low(0, i - 1)
            h_low(0, TT - 1)
            for g in range(1, 4):
                wq_low(g)

            def batch(b, first=False):
                norm_stats(b, b * LN_CHAIN)
                for i in range(TT):
                    modulate(b, i, False)
                    if i:
                        h_low(b, i - 1)
                h_low(b, TT - 1)

            with dve.Fori(1, B) as b:
                batch(b)
            for m in range(2, 6):
                mod_piece(m)

            stage1_over(dve)

            def low(dst, src, hi, bias, done):
                if bias is None:
                    dve.tensor_tensor(dst, src, hi.bitcast(F32), ALU.subtract).then_inc(done, 1)
                else:
                    dve.scalar_tensor_tensor(out=dst, in0=src, scalar=bias, in1=hi.bitcast(F32),
                                             op0=ALU.add, op1=ALU.subtract).then_inc(done, 1)

            def k_part(p, n, h):
                dve.wait_ge(k_hi_ok, n * 2 + (h + 1))
                low(k_lo[:, h, :], bank[h][:, :], k_hi[:, h, :], bk_c[:, bass.ds(p * 2 + h, 1)], k_ok)

            k_part(0, 0, 0)
            k_part(0, 0, 1)
            dve.wait_ge(acc_ok, 1)

            def step(p, b, first, last):
                n = p * B + b

                def maxima(h):
                    for r in range(TT):
                        s = n * 8 + (4 * h + r + 1)
                        dve.wait_ge(s_full, s)
                        dve.tensor_reduce(row_max[:, h, r:r + 1], bank[2 + r % 2][:, 0:(r + 1) * P], AX_X,
                                          ALU.max).then_inc(s_max, 1)
                        dve.wait_ge(s_max, s)
                        dve.tensor_scalar(neg_max[:, h, r:r + 1], row_max[:, h, r:r + 1], -SCALE, None,
                                          ALU.mult).then_inc(s_neg, 1)

                def inverses(h):
                    dve.wait_ge(s_exp, n * 8 + (4 * h + 4))
                    dve.reciprocal(row_inv[:, h, :], row_sum[:, h, :]).then_inc(inv_ok, 1)

                def v_part(g):
                    dve.wait_ge(v_hi_ok, n * 2 + (g + 1))
                    low(v_lo[:, 2 * g:2 * g + 2, :], bank[g][:, :].rearrange("p (i n) -> p i n", i=2),
                        v_hi[:, 2 * g:2 * g + 2, :], None, v_ok)

                def pt_part(h):
                    for g in range(3):
                        dve.wait_ge(pt_hi_ok, n * 6 + (3 * h + g + 1))
                        cols = slice(PT_AT[g], PT_AT[g] + PT_LEN[g])
                        low(pt_lo[:, cols], bank[4 + g % 2][:, 0:PT_LEN[g]], pt_hi[:, cols], None, pt_ok)

                def o_part(h):
                    dve.wait_ge(o_hi_ok, n * 2 + (h + 1))
                    low(o_lo[:, h, :], bank[6 + h][:, :], o_hi[:, h, :], bv_c[:, bass.ds(p * 2 + h, 1)], o_ok)

                maxima(0)
                inverses(0)
                if not first:
                    add_out(n - 1, (b - 1) % B)
                maxima(1)
                inverses(1)
                v_part(0)
                pt_part(0)
                v_part(1)
                o_part(0)
                pt_part(1)
                if not last:
                    pn = p if b < B - 1 else p + 1
                    k_part(pn, n + 1, 0)
                    k_part(pn, n + 1, 1)
                o_part(1)

            def add_out(m, b):
                for i in range(TT):
                    dve.wait_ge(wo_full, m * TT + (i + 1))
                    t = b * TT + i
                    dve.tensor_tensor(acc[:, t, :], acc[:, t, :], bank[i % 2][:, :], ALU.add).then_inc(wo_add, 1)

            walk_steps(dve, step)
            add_out(NIT - 1, B - 1)

            dve.wait_ge(wo_add, NIT * TT)
            dve.wait_ge(c3_ld, 16 * (4 * B + 4))
            dve.tensor_copy(g_hi[:, :, :], g_raw[:, :, :]).then_inc(g_hi_ok, 1)
            dve.wait_ge(g_hi_ok, 1)
            dve.tensor_tensor(g_lo[:, :, :], g_raw[:, :, :], g_hi[:, :, :].bitcast(F32), ALU.subtract)\
                .then_inc(g_ok, 1)

            C_CHAIN = 8

            def c_tile(b, i, t):
                s = i % 2
                base = t * C_CHAIN
                k = [0]

                def chain(ins):
                    k[0] += 1
                    ins.then_inc(c_chain, 1)
                    wait_apart(dve, (c_chain, base + k[0]))

                a = acc[:, bass.ds(t, 1), :]
                chain(dve.tensor_tensor(a, a, bo_b[:, :].unsqueeze(1), ALU.add))
                chain(dve.tensor_tensor(a, a, ga_b[:, bass.ds(b, 1), :], ALU.mult))
                dve.wait_ge(xr_ld[s], (t - s) * 8 + 16)
                dve.tensor_tensor(a, a, xr[:, s, :].unsqueeze(1), ALU.add).then_inc(x1_ok, 1)
                wait_apart(dve, (x1_ok, t + 1))
                chain(dve.bn_stats(stat[:, s, :], acc[:, bass.ds(t, 1), :].rearrange("p a d -> p (a d)")))
                chain(dve.bn_aggr(mv[:, s, :], stat[:, s, :]))
                dve.tensor_scalar(ve[:, s:s + 1], mv[:, s, 1:2], EPS, None, ALU.add).then_inc(c_var, 1)
                dve.wait_ge(c_seed, t + 1)
                r = slice(s, s + 1)
                chain(dve.tensor_tensor(nt1[:, r], rs0[:, r], rs0[:, r], ALU.mult))
                chain(dve.tensor_tensor(nt2[:, r], nt1[:, r], ve[:, r], ALU.mult))
                chain(dve.tensor_scalar(nt1[:, r], nt2[:, r], -0.5, 1.5, ALU.mult, ALU.add))
                chain(dve.tensor_tensor(rstd[:, r], nt1[:, r], rs0[:, r], ALU.mult))
                if not (isinstance(t, int) and t < 2):
                    dve.wait_ge(h2_st[s], (t - s) * 8)
                dve.tensor_scalar(h2[:, s, :].unsqueeze(1), a, mv[:, s, 0:1], rstd[:, r],
                                  ALU.subtract, ALU.mult).then_inc(c_xn, 1)

            def xt_part(n, s):
                dve.wait_ge(xt_hi_ok, n + 1)
                low(xt_lo[:, s], bank[2][:, :].rearrange("p (c n) -> p c n", c=DC), xt_hi[:, s], None, xt_ok)

            def ht_part(m):
                dve.wait_ge(ht_hi_ok, m + 1)
                for f in range(FC):
                    ins = dve.tensor_tensor(ht_lo[0:FK[f], f, :], bank[3][0:FK[f], f * P:(f + 1) * P],
                                            ht_hi[0:FK[f], f, :].bitcast(F32), ALU.subtract)
                ins.then_inc(ht_ok, 1)

            def y_part(m, s, b):
                dve.wait_ge(y_full, m + 1)
                if not (isinstance(m, int) and m < 2):
                    dve.wait_ge(y_add, m - 1)
                dve.tensor_tensor(y_sb[:, s, :].unsqueeze(1), bank[4 + s][:, :].unsqueeze(1),
                                  gb_b[:, bass.ds(b, 1), :], ALU.mult).then_inc(y_gb, 1)

            def job(n, s, prev, nxt, b_prev=None, route=False):
                if prev:
                    ht_part(n - 1)
                dve.wait_ge(up_full, n + 1)
                dve.wait_ge(silu_ok, n + 1)
                if not (isinstance(n, int) and n < 2):
                    dve.wait_ge(ht_full, n - 1)
                dve.tensor_tensor(h_mid[:, s, :], gate_s[:, s, :], bank[1][:, 0:F], ALU.mult).then_inc(mid_ok, 1)
                if nxt:
                    xt_part(n + 1, 1 - s)
                if route:
                    dve.wait_ge(lg_full, n + 1)
                    dve.tensor_copy(lg[:, bass.ds(n, 1), :], bank[6][:, 0:E].unsqueeze(1)).then_inc(lg_ok, 1)
                if prev == "shared":
                    y_part(n - 1, 1 - s, b_prev)

            for t in range(TT):
                c_tile(0, t, t)
            xt_part(0, 0)

            def quad0(b, hidden, first):
                for i in range(TT):
                    n = b * TT + i
                    job(n, i % 2, None if first and i == 0 else "shared", True,
                        b_prev=b if i else b - 1, route=True)
                    if hidden:
                        c_tile(b + 1, i, n + TT)

            quad0(0, True, True)
            with dve.Fori(1, B - 1) as b:
                quad0(b, True, False)
            quad0(B - 1, False, False)

            def bt(a):
                return a.unsqueeze(2).to_broadcast([P, NT, E])

            def route_a():
                dve.wait_ge(lg_ok, NT)
                link(dve.tensor_reduce(r1[:, 0, :], lg[:, :, :], AX_X, ALU.max))
                dve.tensor_tensor(ra[:, :, :], lg[:, :, :], bt(r1[:, 0, :]), ALU.subtract).then_inc(rt_sub, 1)

            iota_e = cf("iota", NT * E, "p (t e) -> p t e", dict(e=E))

            def first_of(scores_, top, hot_):
                link(dve.tensor_reduce(top, scores_, AX_X, ALU.max))
                link(dve.tensor_tensor(ra[:, :, :], scores_, bt(top), ALU.is_equal))
                link(dve.tensor_tensor(ra[:, :, :], ra[:, :, :], iota_e, ALU.mult))
                link(dve.tensor_reduce(r1[:, 1, :], ra[:, :, :], AX_X, ALU.min))
                link(dve.tensor_tensor(hot_, iota_e, bt(r1[:, 1, :]), ALU.is_equal))

            def route_b():
                dve.wait_ge(rt_exp, 1)
                link(dve.tensor_reduce(r1[:, 0, :], sc[:, :, :], AX_X, ALU.add))
                link(dve.reciprocal(r1[:, 2, :], r1[:, 0, :]))
                link(dve.tensor_tensor(sc[:, :, :], sc[:, :, :], bt(r1[:, 2, :]), ALU.mult))
                first_of(sc[:, :, :], r1[:, 3, :], oh1[:, :, :])
                link(dve.scalar_tensor_tensor(out=rb[:, :, :], in0=oh1[:, :, :], scalar=-4.0,
                                              in1=sc[:, :, :], op0=ALU.mult, op1=ALU.add))
                first_of(rb[:, :, :], r1[:, 4, :], oh2[:, :, :])
                dve.tensor_tensor(hot[:, :, :], oh1[:, :, :], oh2[:, :, :], ALU.add).then_inc(rt_hot, 1)
                link(dve.tensor_tensor(r1[:, 5, :], r1[:, 3, :], r1[:, 4, :], ALU.add))
                link(dve.tensor_scalar(r1[:, 5, :], r1[:, 5, :], 1e-20, None, ALU.add))
                link(dve.reciprocal(r1[:, 6, :], r1[:, 5, :]))
                for c in range(2):
                    link(dve.tensor_tensor(top_w[:, c, :], r1[:, 3 + c, :], r1[:, 6, :], ALU.mult))

            def route_c():
                dve.wait_ge(rt_cnt, 1)
                before = bank[7][:, 0:NT * E].rearrange("p (t e) -> p t e", e=E)
                count = bank[7][:, NT * E:2 * NT * E].rearrange("p (t e) -> p e t", e=E)
                link(dve.tensor_copy(cnt_et[:, :, :], count))
                flat = "p e t -> p (e t)"
                link(dve.tensor_tensor_scan(cum_et[:, :, :].rearrange(flat), cf("keep", NT * E),
                                            cnt_et[:, :, :].rearrange(flat), 0.0, ALU.mult, ALU.add))
                total = cum_et[:, :, NT - 1:NT]
                link(dve.tensor_tensor(over[:, :, :], total.to_broadcast([P, E, NT]),
                                       cf("edges", NT * E, "p (e t) -> p e t", dict(t=NT)), ALU.is_gt))
                link(dve.tensor_reduce(e1[:, 0, :], over[:, :, :], AX_X, ALU.add))
                link(dve.tensor_scalar(e1[:, 1, :], e1[:, 0, :], 1.0, None, ALU.max))
                link(dve.tensor_tensor_scan(e1[:, 2, :], cf("one_e", E), e1[:, 1, :], 0.0, ALU.mult, ALU.add))
                link(dve.tensor_tensor(e1[:, 3, :], e1[:, 2, :], e1[:, 1, :], ALU.subtract))
                link(dve.tensor_tensor(cum_et[:, :, :], cum_et[:, :, :], cnt_et[:, :, :], ALU.subtract))
                link(dve.scalar_tensor_tensor(
                    out=over[:, :, :], in0=e1[:, 3, :].unsqueeze(2).to_broadcast([P, E, NT]), scalar=float(P),
                    in1=cum_et[:, :, :], op0=ALU.mult, op1=ALU.add))
                link(dve.tensor_tensor(slot_base[:, :, :], before, over[:, :, :].rearrange("p e t -> p t e"),
                                       ALU.add))
                for c, hot_ in enumerate((oh1, oh2)):
                    link(dve.tensor_tensor(ra[:, :, :], slot_base[:, :, :], hot_[:, :, :], ALU.mult))
                    link(dve.tensor_reduce(r1[:, 7, :], ra[:, :, :], AX_X, ALU.add))
                    link(dve.tensor_copy(pos_i[:, c, :], r1[:, 7, :]))
                    ins = dve.tensor_scalar(pos_r[:, c, :], r1[:, 7, :], float(N), None, ALU.add)
                    link(ins)
                dve.tensor_copy(e1[:, 0, :], e1[:, 3, :]).then_inc(pos_ok, 1)
                tiles = cf("tiles", NSLOT * E, "p (j e) -> p j e", dict(e=E))
                first_ = e1[:, 3, :].unsqueeze(1).to_broadcast([P, NSLOT, E])
                link(dve.tensor_tensor(j_le[:, :, :], first_, tiles, ALU.is_le))
                link(dve.tensor_tensor(j_eq[:, :, :], first_, tiles, ALU.is_equal))
                for row, (src, name) in enumerate(((j_le, "parity"), (j_le, "even"), (j_le, "odd"),
                                                   (j_le, "next"), (j_eq, "load_0"), (j_eq, "load_1"))):
                    weight = cf(name, E).unsqueeze(1).to_broadcast([P, NSLOT, E])
                    link(dve.tensor_tensor(j_t[:, :, :], src[:, :, :], weight, ALU.mult))
                    link(dve.tensor_reduce(j_f[:, row, :], j_t[:, :, :], AX_X, ALU.add))
                dve.tensor_copy(tab[:, :, :], j_f[:, :, :]).then_inc(tab_ok, 1)

            job(NT, 0, "shared", True, b_prev=B - 1)
            route_a()
            job(NT + 1, 1, "shared", True, b_prev=0)
            route_b()
            job(NT + 2, 0, "shared", True, b_prev=0)
            route_c()
            job(NT + 3, 1, "shared", True, b_prev=0)
            with dve.Fori(1, B) as b:
                for i in range(TT):
                    job(b * TT + (NT + i), i % 2, "shared", True, b_prev=b if i else b - 1)
            job(2 * NT, 0, "shared", True, b_prev=B - 1)
            job(2 * NT + 1, 1, "routed", True)
            with dve.Fori(NT + 1, NJ // 2 - 1) as j:
                for k in range(2):
                    job(j * 2 + k, k, "routed", True)
            job(NJ - 2, 0, "routed", True)
            job(NJ - 1, 1, "routed", False)
            ht_part(NJ - 1)

            for t in range(NT):
                s = t % 2
                dve.wait_ge(f_w1, t + 1)
                dve.scalar_tensor_tensor(out=yg[:, 1, s, :], in0=yg[:, 1, s, :], scalar=top_w[:, 1, t:t + 1],
                                         in1=yg[:, 0, s, :], op0=ALU.mult, op1=ALU.add).then_inc(f_w2, 1)
                dve.wait_ge(f_w2, t + 1)
                dve.tensor_tensor(yg[:, 1, s, :], yg[:, 1, s, :], gb_b[:, t // TT, :], ALU.mult).then_inc(f_gb, 1)


def _experts(w_gate, w_up, w_down, sw_gate, sw_up, sw_down):
    out = np.zeros((P, NX, WE), w_gate.dtype)
    for e in range(NX):
        if e < E:
            g, u, d = w_gate[e], w_up[e], w_down[e]
        else:
            part = slice((e - E) * F, (e - E + 1) * F)
            g, u, d = sw_gate[part], sw_up[part], sw_down[:, part]
        for at, w in ((WG, g), (WU, u)):
            out[:, e, at:at + DC * F] = w.T.reshape(DC, P, F).transpose(1, 0, 2).reshape(P, DC * F)
        rows = np.zeros((FC * P, D), d.dtype)
        rows[:F] = d.T
        out[:, e, WD:] = rows.reshape(FC, P, D).transpose(1, 0, 2).reshape(P, FC * D)
    return out.reshape(P, NX * WE)


def kernel(**inputs):
    import concourse.bacc as _bacc
    from concourse.bass_utils import run_bass_kernel_spmd as _run

    a = {k.replace("L0_", ""): np.asarray(v) for k, v in inputs.items()}
    by_head = [np.ascontiguousarray(a[f"attn_b{i}"].reshape(H, P).T) for i in "qkv"]
    arrays = {
        "x": a["attn_x"].reshape(N, D),
        "wq": a["attn_Wq"], "bq": by_head[0],
        "wk": a["attn_Wk"], "bk": by_head[1],
        "wv": a["attn_Wv"], "bv": by_head[2],
        "wo": a["attn_Wo"], "bo": a["attn_bo"].reshape(1, D),
        "gate_t": a["ffn_gate_weight"].T,
        "wexp": _experts(*(a[f"ffn_{n}"] for n in ("w_gate", "w_up", "w_down", "sw_gate", "sw_up", "sw_down"))),
        "c_t": a["c"].T, "wmod": a["wmod"],
        "ident_in": np.eye(P, dtype=np.float32),
        "causal_in": np.triu(np.full((P, P), MASKED, np.float32), 1),
        "tri_in": np.triu(np.ones((P, P), np.float32), 1),
        "coef_in": coefficients(),
    }
    arrays = {k: np.ascontiguousarray(v) for k, v in arrays.items()}
    nc = _bacc.Bacc("TRN2", target_bir_lowering=False, num_devices=1)
    args = {k: nc.dram_tensor(k, v.shape, mybir.dt.from_np(v.dtype), kind="ExternalInput").ap()
            for k, v in arrays.items()}
    out = nc.dram_tensor("out", (N, D), F32, kind="ExternalOutput").ap()
    adaln_layer(nc, out=out, **args)
    r = _run(nc, [arrays], core_ids=[0])
    return r.results[0]["out"].reshape(B, T, D)
```

```python
from contextlib import ExitStack

import numpy as np
import concourse.bass as bass
from concourse import mybir

F32 = mybir.dt.float32
F32R = mybir.dt.float32r
I32 = mybir.dt.int32
U32 = mybir.dt.uint32
ALU = mybir.AluOpType
ACT = mybir.ActivationFunctionType
AX_X = mybir.AxisListType.X

P = 128
D = 512
DC = D // P
B = 4
T = 512
TT = T // P
NT = B * TT
N = B * T
H = 16
HP = H // 2
HD = H * P
NIT = HP * B
TRI = TT * (TT + 1) // 2 * P
E = 8
F = 352
FC = 3
FK = [P, P, F - 2 * P]
NX = E + 2
WG, WU, WD = 0, DC * F, 2 * DC * F
WE = 2 * DC * F + FC * D
NCH = 4 * NIT
CH = NX * WE // NCH
NSLOT = 2 * NT + E
NJ = 2 * NT + NSLOT
SCALE = float(1.0 / np.sqrt(np.float32(P)))
MASKED = -(2.0 ** 100)
EPS = 1e-5
assert CH * NCH == NX * WE and NSLOT % 2 == 0 and F == sum(FK)

ROW_AT = [r * (r + 1) // 2 * P for r in range(TT)]
PT_GROUPS = [[(0, 0)], [(1, 0), (3, (TT - 1) * P)], [(2, 0)]]
PT_AT = [0, T, 2 * T]
S_PARTS = [(0, 1), (2,), (3,)]
PT_LEN = [T, T, 2 * P]


COEFS = [("iota", NT * E), ("keep", E * NT), ("edges", E * NT), ("one_e", E), ("tiles", NSLOT * E),
         ("parity", E), ("even", E), ("odd", E), ("next", E), ("load_0", E), ("load_1", E)]
COEF_AT = {name: sum(w for _, w in COEFS[:i]) for i, (name, _) in enumerate(COEFS)}
COEF_W = sum(w for _, w in COEFS)


def coefficients():
    e, t, j = np.arange(E), np.arange(NT), np.arange(NSLOT)
    rows = {
        "iota": np.tile(e - E, NT),
        "keep": np.tile(t > 0, E),
        "edges": np.tile(P * t, E),
        "one_e": np.ones(E),
        "tiles": np.repeat(j, E),
        "parity": np.where(e == 0, 0, np.where(e % 2 == 1, 1, -1)),
        "even": 32 * ((e % 2 == 0) + (e == 0)),
        "odd": 32 * ((e % 2 == 1) + (e == 0)),
        "next": np.ones(E),
        "load_0": (e < E - 1) & (e % 2 == 1),
        "load_1": (e < E - 1) & (e % 2 == 0),
    }
    flat = np.concatenate([np.asarray(rows[name], np.float32) for name, _ in COEFS])
    return np.ascontiguousarray(np.broadcast_to(flat, (P, COEF_W)))


def adaln_layer(nc, x, wq, bq, wk, bk, wv, bv, wo, bo, gate_t, wexp, c_t, wmod, ident_in, causal_in,
                tri_in, coef_in, out):
    ctx = ExitStack()
    with ctx:
        def sem(name):
            return ctx.enter_context(nc.semaphore(name))

        def sbuf(scope, name, shape, dt=F32):
            return scope.enter_context(nc.sbuf_tensor(name, shape, dt))

        def dram(name, shape, dt=F32):
            return nc.dram_tensor(name, shape, dt, kind="Internal").ap()

        mod_d = dram("mod_rows", (B, 6 * D))
        q_d = dram("q_transposed", (B, H, P, T))
        wx_hi_d = dram("experts_hi", (P, NX * WE))
        wx_lo_d = dram("experts_lo", (P, NX * WE))
        rows_d = dram("ffn_rows", (N + NSLOT * P, D))
        y_d = dram("slot_results", (NSLOT * P, D))

        bank = [ctx.enter_context(nc.psum_tensor(f"bank{i}", [P, T], F32)) for i in range(8)]

        ident = sbuf(ctx, "ident", [P, P])
        ident_r = sbuf(ctx, "ident_r", [P, P], F32R)
        causal = sbuf(ctx, "causal", [P, P])
        causal_r = sbuf(ctx, "causal_r", [P, P], F32R)
        bq_c = sbuf(ctx, "bq_c", [P, H])
        bk_c = sbuf(ctx, "bk_c", [P, H])
        bv_c = sbuf(ctx, "bv_c", [P, H])
        modc = sbuf(ctx, "modc", [P, 2, DC, B])
        zero = sbuf(ctx, "zero", [P, D])
        acc = sbuf(ctx, "acc", [P, NT, D])
        mh = sbuf(ctx, "minus_half", [P, TT])
        stat = sbuf(ctx, "stat", [P, TT, 6])
        mv = sbuf(ctx, "mean_var", [P, TT, 2])
        ve = sbuf(ctx, "var_eps", [P, TT])
        rs0 = sbuf(ctx, "rstd_seed", [P, TT])
        nt1 = sbuf(ctx, "newton1", [P, TT])
        nt2 = sbuf(ctx, "newton2", [P, TT])
        rstd = sbuf(ctx, "rstd", [P, TT])
        acc_cols = acc[:, :, :].rearrange("p t d -> p (t d)")
        stage = [acc_cols[:, s * DC * D:(s + 1) * DC * D].rearrange("p (c n) -> p c n", c=DC) for s in range(3)]
        x_in = acc_cols[:, 3 * DC * D:4 * DC * D].rearrange("p (i n) -> p i n", i=TT)

        s12 = ExitStack()
        h_hi = sbuf(s12, "h_hi", [P, DC, N], F32R)
        h_lo = sbuf(s12, "h_lo", [P, DC, N], F32R)
        wk_raw = sbuf(s12, "wk_raw", [P, DC, 2 * P])
        wv_raw = sbuf(s12, "wv_raw", [P, DC, 2 * P])
        wo_raw = sbuf(s12, "wo_raw", [P, 2, D])

        s1 = ExitStack()
        wq_hi = sbuf(s1, "wq_hi", [P, DC, HD], F32R)
        wq_lo = sbuf(s1, "wq_lo", [P, DC, HD], F32R)
        q_out = sbuf(s1, "q_out", [P, 4, T])
        h_full = sbuf(s1, "h_full", [P, 2, DC, P])
        c_in = sbuf(s1, "c_in", [P, DC, B])
        c_silu = sbuf(s1, "c_silu", [P, DC, B])
        mod_row = sbuf(s1, "mod_row", [B, 2, D])
        mod_a = sbuf(s1, "mod_a", [B, D])
        mod_s = sbuf(s1, "mod_s", [B, D])
        s1.close()

        s2 = ExitStack()
        wk_hi = sbuf(s2, "wk_hi", [P, DC, 2 * P], F32R)
        wk_lo = sbuf(s2, "wk_lo", [P, DC, 2 * P], F32R)
        wv_hi = sbuf(s2, "wv_hi", [P, DC, 2 * P], F32R)
        wv_lo = sbuf(s2, "wv_lo", [P, DC, 2 * P], F32R)
        wo_hi = sbuf(s2, "wo_hi", [P, 2, D], F32R)
        wo_lo = sbuf(s2, "wo_lo", [P, 2, D], F32R)
        k_hi = sbuf(s2, "k_hi", [P, 2, T], F32R)
        k_lo = sbuf(s2, "k_lo", [P, 2, T], F32R)
        v_hi = sbuf(s2, "v_hi", [P, TT, 2 * P], F32R)
        v_lo = sbuf(s2, "v_lo", [P, TT, 2 * P], F32R)
        o_hi = sbuf(s2, "o_hi", [P, 2, T], F32R)
        o_lo = sbuf(s2, "o_lo", [P, 2, T], F32R)
        q_raw = sbuf(s2, "q_raw", [P, H, 64])
        q_hi = sbuf(s2, "q_hi", [P, 2, T], F32R)
        q_lo = sbuf(s2, "q_lo", [P, 2, T], F32R)
        prob = sbuf(s2, "prob", [P, 2, TRI])
        pt_hi = sbuf(s2, "pt_hi", [P, TRI], F32R)
        pt_lo = sbuf(s2, "pt_lo", [P, TRI], F32R)
        row_max = sbuf(s2, "row_max", [P, 2, TT])
        neg_max = sbuf(s2, "neg_max", [P, 2, TT])
        row_sum = sbuf(s2, "row_sum", [P, 2, TT])
        row_inv = sbuf(s2, "row_inv", [P, 2, TT])
        ch_raw = sbuf(s2, "ch_raw", [P, 2, CH])
        ch_hi = sbuf(s2, "ch_hi", [P, 2, CH], F32R)
        ch_lo = sbuf(s2, "ch_lo", [P, 2, CH], F32R)
        s2.close()
        s12.close()

        s3 = ExitStack()
        ga_b = sbuf(s3, "ga_b", [P, B, D])
        cb_b = sbuf(s3, "cb_b", [P, B, D])
        sb_b = sbuf(s3, "sb_b", [P, B, D])
        gb_b = sbuf(s3, "gb_b", [P, B, D])
        xr = sbuf(s3, "xr", [P, 2, D])
        h2 = sbuf(s3, "h2", [P, 2, D])
        xin = sbuf(s3, "xin", [P, 2, D])
        xt_hi = sbuf(s3, "xt_hi", [P, 2, DC, P], F32R)
        xt_lo = sbuf(s3, "xt_lo", [P, 2, DC, P], F32R)
        gate_s = sbuf(s3, "gate_s", [P, 2, F])
        h_mid = sbuf(s3, "h_mid", [P, 2, F])
        ht_hi = sbuf(s3, "ht_hi", [P, FC, P], F32R)
        ht_lo = sbuf(s3, "ht_lo", [P, FC, P], F32R)
        y_sb = sbuf(s3, "y_sb", [P, 2, D])
        bo_b = sbuf(s3, "bo_b", [P, D])
        g_raw = sbuf(s3, "g_raw", [P, DC, E])
        g_hi = sbuf(s3, "g_hi", [P, DC, E], F32R)
        g_lo = sbuf(s3, "g_lo", [P, DC, E], F32R)
        tri = sbuf(s3, "tri", [P, P])
        sign = sbuf(s3, "sign", [1, 1])
        ones = sbuf(s3, "ones", [P, P])
        coef = sbuf(s3, "coef", [P, COEF_W])
        lg = sbuf(s3, "lg", [P, NT, E])
        sc = sbuf(s3, "sc", [P, NT, E])
        ra = sbuf(s3, "ra", [P, NT, E])
        rb = sbuf(s3, "rb", [P, NT, E])
        oh1 = sbuf(s3, "oh1", [P, NT, E])
        oh2 = sbuf(s3, "oh2", [P, NT, E])
        hot = sbuf(s3, "hot", [P, NT, E])
        slot_base = sbuf(s3, "slot_base", [P, NT, E])
        cnt_et = sbuf(s3, "cnt_et", [P, E, NT])
        cum_et = sbuf(s3, "cum_et", [P, E, NT])
        over = sbuf(s3, "over", [P, E, NT])
        r1 = sbuf(s3, "r1", [P, 8, NT])
        e1 = sbuf(s3, "e1", [P, 4, E])
        top_w = sbuf(s3, "top_w", [P, 2, NT])
        pos_i = sbuf(s3, "pos_i", [P, 2, NT], U32)
        pos_r = sbuf(s3, "pos_r", [P, 2, NT], U32)
        j_le = sbuf(s3, "j_le", [P, NSLOT, E])
        j_eq = sbuf(s3, "j_eq", [P, NSLOT, E])
        j_t = sbuf(s3, "j_t", [P, NSLOT, E])
        j_f = sbuf(s3, "j_f", [P, 6, NSLOT])
        tab = sbuf(s3, "tab", [P, 6, NSLOT], I32)
        yg = sbuf(s3, "yg", [P, 2, D])
        s34 = ExitStack()
        w_hi = sbuf(s34, "w_hi", [P, 2 * WE], F32R)
        w_lo = sbuf(s34, "w_lo", [P, 2 * WE], F32R)
        s34.close()
        rows_0 = sbuf(s3, "rows_0", [P, NT, D])
        rows_1 = sbuf(s3, "rows_1", [P, NT, D])
        s3.close()

        def cf(name, width, *dims):
            a = coef[:, COEF_AT[name]:COEF_AT[name] + width]
            return a.rearrange(*dims[0:1], **dims[1]) if dims else a

        const_ld = sem("const_ld")
        stage_ld = [sem(f"stage_ld{s}") for s in range(3)]
        x_ld = sem("x_ld")
        silu_c = sem("silu_c")
        const_r = sem("const_r")
        mod_full = sem("mod_full")
        mod_ev = sem("mod_ev")
        mod_st = [sem("mod_st0"), sem("mod_st1")]
        modt_full = sem("modt_full")
        modc_ok = sem("modc_ok")
        wq_hi_ok = sem("wq_hi_ok")
        wq_ok = sem("wq_ok")
        dchain = sem("dve_chain")
        mh_ok = sem("minus_half_ok")
        split_hi = sem("split_hi")
        ln_chain = sem("ln_chain")
        ln_var = sem("ln_var")
        ln_seed = sem("ln_seed")
        xn_ok = sem("xn_ok")
        tx_full = sem("tx_full")
        hf_ok = sem("h_full_ok")
        hhi_ok = sem("h_hi_ok")
        hlo_ok = sem("h_lo_ok")
        q_full = sem("q_full")
        q_ev = sem("q_ev")
        q_st = [sem(f"q_st{s}") for s in range(4)]
        zero_ok = sem("zero_ok")
        zero_st = sem("zero_st")
        wk_ld = sem("wk_ld")
        wv_ld = sem("wv_ld")
        wo_ld = sem("wo_ld")
        wk_ok = sem("wk_ok")
        wv_ok = sem("wv_ok")
        wo_ok = sem("wo_ok")
        acc_ok = sem("acc_ok")
        q_ld = sem("q_ld")
        q_ok = sem("q_split")
        k_full = sem("k_full")
        k_hi_ok = sem("k_hi_ok")
        k_ok = sem("k_ok")
        v_full = sem("v_full")
        v_hi_ok = sem("v_hi_ok")
        v_ok = sem("v_ok")
        s_full = sem("s_full")
        s_max = sem("s_max")
        s_neg = sem("s_neg")
        s_exp = sem("s_exp")
        inv_ok = sem("inv_ok")
        p_ok = sem("p_ok")
        pt_full = sem("pt_full")
        pt_hi_ok = sem("pt_hi_ok")
        pt_ok = sem("pt_ok")
        o_full = sem("o_full")
        o_hi_ok = sem("o_hi_ok")
        o_ok = sem("o_ok")
        wo_full = sem("wo_full")
        wo_add = sem("wo_add")
        ch_ld = [sem("ch_ld0"), sem("ch_ld1")]
        ch_ok = sem("ch_ok")
        ch_st = [sem("ch_st0"), sem("ch_st1")]
        c3_ld = sem("stage3_constants")
        xr_ld = [sem("xr_ld0"), sem("xr_ld1")]
        x1_ok = sem("x1_ok")
        c_var = sem("c_var")
        c_seed = sem("c_seed")
        c_xn = sem("c_xn")
        c_chain = sem("c_chain")
        h2_scaled = sem("h2_scaled")
        g_hi_ok = sem("g_hi_ok")
        h2_ok = sem("h2_ok")
        h2_st = [sem("h2_st0"), sem("h2_st1")]
        g_ok = sem("g_ok")
        ones_ok = sem("ones_ok")
        w_ld = [sem("w_ld_even"), sem("w_ld_odd")]
        w_ready = sem("w_ready")
        xin_ld = [sem("xin_ld0"), sem("xin_ld1")]
        xt_full = sem("xt_full")
        xt_hi_ok = sem("xt_hi_ok")
        xt_ok = sem("xt_ok")
        gt_full = sem("gate_full")
        up_full = sem("up_full")
        silu_ok = sem("silu_ok")
        mid_ok = sem("mid_ok")
        ht_full = sem("ht_full")
        ht_hi_ok = sem("ht_hi_ok")
        ht_ok = sem("ht_ok")
        y_full = sem("y_full")
        y_gb = sem("y_gb")
        y_add = sem("y_add")
        y_ev = sem("y_ev")
        y_st = [sem("y_st0"), sem("y_st1")]
        lg_full = sem("lg_full")
        lg_ok = sem("lg_ok")
        rt_sub = sem("rt_sub")
        rt_exp = sem("rt_exp")
        rt_hot = sem("rt_hot")
        rt_cnt = sem("rt_cnt")
        pos_ok = sem("pos_ok")
        tab_ok = sem("tab_ok")
        sc_ld = [sem("sc_ld0"), sem("sc_ld1")]
        sc_st = [sem("sc_st0"), sem("sc_st1")]
        g_ld = [sem(f"g_ld{t}") for t in range(NT)]
        f_w1 = sem("f_w1")
        f_w2 = sem("f_w2")
        f_gb = sem("f_gb")
        f_ok = sem("f_ok")
        out_st = sem("out_st")

        block = ctx.enter_context(nc.Block())

        def wait_apart(eng, *waits):
            waits = [(s, v if isinstance(v, int) else eng.to_reg(v)) for s, v in waits]
            eng.wait_ge(const_ld, 6 * 16)
            for s, v in waits:
                eng.wait_ge(s, v)

        def walk_steps(eng, step):
            step(0, 0, True, False)
            with eng.Fori(0, HP - 1) as p:
                for b in range(1, B):
                    step(p, b, False, False)
                step(p + 1, 0, False, False)
            for b in range(1, B):
                step(HP - 1, b, False, b == B - 1)

        x_t = x.rearrange("(t p) d -> p t d", p=P)
        wq_v = wq.rearrange("(c p) n -> p c n", p=P)
        wk_v = wk.rearrange("(c p) n -> p c n", p=P)
        wv_v = wv.rearrange("(c p) n -> p c n", p=P)
        wo_v = wo.rearrange("(h p) n -> p h n", p=P)
        wmod_v = wmod.rearrange("(c p) n -> p c n", p=P)
        out_t = out.rearrange("(t p) d -> p t d", p=P)
        rows_t = rows_d.rearrange("(t p) d -> p t d", p=P)
        y_t = y_d.rearrange("(t p) d -> p t d", p=P)
        q_v = q_d.rearrange("b j p t -> p b j t")

        loads = [("mod", 0), ("mod", 1)] + [("wq", g) for g in range(4)] + [("mod", m) for m in range(2, 6)]
        load_at = {what: i for i, what in enumerate(loads)}

        def stage1_over(eng):
            eng.wait_ge(q_full, B * H)
            eng.wait_ge(hlo_ok, NT)
            for s in q_st:
                eng.wait_ge(s, 16 * B * H // 4)
            for s in mod_st:
                eng.wait_ge(s, 3 * 16)

        @block.sync
        def _(sp):
            sp.dma_start(c_in[:, :, :], c_t.rearrange("(c p) b -> p c b", p=P)).then_inc(const_ld, 16)
            sp.dma_start(ident[:, :], ident_in).then_inc(const_ld, 16)
            sp.dma_start(causal[:, :], causal_in).then_inc(const_ld, 16)
            sp.dma_start(bq_c[:, :], bq).then_inc(const_ld, 16)
            sp.dma_start(bk_c[:, :], bk).then_inc(const_ld, 16)
            sp.dma_start(bv_c[:, :], bv).then_inc(const_ld, 16)
            sp.dma_start(x_in, x_t[:, 0:TT, :]).then_inc(x_ld, 16)
            for i, (kind, m) in enumerate(loads[:-1]):
                if i >= 3:
                    was, k = loads[i - 3]
                    if was == "mod":
                        sp.wait_ge(mod_full, k + 1)
                    else:
                        sp.wait_ge(wq_ok, k + 1)
                src = (wmod_v if kind == "mod" else wq_v)[:, :, m * D:(m + 1) * D]
                sp.dma_start(stage[i % 3], src).then_inc(stage_ld[i % 3], 16)
                if i == 5:
                    for r in range(2):
                        sp.wait_ge(mod_ev, r + 1)
                        sp.dma_start(mod_d[:, r * D:(r + 1) * D], mod_row[:, r, :]).then_inc(mod_st[r], 16)
            sp.wait_ge(zero_ok, 1)
            slots = rows_d[N:, :].rearrange("(a p) d -> p a d", p=P)
            for a in range(0, NSLOT, 8):
                sp.dma_start(slots[:, a:a + 8, :],
                             zero[:, :].unsqueeze(1).to_broadcast([P, 8, D])).then_inc(zero_st, 16)
            sp.dma_start(wk_raw[:, :, :], wk_v[:, :, 0:2 * P]).then_inc(wk_ld, 16)
            sp.dma_start(wv_raw[:, :, :], wv_v[:, :, 0:2 * P]).then_inc(wv_ld, 16)
            sp.dma_start(wo_raw[:, :, :], wo_v[:, 0:2, :]).then_inc(wo_ld, 16)

            def q_rows(b, more):
                if more:
                    sp.wait_ge(tx_full, b * TT + TT)
                    sp.dma_start(x_in, x_t[:, bass.ds((b + 1) * TT, TT), :]).then_inc(x_ld, 16)
                for j in range(H):
                    sp.wait_ge(q_ev, b * H + (j + 1))
                    sp.dma_start(q_v[:, bass.ds(b, 1), j, :], q_out[:, j % 4, :].unsqueeze(1))\
                      .then_inc(q_st[j % 4], 16)
                    if not more and j == H // 2:
                        store_mod(5)

            def store_mod(m):
                sp.wait_ge(mod_ev, m + 1)
                sp.dma_start(mod_d[:, m * D:(m + 1) * D], mod_row[:, m % 2, :]).then_inc(mod_st[m % 2], 16)

            with sp.Fori(0, B - 1) as b:
                q_rows(b, True)
            sp.wait_ge(mod_full, 3)
            i = len(loads) - 1
            sp.dma_start(stage[i % 3], wmod_v[:, :, 5 * D:6 * D]).then_inc(stage_ld[i % 3], 16)
            for m in range(2, 5):
                store_mod(m)
            q_rows(B - 1, False)

            stage1_over(sp)

            def load_q(p, b):
                sp.dma_start(q_raw[:, :, :], q_v[:, b, :, bass.ds(p * 64, 64)]).then_inc(q_ld, 16)

            load_q(0, 0)
            sp.wait_ge(acc_ok, 1)
            for s in range(2):
                sp.dma_start(ch_raw[:, s, :], wexp[:, s * CH:(s + 1) * CH]).then_inc(ch_ld[s], 16)

            def step(p, b, first, last):
                n = p * B + b
                if not last:
                    sp.wait_ge(q_ok, n * 2 + 2)
                    load_q(p if b < B - 1 else p + 1, (b + 1) % B)
                if b == 1 and not (isinstance(p, int) and p == HP - 1):
                    nxt = (p + 1) * 2 * P
                    sp.wait_ge(wk_ok, p + 1)
                    sp.dma_start(wk_raw[:, :, :], wk_v[:, :, bass.ds(nxt, 2 * P)]).then_inc(wk_ld, 16)
                    sp.wait_ge(wv_ok, p + 1)
                    sp.dma_start(wv_raw[:, :, :], wv_v[:, :, bass.ds(nxt, 2 * P)]).then_inc(wv_ld, 16)
                    sp.wait_ge(wo_ok, p + 1)
                    sp.dma_start(wo_raw[:, :, :], wo_v[:, bass.ds((p + 1) * 2, 2), :]).then_inc(wo_ld, 16)
                for q in range(4):
                    c, s = n * 4 + q, q % 2
                    sp.wait_ge(ch_ok, c + 1)
                    sp.dma_start(wx_hi_d[:, bass.ds(c * CH, CH)], ch_hi[:, s, :].bitcast(F32)).then_inc(ch_st[s], 16)
                    sp.dma_start(wx_lo_d[:, bass.ds(c * CH, CH)], ch_lo[:, s, :].bitcast(F32)).then_inc(ch_st[s], 16)
                    if not (last and q >= 2):
                        sp.dma_start(ch_raw[:, s, :], wexp[:, bass.ds((c + 2) * CH, CH)]).then_inc(ch_ld[s], 16)

            walk_steps(sp, step)

            sp.wait_ge(wo_add, NIT * TT)
            for s in range(2):
                sp.wait_ge(mod_st[s], 3 * 16)
                sp.wait_ge(ch_st[s], 16 * NCH)
            for i, dst in ((2, ga_b), (4, cb_b), (3, sb_b), (5, gb_b)):
                for b in range(B):
                    sp.dma_start(dst[:, b, :], mod_d[b:b + 1, i * D:(i + 1) * D].to_broadcast([P, D]))\
                      .then_inc(c3_ld, 16)
            sp.dma_start(g_raw[:, :, :], gate_t.rearrange("(c p) e -> p c e", p=P)).then_inc(c3_ld, 16)
            sp.dma_start(tri[:, :], tri_in).then_inc(c3_ld, 16)
            sp.dma_start(coef[:, :], coef_in).then_inc(c3_ld, 16)
            sp.dma_start(bo_b[:, :], bo.to_broadcast([P, D])).then_inc(c3_ld, 16)

            def load_xr(t, s):
                sp.dma_start(xr[:, s, :].unsqueeze(1), x_t[:, bass.ds(t, 1), :]).then_inc(xr_ld[s], 16)

            def load_w(e, s):
                sp.dma_start(w_hi[:, s * WE:(s + 1) * WE].bitcast(F32), wx_hi_d[:, e * WE:(e + 1) * WE]).then_inc(w_ld[s], 16)
                sp.dma_start(w_lo[:, s * WE:(s + 1) * WE].bitcast(F32), wx_lo_d[:, e * WE:(e + 1) * WE]).then_inc(w_ld[s], 16)

            load_xr(0, 0)
            load_xr(1, 1)
            load_w(E, 0)
            load_w(E + 1, 1)

            def c_tile(t, i, more):
                s = i % 2
                sp.wait_ge(h2_ok, t + 1)
                sp.dma_start(rows_t[:, bass.ds(t, 1), :], h2[:, s, :].unsqueeze(1)).then_inc(h2_st[s], 16)
                if more:
                    sp.wait_ge(x1_ok, t + 1)
                    load_xr(t + 2, s)

            for b in range(B):
                for i in range(TT):
                    c_tile(b * TT + i, i, b < B - 1 or i < 2)
            sp.wait_ge(y_full, NT)
            load_w(0, 0)
            for t in range(NT):
                if t >= 2:
                    sp.wait_ge(sc_st[t % 2], (t // 2) * 32)
                sp.dma_start(yg[:, t % 2, :], rows_t[:, t, :]).then_inc(sc_ld[t % 2], 16)

            sp.wait_ge(tab_ok, 1)

            def routed(j, first, last):
                for k in range(2):
                    r = j * 2 + k
                    n = r + 2 * NT
                    nxt = sp.value_load(tab[0:1, 3, bass.ds(r, 1)], min_val=1, max_val=E)
                    load = [sp.value_load(tab[0:1, 4 + s, bass.ds(r, 1)], min_val=0, max_val=1) for s in range(2)]
                    wait_apart(sp, (y_full, n))
                    for s in range(2):
                        with sp.If(load[s]):
                            sp.dma_start(w_hi[:, s * WE:(s + 1) * WE].bitcast(F32), wx_hi_d[:, bass.ds(nxt * WE, WE)])\
                              .then_inc(w_ld[s], 16)
                            sp.dma_start(w_lo[:, s * WE:(s + 1) * WE].bitcast(F32), wx_lo_d[:, bass.ds(nxt * WE, WE)])\
                              .then_inc(w_ld[s], 16)
                    if not (first and k == 0):
                        store_y(r - 1, (k + 1) % 2)

            def store_y(r, s):
                sp.wait_ge(y_ev, r + 1)
                sp.dma_start(y_t[:, bass.ds(r, 1), :], y_sb[:, s, :].unsqueeze(1)).then_inc(y_st[s], 16)

            routed(0, True, False)
            with sp.Fori(1, NSLOT // 2 - 1) as j:
                routed(j, False, False)
            routed(NSLOT // 2 - 1, False, True)
            store_y(NSLOT - 1, 1)

            for t in range(NT):
                sp.wait_ge(f_ok, t + 1)
                sp.dma_start(out_t[:, t, :], rows_1[:, t, :]).then_inc(out_st, 16)
            sp.wait_ge(out_st, 16 * NT)
            for s in range(2):
                sp.wait_ge(y_st[s], 16 * NSLOT // 2)
            sp.wait_ge(zero_st, 16 * (NSLOT // 8))

        @block.gpsimd
        def _(pool):
            pool.memset(zero[:, :], 0.0).then_inc(zero_ok, 1)
            pool.memset(mh[:, :], -0.5).then_inc(mh_ok, 1)
            pool.wait_ge(mh_ok, 1)

            def seed(b):
                pool.wait_ge(ln_var, b + 1)
                pool.tensor_tensor(rs0[:, :], ve[:, :], mh[:, :], ALU.pow).then_inc(ln_seed, 1)

            seed(0)
            with pool.Fori(0, B - 1) as b:
                seed(b + 1)

            stage1_over(pool)
            pool.memset(acc[:, :, :], 0.0).then_inc(acc_ok, 1)

            q_nat_hi = q_hi[:, :, :].rearrange("p h (r j) -> p h r j", j=H)
            q_nat_lo = q_lo[:, :, :].rearrange("p h (r j) -> p h r j", j=H)
            q_in = q_raw[:, :, :].rearrange("p j (h r) -> p h r j", h=2)

            def run(what, base):
                for k, (raw, hi, lo, waits, done) in enumerate(what):
                    wait_apart(pool, *waits)
                    pool.tensor_copy(hi, raw).then_inc(split_hi, 1)
                    pool.wait_ge(split_hi, base + (k + 1))
                    pool.tensor_tensor(lo, raw, hi.bitcast(F32), ALU.subtract).then_inc(done, 1)

            SPB = [7, 6, 7, 7]
            SPP = sum(SPB)

            def base_of(p, b):
                done = 4 + sum(SPB[:b])
                if isinstance(p, int) and p == HP - 1 and b == B - 1:
                    done -= 1
                return p * SPP + done

            run([
                (wk_raw[:, :, :], wk_hi[:, :, :], wk_lo[:, :, :], [(wk_ld, 16)], wk_ok),
                (q_in[:, 0], q_nat_hi[:, 0], q_nat_lo[:, 0], [(q_ld, 16)], q_ok),
                (q_in[:, 1], q_nat_hi[:, 1], q_nat_lo[:, 1], [], q_ok),
                (wv_raw[:, :, :], wv_hi[:, :, :], wv_lo[:, :, :], [(wv_ld, 16)], wv_ok)], 0)

            def step(p, b, first, last):
                n = p * B + b
                base = base_of(p, b)
                k = 0
                for h in range(2):
                    if not last:
                        run([(q_in[:, h], q_nat_hi[:, h], q_nat_lo[:, h],
                                    [(q_ld, n * 16 + 32), (s_full, n * 6 + (3 * h + 3))], q_ok)], base + k)
                        k += 1
                for q in range(4):
                    c, s = n * 4 + q, q % 2
                    waits = [(ch_ld[s], n * 32 + (q // 2 + 1) * 16)]
                    if not (first and q < 2):
                        waits.append((ch_st[s], n * 64 + (q // 2) * 32))
                    run([(ch_raw[:, s, :], ch_hi[:, s, :], ch_lo[:, s, :], waits, ch_ok)], base + k)
                    k += 1
                at_end = isinstance(p, int) and p == HP - 1
                if b == 0:
                    waits = [(wo_ld, p * 16 + 16)]
                    if not first:
                        waits.append((wo_full, n * TT))
                    run([(wo_raw[:, :, :], wo_hi[:, :, :], wo_lo[:, :, :], waits, wo_ok)], base + k)
                    k += 1
                if b == 2 and not at_end:
                    run([(wk_raw[:, :, :], wk_hi[:, :, :], wk_lo[:, :, :],
                                [(wk_ld, p * 16 + 32), (k_full, n * 2 + 4)], wk_ok)], base + k)
                    k += 1
                if b == 3 and not at_end:
                    run([(wv_raw[:, :, :], wv_hi[:, :, :], wv_lo[:, :, :],
                                [(wv_ld, p * 16 + 32), (v_full, n * 2 + 2)], wv_ok)], base + k)
                    k += 1
                assert at_end or k == SPB[b]

            walk_steps(pool, step)

            pool.wait_ge(wo_add, NIT * TT)
            pool.memset(ones[:, :], 1.0).then_inc(ones_ok, 1)
            pool.wait_ge(c3_ld, 16 * (4 * B + 4))

            def c_tile(b, i, t):
                s = i % 2
                pool.wait_ge(c_var, t + 1)
                pool.tensor_tensor(rs0[:, s:s + 1], ve[:, s:s + 1], mh[:, s:s + 1], ALU.pow).then_inc(c_seed, 1)
                wait_apart(pool, (c_xn, t + 1))
                pool.tensor_tensor(h2[:, s, :].unsqueeze(1), h2[:, s, :].unsqueeze(1), cb_b[:, bass.ds(b, 1), :], ALU.mult)\
                    .then_inc(h2_scaled, 1)
                wait_apart(pool, (h2_scaled, t + 1))
                pool.tensor_tensor(h2[:, s, :].unsqueeze(1), h2[:, s, :].unsqueeze(1), sb_b[:, bass.ds(b, 1), :], ALU.add)\
                    .then_inc(h2_ok, 1)

            def add_y(t, n, s):
                wait_apart(pool, (y_gb, n + 1))
                pool.tensor_tensor(acc[:, bass.ds(t, 1), :], acc[:, bass.ds(t, 1), :], y_sb[:, s, :].unsqueeze(1),
                                   ALU.add).then_inc(y_add, 1)

            for t in range(TT):
                c_tile(0, t, t)

            def quad0(b, hidden, first):
                for i in range(TT):
                    n = b * TT + i
                    if hidden:
                        c_tile(b + 1, i, n + TT)
                    if not (first and i == 0):
                        add_y(n - 1, n - 1, (i + 1) % 2)

            quad0(0, True, True)
            with pool.Fori(1, B - 1) as b:
                quad0(b, True, False)
            quad0(B - 1, False, False)

            def scatter(t, k, count):
                pool.wait_ge(sc_ld[k], count)
                for c in range(2):
                    pool.indirect_dma_start(
                        out=rows_d, out_offset=bass.IndirectOffsetOnAxis(ap=pos_r[:, c, t:t + 1], axis=0),
                        in_=yg[:, k, :], in_offset=None,
                        bounds_check=N + NSLOT * P - 1, oob_is_err=True).then_inc(sc_st[k], 16)

            for b in range(B):
                for i in range(TT):
                    n = NT + b * TT + i
                    add_y((n - 1) % NT, n - 1, (i + 1) % 2)
                    if b in (1, 2):
                        if b == 1 and i == 0:
                            pool.wait_ge(pos_ok, 1)
                            pool.wait_ge(zero_st, 16 * (NSLOT // 8))
                        for k in range(2):
                            t = (b - 1) * 2 * TT + 2 * i + k
                            scatter(t, k, 16 * (t // 2 + 1))

            pool.wait_ge(tab_ok, 1)

            def weights_ready(r):
                loads = [pool.value_load(tab[0:1, 1 + s, bass.ds(r, 1)], min_val=32, max_val=32 * E)
                         for s in range(2)]
                own = [] if isinstance(r, int) else [(w_ready, r)]
                wait_apart(pool, (w_ld[0], loads[0]), (w_ld[1], loads[1]), *own)
                pool.memset(sign[:, :], 1.0).then_inc(w_ready, 1)

            weights_ready(0)
            add_y(NT - 1, 2 * NT - 1, 1)
            with pool.Fori(1, NSLOT) as r:
                weights_ready(r)

            pool.wait_ge(y_full, NJ)
            for s in range(2):
                pool.wait_ge(y_st[s], 16 * NSLOT // 2)
            for t in range(NT):
                for c, rows in enumerate((rows_0, rows_1)):
                    pool.indirect_dma_start(
                        out=rows[:, t, :], out_offset=None, in_=y_d,
                        in_offset=bass.IndirectOffsetOnAxis(ap=pos_i[:, c, t:t + 1], axis=0),
                        bounds_check=NSLOT * P - 1, oob_is_err=True).then_inc(g_ld[t], 16)

        @block.scalar
        def _(act):
            act.wait_ge(const_ld, 6 * 16)
            act.activation(c_silu[:, :, :], c_in[:, :, :], ACT.Silu).then_inc(silu_c, 1)
            for g in range(4):
                i = load_at["wq", g]
                act.wait_ge(stage_ld[i % 3], 16 * (i // 3 + 1))
                act.activation(wq_hi[:, :, g * D:(g + 1) * D], stage[i % 3], ACT.Copy).then_inc(wq_hi_ok, 1)
                if g == 0:
                    for i in range(TT):
                        act.wait_ge(hf_ok, i + 1)
                        act.activation(h_hi[:, :, i * P:(i + 1) * P], h_full[:, i % 2], ACT.Copy)\
                           .then_inc(hhi_ok, 1)

            def q_rows(b, more, first):
                for j in range(H):
                    act.wait_ge(q_full, b * H + (j + 1))
                    if not (first and j < 4):
                        act.wait_ge(q_st[j % 4], b * (16 * H // 4) + 16 * (j // 4))
                    act.activation(q_out[:, j % 4, :], bank[j % 4][:, :], ACT.Identity,
                                   bias=bq_c[:, j:j + 1]).then_inc(q_ev, 1)
                    if more and j >= 11 and j < 15:
                        i = j - 11
                        wait_apart(act, (hf_ok, b * TT + (TT + i + 1)))
                        act.activation(h_hi[:, :, bass.ds((b + 1) * T + i * P, P)], h_full[:, i % 2],
                                       ACT.Copy).then_inc(hhi_ok, 1)

            q_rows(0, True, True)
            with act.Fori(1, B - 1) as b:
                q_rows(b, True, False)
            q_rows(B - 1, False, False)

            stage1_over(act)

            def k_part(p, n, h):
                wait_apart(act, (k_full, n * 2 + (h + 1)))
                act.activation(k_hi[:, h, :], bank[h][:, :], ACT.Identity,
                               bias=bk_c[:, bass.ds(p * 2 + h, 1)]).then_inc(k_hi_ok, 1)

            k_part(0, 0, 0)
            k_part(0, 0, 1)

            def step(p, b, first, last):
                n = p * B + b

                def exps(i):
                    h, rows = i // 3, S_PARTS[i % 3]
                    if i % 3 == 0 and not first:
                        act.wait_ge(pt_full, n * 6 + (3 * h - 3))
                    act.wait_ge(s_neg, n * 6 + (i + 1))
                    for r in rows:
                        at = ROW_AT[r] - ROW_AT[rows[0]]
                        ins = act.activation(prob[:, h, ROW_AT[r]:ROW_AT[r] + (r + 1) * P],
                                             bank[2 + i % 2][:, at:at + (r + 1) * P], ACT.Exp,
                                             bias=neg_max[:, h, r:r + 1], scale=SCALE,
                                             accum_out=row_sum[:, h, r:r + 1])
                    ins.then_inc(s_exp, 1)

                def v_part(g):
                    if g == 0 and not first:
                        act.wait_ge(o_full, n * 2)
                    act.wait_ge(v_full, n * 2 + (g + 1))
                    act.activation(v_hi[:, 2 * g:2 * g + 2, :], bank[g][:, :].rearrange("p (i n) -> p i n", i=2),
                                   ACT.Copy).then_inc(v_hi_ok, 1)

                def pt_part(h, g):
                    if g == 0 and not (first and h == 0):
                        act.wait_ge(o_full, n * 2 + h)
                    act.wait_ge(pt_full, n * 6 + (3 * h + g + 1))
                    act.activation(pt_hi[:, PT_AT[g]:PT_AT[g] + PT_LEN[g]], bank[4 + g % 2][:, 0:PT_LEN[g]],
                                   ACT.Copy).then_inc(pt_hi_ok, 1)

                def o_part(h):
                    free = [(wo_full, n * TT)] if h == 0 and not first else []
                    wait_apart(act, *free, (o_full, n * 2 + (h + 1)))
                    act.activation(o_hi[:, h, :], bank[6 + h][:, :], ACT.Identity,
                                   bias=bv_c[:, bass.ds(p * 2 + h, 1)]).then_inc(o_hi_ok, 1)

                pn = p if b < B - 1 else p + 1
                for i in range(5):
                    exps(i)
                v_part(0)
                exps(5)
                v_part(1)
                pt_part(0, 0)
                pt_part(0, 1)
                if not last:
                    k_part(pn, n + 1, 0)
                pt_part(0, 2)
                o_part(0)
                for g in range(3):
                    pt_part(1, g)
                o_part(1)
                if not last:
                    k_part(pn, n + 1, 1)

            walk_steps(act, step)

            act.wait_ge(wo_add, NIT * TT)

            def xt_part(n, s):
                act.wait_ge(xt_full, n + 1)
                act.activation(xt_hi[:, s], bank[2][:, :].rearrange("p (c n) -> p c n", c=DC), ACT.Copy)\
                   .then_inc(xt_hi_ok, 1)

            def load_xin(m, s, tile):
                act.dma_start(xin[:, s, :].unsqueeze(1), rows_t[:, bass.ds(tile, 1), :]).then_inc(xin_ld[s], 16)

            def load_hidden(m, s):
                act.wait_ge(h2_st[s], (m - s) * 8 + 16)
                load_xin(m, s, m)

            def job(n, s, prev, nxt, load="again"):
                act.wait_ge(gt_full, n + 1)
                act.activation(gate_s[:, s, :], bank[0][:, 0:F], ACT.Silu).then_inc(silu_ok, 1)
                if prev:
                    ht_part(n - 1)
                if nxt:
                    if not (isinstance(n, int) and n == 0):
                        act.wait_ge(up_full, n)
                    xt_part(n + 1, 1 - s)
                if load == "first":
                    load_hidden(n + 3, 1 - s)
                elif load == "again":
                    load_xin(n + 3, 1 - s, n + (3 - NT))
                if prev == "routed":
                    y_part(n - 1, 1 - s)

            def ht_part(m):
                act.wait_ge(ht_full, m + 1)
                for f in range(FC):
                    ins = act.activation(ht_hi[0:FK[f], f, :], bank[3][0:FK[f], f * P:(f + 1) * P], ACT.Copy)
                ins.then_inc(ht_hi_ok, 1)

            def y_part(m, s):
                act.wait_ge(y_full, m + 1)
                if not (isinstance(m, int) and m < 2 * NT + 2):
                    act.wait_ge(y_st[s], (m - (2 * NT + s)) * 8)
                act.activation(y_sb[:, s, :], bank[4 + s][:, :], ACT.Copy).then_inc(y_ev, 1)

            load_hidden(0, 0)
            load_hidden(1, 1)
            xt_part(0, 0)
            load_hidden(2, 0)
            job(0, 0, None, True, "first")
            job(1, 1, "shared", True, "first")
            with act.Fori(1, NT // 2 - 2) as j:
                for k in range(2):
                    job(j * 2 + k, k, "shared", True, "first")
            job(NT - 4, 0, "shared", True, "first")
            for n in range(NT - 3, NT + 1):
                job(n, n % 2, "shared", True)
            act.wait_ge(rt_sub, 1)
            act.activation(sc[:, :, :], ra[:, :, :], ACT.Exp).then_inc(rt_exp, 1)
            job(NT + 1, 1, "shared", True)
            with act.Fori(NT // 2 + 1, NT - 2) as j:
                for k in range(2):
                    job(j * 2 + k, k, "shared", True)
            job(2 * NT - 4, 0, "shared", True)
            for s in range(2):
                act.wait_ge(sc_st[s], 16 * NT)
            for n in range(2 * NT - 3, 2 * NT):
                job(n, n % 2, "shared", True)
            job(2 * NT, 0, "shared", True)
            act.wait_ge(y_add, 2 * NT)
            job(2 * NT + 1, 1, "routed", True)
            with act.Fori(NT + 1, NJ // 2 - 2) as j:
                for k in range(2):
                    job(j * 2 + k, k, "routed", True)
            job(NJ - 4, 0, "routed", True)
            job(NJ - 3, 1, "routed", True, None)
            job(NJ - 2, 0, "routed", True, None)
            job(NJ - 1, 1, "routed", False, None)
            ht_part(NJ - 1)
            y_part(NJ - 1, 1)

            for t in range(NT):
                act.wait_ge(g_ld[t], 32)
                act.activation(rows_0[:, t, :], rows_0[:, t, :], ACT.Copy, scale=top_w[:, 0, t:t + 1])\
                   .then_inc(f_w1, 1)

        @block.tensor
        def _(pe):
            def mm3(dst, terms):
                k, last = 0, 3 * len(terms) - 1
                for sh, sl, mh_, ml in terms:
                    for a, m in ((sh, mh_), (sh, ml), (sl, mh_)):
                        ins = pe.matmul(dst, a, m, start=(k == 0), stop=(k == last))
                        k += 1
                return ins

            pe.wait_ge(const_ld, 6 * 16)
            pe.wait_ge(silu_c, 1)

            def mod_piece(m):
                i = load_at["mod", m]
                pe.wait_ge(stage_ld[i % 3], 16 * (i // 3 + 1))
                if m >= 1:
                    pe.wait_ge(mod_ev, m)
                for c in range(DC):
                    ins = pe.matmul(bank[6][0:B, :], c_silu[:, c, :], stage[i % 3][:, c, :],
                                    start=(c == 0), stop=(c == DC - 1))
                ins.then_inc(mod_full, 1)

            for m in range(2):
                mod_piece(m)
            for m in range(2):
                pe.wait_ge(mod_ev, m + 1)
                for c in range(DC):
                    ins = pe.transpose(bank[7][:, (m * DC + c) * B:(m * DC + c + 1) * B],
                                       mod_row[:, m, c * P:(c + 1) * P], ident[0:B, 0:B])
            ins.then_inc(modt_full, 1)

            def transposes(b, i):
                pe.wait_ge(xn_ok, b * TT + (i + 1))
                if not (isinstance(b, int) and b == 0 and i < 2):
                    pe.wait_ge(hf_ok, b * TT + (i - 1))
                for c in range(DC):
                    ins = pe.transpose(bank[4 + i % 2][:, c * P:(c + 1) * P], x_in[:, i, c * P:(c + 1) * P],
                                       ident[:, :])
                ins.then_inc(tx_full, 1)

            for i in range(TT):
                transposes(0, i)

            def q_rows(b, more, first):
                cols = bass.ds(b * T, T)
                pe.wait_ge(hlo_ok, b * TT + TT)
                for j in range(H):
                    if first and j % 4 == 0:
                        pe.wait_ge(wq_ok, j // 4 + 1)
                    if not (first and j < 4):
                        pe.wait_ge(q_ev, b * H + (j - 3))
                    mm3(bank[j % 4][:, :],
                        [(wq_hi[:, c, j * P:(j + 1) * P], wq_lo[:, c, j * P:(j + 1) * P],
                          h_hi[:, c, cols], h_lo[:, c, cols]) for c in range(DC)]).then_inc(q_full, 1)
                    if more and j >= 10 and j < 14:
                        transposes(b + 1, j - 10)
                    if not more and j == H // 2 - 1:
                        mod_piece(5)

            q_rows(0, True, True)
            with pe.Fori(1, B - 1) as b:
                q_rows(b, True, False)
            for m in range(2, 5):
                mod_piece(m)
            q_rows(B - 1, False, False)

            pe.wait_ge(const_r, 2)
            pe.wait_ge(q_ev, B * H)
            pe.wait_ge(mod_ev, 6)
            pe.wait_ge(hlo_ok, NT)

            def keys(n, pair, b, h, chunks):
                if chunks[0] == 0:
                    pe.wait_ge(wk_ok, pair + 1)
                    if not (isinstance(n, int) and n == 0):
                        pe.wait_ge(v_ok, n * 2 + (h - 1))
                for c in chunks:
                    for k, (a, m) in enumerate(((wk_hi, h_hi), (wk_hi, h_lo), (wk_lo, h_hi))):
                        ins = pe.matmul(bank[h][:, :], a[:, c, h * P:(h + 1) * P], m[:, c, b * T:(b + 1) * T],
                                        start=(c == 0 and k == 0), stop=(c == DC - 1 and k == 2))
                if chunks[-1] == DC - 1:
                    ins.then_inc(k_full, 1)

            for h in range(2):
                keys(0, 0, 0, h, range(DC))

            def out_tile(m, pair, i, after):
                if i == 0:
                    pe.wait_ge(wo_ok, pair + 1)
                    pe.wait_ge(o_ok, m * 2 + 2)
                if after:
                    pe.wait_ge(*after)
                mm3(bank[i % 2][:, :],
                    [(o_hi[:, h, i * P:(i + 1) * P], o_lo[:, h, i * P:(i + 1) * P],
                      wo_hi[:, h, :], wo_lo[:, h, :]) for h in range(2)]).then_inc(wo_full, 1)

            def step(p, b, first, last):
                n = p * B + b

                def scores(i):
                    h, rows = i // 3, S_PARTS[i % 3]
                    if i % 3 == 0:
                        pe.wait_ge(k_ok, n * 2 + (h + 1))
                        pe.wait_ge(q_ok, n * 2 + (h + 1))
                    if not (first and i < 2):
                        pe.wait_ge(s_exp, n * 6 + (i - 1))
                    for r in rows:
                        w = (r + 1) * P
                        at = ROW_AT[r] - ROW_AT[rows[0]]
                        dst = bank[2 + i % 2][:, at:at + w]
                        for k, (a, m) in enumerate(((q_hi, k_hi), (q_hi, k_lo), (q_lo, k_hi))):
                            pe.matmul(dst, a[:, h, r * P:w], m[:, h, 0:w], start=(k == 0), stop=False)
                        ins = pe.matmul(dst[:, r * P:w], ident_r[:, :], causal_r[:, :], start=False, stop=True)
                    ins.then_inc(s_full, 1)

                def values(t):
                    g, i = t // 2, t % 2
                    if i == 0:
                        pe.wait_ge(wv_ok, p + 1)
                        if not first:
                            pe.wait_ge(wo_add, n * TT + (g - 1))
                    rows = slice((b * TT + t) * P, (b * TT + t + 1) * P)
                    ins = mm3(bank[g][:, i * 2 * P:(i + 1) * 2 * P],
                              [(h_hi[:, c, rows], h_lo[:, c, rows], wv_hi[:, c, :], wv_lo[:, c, :])
                               for c in range(DC)])
                    if i == 1:
                        ins.then_inc(v_full, 1)

                def turn(h, groups):
                    if groups[0] == 0:
                        pe.wait_ge(p_ok, n * 6 + (3 * h + 3))
                    for g in groups:
                        blocks = PT_GROUPS[g]
                        if not (first and h == 0 and g < 2):
                            pe.wait_ge(pt_ok, n * 6 + (3 * h + (1 if g == 2 else 0)))
                        for k, at in blocks:
                            for r in range(k, TT):
                                ins = pe.transpose(
                                    bank[4 + g % 2][:, at + (r - k) * P:at + (r - k + 1) * P],
                                    prob[:, h, ROW_AT[r] + k * P:ROW_AT[r] + (k + 1) * P], ident[:, :])
                        ins.then_inc(pt_full, 1)

                def weigh(h):
                    if not first:
                        pe.wait_ge(o_ok, n * 2 + (h - 1))
                    for g, blocks in enumerate(PT_GROUPS):
                        pe.wait_ge(pt_ok, n * 6 + (3 * h + g + 1))
                        pe.wait_ge(v_ok, n * 2 + (1 if g == 0 else 2))
                        for k, at in blocks:
                            w = (TT - k) * P
                            cols = slice(PT_AT[g] + at, PT_AT[g] + at + w)
                            vals = slice(h * P, (h + 1) * P)
                            for q, (a, m) in enumerate(((v_hi, pt_hi), (v_hi, pt_lo), (v_lo, pt_hi))):
                                ins = pe.matmul(bank[6 + h][:, k * P:T], a[:, k, vals], m[:, cols],
                                                start=(k == 0 and q == 0), stop=(g == 2 and q == 2))
                    ins.then_inc(o_full, 1)

                def project(i):
                    if not first:
                        free = [(k_ok, n * 2 + 1), (k_ok, n * 2 + 2), (wo_add, n * TT - 3), (wo_add, n * TT - 2)][i]
                        out_tile(n - 1, p if b > 0 else p - 1, i, free)

                def next_keys(h, chunks):
                    if not last:
                        keys(n + 1, p if b < B - 1 else p + 1, (b + 1) % B, h, chunks)

                scores(0)
                scores(1)
                project(0)
                project(1)
                scores(2)
                project(2)
                scores(3)
                project(3)
                values(0)
                scores(4)
                values(1)
                scores(5)
                values(2)
                values(3)
                turn(0, (0, 1))
                next_keys(0, range(DC))
                turn(0, (2,))
                weigh(0)
                turn(1, (0, 1))
                next_keys(1, range(DC // 2))
                turn(1, (2,))
                weigh(1)
                next_keys(1, range(DC // 2, DC))

            walk_steps(pe, step)
            out_tile(NIT - 1, HP - 1, 0, (v_ok, 2 * NIT - 1))
            out_tile(NIT - 1, HP - 1, 1, (v_ok, 2 * NIT))
            out_tile(NIT - 1, HP - 1, 2, (wo_add, NIT * TT - 3))
            out_tile(NIT - 1, HP - 1, 3, (wo_add, NIT * TT - 2))

            pe.wait_ge(wo_add, NIT * TT)
            pe.wait_ge(pt_ok, NIT * 6)
            pe.wait_ge(o_ok, NIT * 2)

            def turn_rows(n, s, count):
                pe.wait_ge(xin_ld[s], count)
                if not (isinstance(n, int) and n == 0):
                    pe.wait_ge(xt_ok, n)
                for c in range(DC):
                    ins = pe.transpose(bank[2][:, c * P:(c + 1) * P], xin[:, s, c * P:(c + 1) * P], ident[:, :])
                ins.then_inc(xt_full, 1)

            def half(n, s, wofs, which):
                if which == 0:
                    pe.wait_ge(xt_ok, n + 1)
                if not (isinstance(n, int) and n == 0):
                    pe.wait_ge((silu_ok, mid_ok)[which], n)
                at = (WG, WU)[which]
                mm3(bank[which][:, 0:F],
                    [(xt_hi[:, s, c, :], xt_lo[:, s, c, :], w_hi[:, wcol(wofs, at + c * F, F)],
                      w_lo[:, wcol(wofs, at + c * F, F)]) for c in range(DC)])\
                    .then_inc((gt_full, up_full)[which], 1)

            def wcol(wofs, at, width):
                if isinstance(wofs, int):
                    return slice(wofs + at, wofs + at + width)
                return bass.ds(wofs + at, width)

            def logits(n, s):
                if not (isinstance(n, int) and n == 0):
                    pe.wait_ge(lg_ok, n)
                mm3(bank[6][:, 0:E],
                    [(xt_hi[:, s, c, :], xt_lo[:, s, c, :], g_hi[:, c, :], g_lo[:, c, :])
                     for c in range(DC)]).then_inc(lg_full, 1)

            def turn_mid(m, s):
                pe.wait_ge(mid_ok, m + 1)
                if not (isinstance(m, int) and m == 0):
                    pe.wait_ge(ht_ok, m)
                for f in range(FC):
                    ins = pe.transpose(bank[3][0:FK[f], f * P:(f + 1) * P],
                                       h_mid[:, s, f * P:f * P + FK[f]], ident[:, :])
                ins.then_inc(ht_full, 1)

            def down(m, s, wofs, free):
                pe.wait_ge(ht_ok, m + 1)
                if free:
                    pe.wait_ge(*free)
                mm3(bank[4 + s][:, :],
                    [(ht_hi[0:FK[f], f, :], ht_lo[0:FK[f], f, :], w_hi[0:FK[f], wcol(wofs, WD + f * D, D)],
                      w_lo[0:FK[f], wcol(wofs, WD + f * D, D)]) for f in range(FC)]).then_inc(y_full, 1)

            def job(n, s, wofs, prev_ofs, route=False, prev=True, nxt=True, free=None):
                half(n, s, wofs, 0)
                if prev:
                    turn_mid(n - 1, 1 - s)
                half(n, s, wofs, 1)
                if route:
                    logits(n, s)
                if nxt:
                    turn_rows(n + 1, 1 - s, xcount(n + 1, 1 - s))
                if prev:
                    down(n - 1, 1 - s, prev_ofs, free)

            def xcount(m, s):
                return (m - s) * 8 + 16

            pe.wait_ge(g_ok, 1)
            turn_rows(0, 0, 16)
            pe.wait_ge(w_ld[0], 32)
            job(0, 0, 0, 0, route=True, prev=False)
            job(1, 1, 0, 0, route=True)
            job(2, 0, 0, 0, route=True)
            job(3, 1, 0, 0, route=True, free=(y_gb, 1))
            with pe.Fori(2, NT // 2) as j:
                for k in range(2):
                    job(j * 2 + k, k, 0, 0, route=True, free=(y_gb, j * 2 + (k - 2)))
            pe.wait_ge(w_ld[1], 32)
            job(NT, 0, WE, 0, free=(y_gb, NT - 2))
            job(NT + 1, 1, WE, WE, free=(y_gb, NT - 1))
            pe.wait_ge(rt_hot, 1)
            pe.wait_ge(ones_ok, 1)
            hot_cols = hot[:, :, :].rearrange("p t e -> p (t e)")
            pe.matmul(bank[7][:, 0:NT * E], tri[:, :], hot_cols, start=True, stop=True)
            pe.matmul(bank[7][:, NT * E:2 * NT * E], ones[:, :], hot_cols, start=True, stop=True)\
              .then_inc(rt_cnt, 1)
            with pe.Fori(NT // 2 + 1, NT) as j:
                for k in range(2):
                    job(j * 2 + k, k, WE, WE, free=(y_gb, j * 2 + (k - 2)))

            pe.wait_ge(tab_ok, 1)

            def read(row, r, most):
                return pe.value_load(tab[0:1, row, bass.ds(r, 1)], min_val=0, max_val=most)

            def routed(j, first, last):
                for k in range(2):
                    r = j * 2 + k
                    n = r + 2 * NT
                    if k == 1:
                        was = par
                    par = read(0, r, 1)
                    if first and k == 0:
                        free, prev_ofs = (y_gb, n - 2), WE
                    else:
                        prev_ofs = (was if k == 1 else read(0, r - 1, 1)) * WE
                        if first:
                            free = (y_gb, 2 * NT - 1)
                        elif k == 0 and isinstance(j, int) and j == 1:
                            free = (y_gb, 2 * NT)
                        else:
                            free = (y_ev, r - 2)
                    pe.wait_ge(w_ready, r + 1)
                    job(n, k, par * WE, prev_ofs, nxt=not (last and k == 1), free=free)

            routed(0, True, False)
            routed(1, False, False)
            with pe.Fori(2, NSLOT // 2 - 1) as j:
                routed(j, False, False)
            routed(NSLOT // 2 - 1, False, True)
            turn_mid(NJ - 1, 1)
            down(NJ - 1, 1, read(0, NSLOT - 1, 1) * WE, (y_ev, NSLOT - 2))

        @block.vector
        def _(dve):
            dve.wait_ge(const_ld, 6 * 16)
            dve.tensor_copy(ident_r[:, :], ident[:, :]).then_inc(const_r, 1)
            dve.tensor_copy(causal_r[:, :], causal[:, :]).then_inc(const_r, 1)

            dc = [0]

            def link(ins):
                dc[0] += 1
                ins.then_inc(dchain, 1)
                dve.wait_ge(dchain, dc[0])

            def mod_piece(m):
                dst = mod_row[:, m % 2, :]
                if m >= 2:
                    dve.wait_ge(mod_st[m % 2], 16 * (m // 2))
                dve.wait_ge(mod_full, m + 1)
                src = bank[6][0:B, :]
                if m in (1, 4):
                    dve.tensor_scalar(dst, src, 1.0, None, ALU.add).then_inc(mod_ev, 1)
                elif m in (0, 3):
                    dve.tensor_copy(dst, src).then_inc(mod_ev, 1)
                else:
                    link(dve.tensor_scalar(mod_a[:, :], src, -1.0, None, ALU.mult))
                    link(dve.tensor_tensor(mod_a[:, :], mod_a[:, :], src, ALU.max))
                    link(dve.tensor_scalar(mod_a[:, :], mod_a[:, :], 0.25, None, ALU.max))
                    link(dve.tensor_scalar(mod_s[:, :], src, 0.0, 2.0, ALU.is_ge, ALU.mult))
                    dve.scalar_tensor_tensor(out=dst, in0=mod_s[:, :], scalar=-1.0, in1=mod_a[:, :],
                                             op0=ALU.add, op1=ALU.mult).then_inc(mod_ev, 1)

            def norm_stats(b, base):
                wait_apart(dve, (x_ld, b * 16 + 16))
                k = [0]

                def chain(ins):
                    k[0] += 1
                    ins.then_inc(ln_chain, 1)
                    wait_apart(dve, (ln_chain, base + k[0]))

                for i in range(TT):
                    ins = dve.bn_stats(stat[:, i, :], x_in[:, i, :])
                chain(ins)
                for i in range(TT):
                    ins = dve.bn_aggr(mv[:, i, :], stat[:, i, :])
                chain(ins)
                dve.tensor_scalar(ve[:, :], mv[:, :, 1], EPS, None, ALU.add).then_inc(ln_var, 1)
                dve.wait_ge(ln_seed, b + 1)
                chain(dve.tensor_tensor(nt1[:, :], rs0[:, :], rs0[:, :], ALU.mult))
                chain(dve.tensor_tensor(nt2[:, :], nt1[:, :], ve[:, :], ALU.mult))
                chain(dve.tensor_scalar(nt1[:, :], nt2[:, :], -0.5, 1.5, ALU.mult, ALU.add))
                chain(dve.tensor_tensor(rstd[:, :], nt1[:, :], rs0[:, :], ALU.mult))
                for i in range(TT):
                    dve.tensor_scalar(x_in[:, i, :], x_in[:, i, :], mv[:, i, 0:1], rstd[:, i:i + 1],
                                      ALU.subtract, ALU.mult).then_inc(xn_ok, 1)

            LN_CHAIN = 6

            def modulate(b, i, first):
                dve.wait_ge(tx_full, b * TT + (i + 1))
                if not (first and i < 2):
                    dve.wait_ge(hlo_ok, b * TT + (i - 1))
                for c in range(DC):
                    ins = dve.tensor_scalar(h_full[:, i % 2, c, :], bank[4 + i % 2][:, c * P:(c + 1) * P],
                                            modc[:, 1, c, bass.ds(b, 1)], modc[:, 0, c, bass.ds(b, 1)],
                                            ALU.mult, ALU.add)
                ins.then_inc(hf_ok, 1)

            def h_low(b, i):
                dve.wait_ge(hhi_ok, b * TT + (i + 1))
                cols = bass.ds(b * T + i * P, P)
                dve.tensor_tensor(h_lo[:, :, cols], h_full[:, i % 2], h_hi[:, :, cols].bitcast(F32), ALU.subtract)\
                    .then_inc(hlo_ok, 1)

            norm_stats(0, 0)
            mod_piece(0)
            mod_piece(1)
            dve.wait_ge(modt_full, 1)
            dve.tensor_copy(modc[:, :, :, :].rearrange("p m c b -> p (m c b)"), bank[7][:, 0:2 * DC * B])\
                .then_inc(modc_ok, 1)
            dve.wait_ge(modc_ok, 1)
            def wq_low(g):
                i = load_at["wq", g]
                dve.wait_ge(wq_hi_ok, g + 1)
                dve.tensor_tensor(wq_lo[:, :, g * D:(g + 1) * D], stage[i % 3],
                                  wq_hi[:, :, g * D:(g + 1) * D].bitcast(F32), ALU.subtract).then_inc(wq_ok, 1)

            wq_low(0)
            for i in range(TT):
                modulate(0, i, True)
                if i:
                    h_low(0, i - 1)
            h_low(0, TT - 1)
            for g in range(1, 4):
                wq_low(g)

            def batch(b, first=False):
                norm_stats(b, b * LN_CHAIN)
                for i in range(TT):
                    modulate(b, i, False)
                    if i:
                        h_low(b, i - 1)
                h_low(b, TT - 1)

            with dve.Fori(1, B) as b:
                batch(b)
            for m in range(2, 6):
                mod_piece(m)

            stage1_over(dve)

            def low(dst, src, hi, bias, done):
                if bias is None:
                    dve.tensor_tensor(dst, src, hi.bitcast(F32), ALU.subtract).then_inc(done, 1)
                else:
                    dve.scalar_tensor_tensor(out=dst, in0=src, scalar=bias, in1=hi.bitcast(F32),
                                             op0=ALU.add, op1=ALU.subtract).then_inc(done, 1)

            def k_part(p, n, h):
                dve.wait_ge(k_hi_ok, n * 2 + (h + 1))
                low(k_lo[:, h, :], bank[h][:, :], k_hi[:, h, :], bk_c[:, bass.ds(p * 2 + h, 1)], k_ok)

            k_part(0, 0, 0)
            k_part(0, 0, 1)
            dve.wait_ge(acc_ok, 1)

            def step(p, b, first, last):
                n = p * B + b

                def maxima(i):
                    h, rows = i // 3, S_PARTS[i % 3]
                    dve.wait_ge(s_full, n * 6 + (i + 1))
                    for r in rows:
                        at = ROW_AT[r] - ROW_AT[rows[0]]
                        ins = dve.tensor_reduce(row_max[:, h, r:r + 1], bank[2 + i % 2][:, at:at + (r + 1) * P],
                                                AX_X, ALU.max)
                    ins.then_inc(s_max, 1)
                    dve.wait_ge(s_max, n * 6 + (i + 1))
                    cols = slice(rows[0], rows[-1] + 1)
                    dve.tensor_scalar(neg_max[:, h, cols], row_max[:, h, cols], -SCALE, None,
                                      ALU.mult).then_inc(s_neg, 1)

                def normalise(i):
                    h, rows = i // 3, S_PARTS[i % 3]
                    dve.wait_ge(s_exp, n * 6 + (i + 1))
                    cols = slice(rows[0], rows[-1] + 1)
                    dve.reciprocal(row_inv[:, h, cols], row_sum[:, h, cols]).then_inc(inv_ok, 1)
                    wait_apart(dve, (inv_ok, n * 6 + (i + 1)))
                    for r in rows:
                        part = prob[:, h, ROW_AT[r]:ROW_AT[r] + (r + 1) * P]
                        ins = dve.tensor_scalar(part, part, row_inv[:, h, r:r + 1], None, ALU.mult)
                    ins.then_inc(p_ok, 1)

                def v_part(g):
                    dve.wait_ge(v_hi_ok, n * 2 + (g + 1))
                    low(v_lo[:, 2 * g:2 * g + 2, :], bank[g][:, :].rearrange("p (i n) -> p i n", i=2),
                        v_hi[:, 2 * g:2 * g + 2, :], None, v_ok)

                def pt_part(h, g):
                    dve.wait_ge(pt_hi_ok, n * 6 + (3 * h + g + 1))
                    cols = slice(PT_AT[g], PT_AT[g] + PT_LEN[g])
                    low(pt_lo[:, cols], bank[4 + g % 2][:, 0:PT_LEN[g]], pt_hi[:, cols], None, pt_ok)

                def o_part(h):
                    dve.wait_ge(o_hi_ok, n * 2 + (h + 1))
                    low(o_lo[:, h, :], bank[6 + h][:, :], o_hi[:, h, :], bv_c[:, bass.ds(p * 2 + h, 1)], o_ok)

                def add(i):
                    if not first:
                        add_out(n - 1, (b - 1) % B, i)

                pn = p if b < B - 1 else p + 1
                maxima(0)
                maxima(1)
                normalise(0)
                add(0)
                add(1)
                maxima(2)
                normalise(1)
                add(2)
                maxima(3)
                normalise(2)
                add(3)
                maxima(4)
                normalise(3)
                v_part(0)
                maxima(5)
                normalise(4)
                v_part(1)
                normalise(5)
                pt_part(0, 0)
                pt_part(0, 1)
                if not last:
                    k_part(pn, n + 1, 0)
                pt_part(0, 2)
                o_part(0)
                for g in range(3):
                    pt_part(1, g)
                o_part(1)
                if not last:
                    k_part(pn, n + 1, 1)

            def add_out(m, b, i):
                dve.wait_ge(wo_full, m * TT + (i + 1))
                t = b * TT + i
                dve.tensor_tensor(acc[:, t, :], acc[:, t, :], bank[i % 2][:, :], ALU.add).then_inc(wo_add, 1)

            walk_steps(dve, step)
            for i in range(TT):
                add_out(NIT - 1, B - 1, i)

            dve.wait_ge(wo_add, NIT * TT)
            dve.wait_ge(c3_ld, 16 * (4 * B + 4))
            dve.tensor_copy(g_hi[:, :, :], g_raw[:, :, :]).then_inc(g_hi_ok, 1)
            dve.wait_ge(g_hi_ok, 1)
            dve.tensor_tensor(g_lo[:, :, :], g_raw[:, :, :], g_hi[:, :, :].bitcast(F32), ALU.subtract)\
                .then_inc(g_ok, 1)

            C_CHAIN = 8

            def c_tile(b, i, t):
                s = i % 2
                base = t * C_CHAIN
                k = [0]

                def chain(ins):
                    k[0] += 1
                    ins.then_inc(c_chain, 1)
                    wait_apart(dve, (c_chain, base + k[0]))

                a = acc[:, bass.ds(t, 1), :]
                chain(dve.tensor_tensor(a, a, bo_b[:, :].unsqueeze(1), ALU.add))
                chain(dve.tensor_tensor(a, a, ga_b[:, bass.ds(b, 1), :], ALU.mult))
                dve.wait_ge(xr_ld[s], (t - s) * 8 + 16)
                dve.tensor_tensor(a, a, xr[:, s, :].unsqueeze(1), ALU.add).then_inc(x1_ok, 1)
                wait_apart(dve, (x1_ok, t + 1))
                chain(dve.bn_stats(stat[:, s, :], acc[:, bass.ds(t, 1), :].rearrange("p a d -> p (a d)")))
                chain(dve.bn_aggr(mv[:, s, :], stat[:, s, :]))
                dve.tensor_scalar(ve[:, s:s + 1], mv[:, s, 1:2], EPS, None, ALU.add).then_inc(c_var, 1)
                dve.wait_ge(c_seed, t + 1)
                r = slice(s, s + 1)
                chain(dve.tensor_tensor(nt1[:, r], rs0[:, r], rs0[:, r], ALU.mult))
                chain(dve.tensor_tensor(nt2[:, r], nt1[:, r], ve[:, r], ALU.mult))
                chain(dve.tensor_scalar(nt1[:, r], nt2[:, r], -0.5, 1.5, ALU.mult, ALU.add))
                chain(dve.tensor_tensor(rstd[:, r], nt1[:, r], rs0[:, r], ALU.mult))
                if not (isinstance(t, int) and t < 2):
                    dve.wait_ge(h2_st[s], (t - s) * 8)
                dve.tensor_scalar(h2[:, s, :].unsqueeze(1), a, mv[:, s, 0:1], rstd[:, r],
                                  ALU.subtract, ALU.mult).then_inc(c_xn, 1)

            def xt_part(n, s):
                dve.wait_ge(xt_hi_ok, n + 1)
                low(xt_lo[:, s], bank[2][:, :].rearrange("p (c n) -> p c n", c=DC), xt_hi[:, s], None, xt_ok)

            def ht_part(m):
                dve.wait_ge(ht_hi_ok, m + 1)
                for f in range(FC):
                    ins = dve.tensor_tensor(ht_lo[0:FK[f], f, :], bank[3][0:FK[f], f * P:(f + 1) * P],
                                            ht_hi[0:FK[f], f, :].bitcast(F32), ALU.subtract)
                ins.then_inc(ht_ok, 1)

            def y_part(m, s, b):
                dve.wait_ge(y_full, m + 1)
                if not (isinstance(m, int) and m < 2):
                    dve.wait_ge(y_add, m - 1)
                dve.tensor_tensor(y_sb[:, s, :].unsqueeze(1), bank[4 + s][:, :].unsqueeze(1),
                                  gb_b[:, bass.ds(b, 1), :], ALU.mult).then_inc(y_gb, 1)

            def job(n, s, prev, nxt, b_prev=None, route=False):
                if prev:
                    ht_part(n - 1)
                dve.wait_ge(up_full, n + 1)
                dve.wait_ge(silu_ok, n + 1)
                if not (isinstance(n, int) and n < 2):
                    dve.wait_ge(ht_full, n - 1)
                dve.tensor_tensor(h_mid[:, s, :], gate_s[:, s, :], bank[1][:, 0:F], ALU.mult).then_inc(mid_ok, 1)
                if nxt:
                    xt_part(n + 1, 1 - s)
                if route:
                    dve.wait_ge(lg_full, n + 1)
                    dve.tensor_copy(lg[:, bass.ds(n, 1), :], bank[6][:, 0:E].unsqueeze(1)).then_inc(lg_ok, 1)
                if prev == "shared":
                    y_part(n - 1, 1 - s, b_prev)

            for t in range(TT):
                c_tile(0, t, t)
            xt_part(0, 0)

            def quad0(b, hidden, first):
                for i in range(TT):
                    n = b * TT + i
                    job(n, i % 2, None if first and i == 0 else "shared", True,
                        b_prev=b if i else b - 1, route=True)
                    if hidden:
                        c_tile(b + 1, i, n + TT)

            quad0(0, True, True)
            with dve.Fori(1, B - 1) as b:
                quad0(b, True, False)
            quad0(B - 1, False, False)

            def bt(a):
                return a.unsqueeze(2).to_broadcast([P, NT, E])

            def route_a():
                dve.wait_ge(lg_ok, NT)
                link(dve.tensor_reduce(r1[:, 0, :], lg[:, :, :], AX_X, ALU.max))
                dve.tensor_tensor(ra[:, :, :], lg[:, :, :], bt(r1[:, 0, :]), ALU.subtract).then_inc(rt_sub, 1)

            iota_e = cf("iota", NT * E, "p (t e) -> p t e", dict(e=E))

            def first_of(scores_, top, hot_):
                link(dve.tensor_reduce(top, scores_, AX_X, ALU.max))
                link(dve.tensor_tensor(ra[:, :, :], scores_, bt(top), ALU.is_equal))
                link(dve.tensor_tensor(ra[:, :, :], ra[:, :, :], iota_e, ALU.mult))
                link(dve.tensor_reduce(r1[:, 1, :], ra[:, :, :], AX_X, ALU.min))
                link(dve.tensor_tensor(hot_, iota_e, bt(r1[:, 1, :]), ALU.is_equal))

            def route_b():
                dve.wait_ge(rt_exp, 1)
                link(dve.tensor_reduce(r1[:, 0, :], sc[:, :, :], AX_X, ALU.add))
                link(dve.reciprocal(r1[:, 2, :], r1[:, 0, :]))
                link(dve.tensor_tensor(sc[:, :, :], sc[:, :, :], bt(r1[:, 2, :]), ALU.mult))
                first_of(sc[:, :, :], r1[:, 3, :], oh1[:, :, :])
                link(dve.scalar_tensor_tensor(out=rb[:, :, :], in0=oh1[:, :, :], scalar=-4.0,
                                              in1=sc[:, :, :], op0=ALU.mult, op1=ALU.add))
                first_of(rb[:, :, :], r1[:, 4, :], oh2[:, :, :])
                dve.tensor_tensor(hot[:, :, :], oh1[:, :, :], oh2[:, :, :], ALU.add).then_inc(rt_hot, 1)
                link(dve.tensor_tensor(r1[:, 5, :], r1[:, 3, :], r1[:, 4, :], ALU.add))
                link(dve.tensor_scalar(r1[:, 5, :], r1[:, 5, :], 1e-20, None, ALU.add))
                link(dve.reciprocal(r1[:, 6, :], r1[:, 5, :]))
                for c in range(2):
                    link(dve.tensor_tensor(top_w[:, c, :], r1[:, 3 + c, :], r1[:, 6, :], ALU.mult))

            def route_c():
                dve.wait_ge(rt_cnt, 1)
                before = bank[7][:, 0:NT * E].rearrange("p (t e) -> p t e", e=E)
                count = bank[7][:, NT * E:2 * NT * E].rearrange("p (t e) -> p e t", e=E)
                link(dve.tensor_copy(cnt_et[:, :, :], count))
                flat = "p e t -> p (e t)"
                link(dve.tensor_tensor_scan(cum_et[:, :, :].rearrange(flat), cf("keep", NT * E),
                                            cnt_et[:, :, :].rearrange(flat), 0.0, ALU.mult, ALU.add))
                total = cum_et[:, :, NT - 1:NT]
                link(dve.tensor_tensor(over[:, :, :], total.to_broadcast([P, E, NT]),
                                       cf("edges", NT * E, "p (e t) -> p e t", dict(t=NT)), ALU.is_gt))
                link(dve.tensor_reduce(e1[:, 0, :], over[:, :, :], AX_X, ALU.add))
                link(dve.tensor_scalar(e1[:, 1, :], e1[:, 0, :], 1.0, None, ALU.max))
                link(dve.tensor_tensor_scan(e1[:, 2, :], cf("one_e", E), e1[:, 1, :], 0.0, ALU.mult, ALU.add))
                link(dve.tensor_tensor(e1[:, 3, :], e1[:, 2, :], e1[:, 1, :], ALU.subtract))
                link(dve.tensor_tensor(cum_et[:, :, :], cum_et[:, :, :], cnt_et[:, :, :], ALU.subtract))
                link(dve.scalar_tensor_tensor(
                    out=over[:, :, :], in0=e1[:, 3, :].unsqueeze(2).to_broadcast([P, E, NT]), scalar=float(P),
                    in1=cum_et[:, :, :], op0=ALU.mult, op1=ALU.add))
                link(dve.tensor_tensor(slot_base[:, :, :], before, over[:, :, :].rearrange("p e t -> p t e"),
                                       ALU.add))
                for c, hot_ in enumerate((oh1, oh2)):
                    link(dve.tensor_tensor(ra[:, :, :], slot_base[:, :, :], hot_[:, :, :], ALU.mult))
                    link(dve.tensor_reduce(r1[:, 7, :], ra[:, :, :], AX_X, ALU.add))
                    link(dve.tensor_copy(pos_i[:, c, :], r1[:, 7, :]))
                    ins = dve.tensor_scalar(pos_r[:, c, :], r1[:, 7, :], float(N), None, ALU.add)
                    link(ins)
                dve.tensor_copy(e1[:, 0, :], e1[:, 3, :]).then_inc(pos_ok, 1)
                tiles = cf("tiles", NSLOT * E, "p (j e) -> p j e", dict(e=E))
                first_ = e1[:, 3, :].unsqueeze(1).to_broadcast([P, NSLOT, E])
                link(dve.tensor_tensor(j_le[:, :, :], first_, tiles, ALU.is_le))
                link(dve.tensor_tensor(j_eq[:, :, :], first_, tiles, ALU.is_equal))
                for row, (src, name) in enumerate(((j_le, "parity"), (j_le, "even"), (j_le, "odd"),
                                                   (j_le, "next"), (j_eq, "load_0"), (j_eq, "load_1"))):
                    weight = cf(name, E).unsqueeze(1).to_broadcast([P, NSLOT, E])
                    link(dve.tensor_tensor(j_t[:, :, :], src[:, :, :], weight, ALU.mult))
                    link(dve.tensor_reduce(j_f[:, row, :], j_t[:, :, :], AX_X, ALU.add))
                dve.tensor_copy(tab[:, :, :], j_f[:, :, :]).then_inc(tab_ok, 1)

            job(NT, 0, "shared", True, b_prev=B - 1)
            route_a()
            job(NT + 1, 1, "shared", True, b_prev=0)
            route_b()
            job(NT + 2, 0, "shared", True, b_prev=0)
            route_c()
            job(NT + 3, 1, "shared", True, b_prev=0)
            with dve.Fori(1, B) as b:
                for i in range(TT):
                    job(b * TT + (NT + i), i % 2, "shared", True, b_prev=b if i else b - 1)
            job(2 * NT, 0, "shared", True, b_prev=B - 1)
            job(2 * NT + 1, 1, "routed", True)
            with dve.Fori(NT + 1, NJ // 2 - 1) as j:
                for k in range(2):
                    job(j * 2 + k, k, "routed", True)
            job(NJ - 2, 0, "routed", True)
            job(NJ - 1, 1, "routed", False)
            ht_part(NJ - 1)

            for t in range(NT):
                a = rows_1[:, t, :]
                dve.wait_ge(f_w1, t + 1)
                dve.scalar_tensor_tensor(out=a, in0=a, scalar=top_w[:, 1, t:t + 1],
                                         in1=rows_0[:, t, :], op0=ALU.mult, op1=ALU.add).then_inc(f_w2, 1)
                dve.wait_ge(f_w2, t + 1)
                dve.tensor_tensor(a, a, gb_b[:, t // TT, :], ALU.mult).then_inc(f_gb, 1)
                dve.wait_ge(f_gb, t + 1)
                dve.tensor_tensor(a, a, acc[:, t, :], ALU.add).then_inc(f_ok, 1)


def _experts(w_gate, w_up, w_down, sw_gate, sw_up, sw_down):
    out = np.zeros((P, NX, WE), w_gate.dtype)
    for e in range(NX):
        if e < E:
            g, u, d = w_gate[e], w_up[e], w_down[e]
        else:
            part = slice((e - E) * F, (e - E + 1) * F)
            g, u, d = sw_gate[part], sw_up[part], sw_down[:, part]
        for at, w in ((WG, g), (WU, u)):
            out[:, e, at:at + DC * F] = w.T.reshape(DC, P, F).transpose(1, 0, 2).reshape(P, DC * F)
        rows = np.zeros((FC * P, D), d.dtype)
        rows[:F] = d.T
        out[:, e, WD:] = rows.reshape(FC, P, D).transpose(1, 0, 2).reshape(P, FC * D)
    return out.reshape(P, NX * WE)


def kernel(**inputs):
    import concourse.bacc as _bacc
    from concourse.bass_utils import run_bass_kernel_spmd as _run

    a = {k.replace("L0_", ""): np.asarray(v) for k, v in inputs.items()}
    by_head = [np.ascontiguousarray(a[f"attn_b{i}"].reshape(H, P).T) for i in "qkv"]
    arrays = {
        "x": a["attn_x"].reshape(N, D),
        "wq": a["attn_Wq"], "bq": by_head[0],
        "wk": a["attn_Wk"], "bk": by_head[1],
        "wv": a["attn_Wv"], "bv": by_head[2],
        "wo": a["attn_Wo"], "bo": a["attn_bo"].reshape(1, D),
        "gate_t": a["ffn_gate_weight"].T,
        "wexp": _experts(*(a[f"ffn_{n}"] for n in ("w_gate", "w_up", "w_down", "sw_gate", "sw_up", "sw_down"))),
        "c_t": a["c"].T, "wmod": a["wmod"],
        "ident_in": np.eye(P, dtype=np.float32),
        "causal_in": np.triu(np.full((P, P), MASKED, np.float32), 1),
        "tri_in": np.triu(np.ones((P, P), np.float32), 1),
        "coef_in": coefficients(),
    }
    arrays = {k: np.ascontiguousarray(v) for k, v in arrays.items()}
    nc = _bacc.Bacc("TRN2", target_bir_lowering=False, num_devices=1)
    args = {k: nc.dram_tensor(k, v.shape, mybir.dt.from_np(v.dtype), kind="ExternalInput").ap()
            for k, v in arrays.items()}
    out = nc.dram_tensor("out", (N, D), F32, kind="ExternalOutput").ap()
    adaln_layer(nc, out=out, **args)
    r = _run(nc, [arrays], core_ids=[0])
    return r.results[0]["out"].reshape(B, T, D)
```

```python
from contextlib import ExitStack

import numpy as np
import concourse.bass as bass
from concourse import mybir

F32 = mybir.dt.float32
F32R = mybir.dt.float32r
I32 = mybir.dt.int32
U32 = mybir.dt.uint32
ALU = mybir.AluOpType
ACT = mybir.ActivationFunctionType
AX_X = mybir.AxisListType.X

P = 128
D = 512
DC = D // P
B = 4
T = 512
TT = T // P
NT = B * TT
N = B * T
H = 16
HP = H // 2
HD = H * P
NIT = HP * B
TRI = TT * (TT + 1) // 2 * P
E = 8
F = 352
FC = 3
FK = [P, P, F - 2 * P]
NX = E + 2
WG, WU, WD = 0, DC * F, 2 * DC * F
WE = 2 * DC * F + FC * D
NCH = 4 * NIT
CH = NX * WE // NCH
NSLOT = 2 * NT + E
NJ = 2 * NT + NSLOT
MOD_PIECES = {1: 2, 3: 3, 5: 4, 9: 5}
MOD_STORES = {3: 2, 5: 3, 7: 4, 11: 5}
SCATTER_AT = NT + 6
SCALE = float(1.0 / np.sqrt(np.float32(P)))
MASKED = -(2.0 ** 100)
EPS = 1e-5
assert CH * NCH == NX * WE and NSLOT % HP == 0 and F == sum(FK)

ROW_AT = [r * (r + 1) // 2 * P for r in range(TT)]
PT_GROUPS = [[(0, 0)], [(1, 0), (3, (TT - 1) * P)], [(2, 0)]]
PT_AT = [0, T, 2 * T]
S_PARTS = [(0, 1), (2,), (3,)]
PT_LEN = [T, T, 2 * P]


COEFS = [("iota", NT * E), ("keep", E * NT), ("edges", E * NT), ("one_e", E), ("tiles", NSLOT * E),
         ("parity", E), ("even", E), ("odd", E), ("next", E), ("load_0", E), ("load_1", E)]
COEF_AT = {name: sum(w for _, w in COEFS[:i]) for i, (name, _) in enumerate(COEFS)}
COEF_W = sum(w for _, w in COEFS)


def coefficients():
    e, t, j = np.arange(E), np.arange(NT), np.arange(NSLOT)
    rows = {
        "iota": np.tile(e - E, NT),
        "keep": np.tile(t > 0, E),
        "edges": np.tile(P * t, E),
        "one_e": np.ones(E),
        "tiles": np.repeat(j, E),
        "parity": np.where(e == 0, 0, np.where(e % 2 == 1, 1, -1)),
        "even": 32 * (e % 2 == 0),
        "odd": 32 * ((e % 2 == 1) + (e == 0)),
        "next": np.ones(E),
        "load_0": (e < E - 1) & (e % 2 == 1),
        "load_1": (e < E - 1) & (e % 2 == 0),
    }
    flat = np.concatenate([np.asarray(rows[name], np.float32) for name, _ in COEFS])
    return np.ascontiguousarray(np.broadcast_to(flat, (P, COEF_W)))


def adaln_layer(nc, x, wq, bq, wk, bk, wv, bv, wo, bo, gate_t, wexp, c_t, wmod, ident_in, causal_in,
                tri_in, coef_in, out):
    ctx = ExitStack()
    with ctx:
        def sem(name):
            return ctx.enter_context(nc.semaphore(name))

        def sbuf(scope, name, shape, dt=F32):
            return scope.enter_context(nc.sbuf_tensor(name, shape, dt))

        def dram(name, shape, dt=F32):
            return nc.dram_tensor(name, shape, dt, kind="Internal").ap()

        mod_d = dram("mod_rows", (B, 6 * D))
        q_d = dram("q_transposed", (B, H, P, T))
        wx_hi_d = dram("experts_hi", (P, NX * WE))
        wx_lo_d = dram("experts_lo", (P, NX * WE))
        rows_d = dram("ffn_rows", (N + NSLOT * P, D))
        y_d = dram("slot_results", (NSLOT * P, D))

        bank = [ctx.enter_context(nc.psum_tensor(f"bank{i}", [P, T], F32)) for i in range(8)]

        ident = sbuf(ctx, "ident", [P, P])
        causal = sbuf(ctx, "causal", [P, P])
        bq_c = sbuf(ctx, "bq_c", [P, H])
        bk_c = sbuf(ctx, "bk_c", [P, H])
        bv_c = sbuf(ctx, "bv_c", [P, H])
        modc = sbuf(ctx, "modc", [P, 2, DC, B])
        zero = sbuf(ctx, "zero", [P, D])
        bo_b = sbuf(ctx, "bo_b", [P, D])
        acc = sbuf(ctx, "acc", [P, NT, D])
        mh = sbuf(ctx, "minus_half", [P, TT])
        stat = sbuf(ctx, "stat", [P, TT, 6])
        mv = sbuf(ctx, "mean_var", [P, TT, 2])
        ve = sbuf(ctx, "var_eps", [P, TT])
        rs0 = sbuf(ctx, "rstd_seed", [P, TT])
        nt1 = sbuf(ctx, "newton1", [P, TT])
        nt2 = sbuf(ctx, "newton2", [P, TT])
        rstd = sbuf(ctx, "rstd", [P, TT])
        acc_cols = acc[:, :, :].rearrange("p t d -> p (t d)")
        stage = [acc_cols[:, s * DC * D:(s + 1) * DC * D].rearrange("p (c n) -> p c n", c=DC) for s in range(3)]
        x_in = acc_cols[:, 3 * DC * D:4 * DC * D].rearrange("p (i n) -> p i n", i=TT)

        s12 = ExitStack()
        h_hi = sbuf(s12, "h_hi", [P, B * DC, T], F32R)
        h_lo = sbuf(s12, "h_lo", [P, B * DC, T], F32R)
        wk_raw = sbuf(s12, "wk_raw", [P, DC, 2 * P])
        wv_raw = sbuf(s12, "wv_raw", [P, DC, 2 * P])
        wo_raw = sbuf(s12, "wo_raw", [P, 2, D])
        wk_hi = sbuf(s12, "wk_hi", [P, DC, 2 * P], F32R)
        wk_lo = sbuf(s12, "wk_lo", [P, DC, 2 * P], F32R)

        s1 = ExitStack()
        wq_hi = sbuf(s1, "wq_hi", [P, DC, HD], F32R)
        wq_lo = sbuf(s1, "wq_lo", [P, DC, HD], F32R)
        q_out = sbuf(s1, "q_out", [P, 4, T])
        h_full = sbuf(s1, "h_full", [P, 2, DC, P])
        c_in = sbuf(s1, "c_in", [P, DC, B])
        c_silu = sbuf(s1, "c_silu", [P, DC, B])
        mod_row = sbuf(s1, "mod_row", [B, 2, D])
        mod_a = sbuf(s1, "mod_a", [B, D])
        mod_s = sbuf(s1, "mod_s", [B, D])
        s1.close()

        s2 = ExitStack()
        wv_hi = sbuf(s2, "wv_hi", [P, DC, 2 * P], F32R)
        wv_lo = sbuf(s2, "wv_lo", [P, DC, 2 * P], F32R)
        k_hi = sbuf(s2, "k_hi", [P, 2, T], F32R)
        wo_hi = sbuf(s2, "wo_hi", [P, 2, D], F32R)
        wo_lo = sbuf(s2, "wo_lo", [P, 2, D], F32R)
        v_hi = sbuf(s2, "v_hi", [P, TT, 2 * P], F32R)
        v_lo = sbuf(s2, "v_lo", [P, TT, 2 * P], F32R)
        o_hi = sbuf(s2, "o_hi", [P, 2, T], F32R)
        o_lo = sbuf(s2, "o_lo", [P, 2, T], F32R)
        k_lo = sbuf(s2, "k_lo", [P, 2, T], F32R)
        q_hi = sbuf(s2, "q_hi", [P, 2, T], F32R)
        q_lo = sbuf(s2, "q_lo", [P, 2, T], F32R)
        q_raw = sbuf(s2, "q_raw", [P, H, 64])
        prob = sbuf(s2, "prob", [P, 2, TRI])
        pt_hi = sbuf(s2, "pt_hi", [P, TRI], F32R)
        pt_lo = sbuf(s2, "pt_lo", [P, TRI], F32R)
        row_max = sbuf(s2, "row_max", [P, 2, TT])
        neg_max = sbuf(s2, "neg_max", [P, 2, TT])
        row_sum = sbuf(s2, "row_sum", [P, 2, TT])
        row_inv = sbuf(s2, "row_inv", [P, 2, TT])
        ch_raw = sbuf(s2, "ch_raw", [P, 2, CH])
        ch_hi = sbuf(s2, "ch_hi", [P, 2, CH], F32R)
        ch_lo = sbuf(s2, "ch_lo", [P, 2, CH], F32R)
        s2.close()
        s12.close()

        s3 = ExitStack()
        mods = sbuf(s3, "mods", [P, B, 4, D])
        xr = sbuf(s3, "xr", [P, TT, D])
        h2 = sbuf(s3, "h2", [P, TT, D])
        xin = sbuf(s3, "xin", [P, 2, D])
        xt_hi = sbuf(s3, "xt_hi", [P, 2, DC, P], F32R)
        xt_lo = sbuf(s3, "xt_lo", [P, 2, DC, P], F32R)
        y_sb = sbuf(s3, "y_sb", [P, 2, D])
        g_raw = sbuf(s3, "g_raw", [P, DC, E])
        tri = sbuf(s3, "tri", [P, P])
        coef = sbuf(s3, "coef", [P, COEF_W])
        gate_s = sbuf(s3, "gate_s", [P, 2, F])
        h_mid = sbuf(s3, "h_mid", [P, 2, F])
        ht_hi = sbuf(s3, "ht_hi", [P, FC, P], F32R)
        ht_lo = sbuf(s3, "ht_lo", [P, FC, P], F32R)
        g_hi = sbuf(s3, "g_hi", [P, DC, E], F32R)
        g_lo = sbuf(s3, "g_lo", [P, DC, E], F32R)
        sign = sbuf(s3, "sign", [1, 1])
        ones = sbuf(s3, "ones", [P, P])
        lg = sbuf(s3, "lg", [P, NT, E])
        sc = sbuf(s3, "sc", [P, NT, E])
        ra = sbuf(s3, "ra", [P, NT, E])
        rb = sbuf(s3, "rb", [P, NT, E])
        oh1 = sbuf(s3, "oh1", [P, NT, E])
        oh2 = sbuf(s3, "oh2", [P, NT, E])
        hot = sbuf(s3, "hot", [P, NT, E])
        slot_base = sbuf(s3, "slot_base", [P, NT, E])
        cnt_et = sbuf(s3, "cnt_et", [P, E, NT])
        cum_et = sbuf(s3, "cum_et", [P, E, NT])
        over = sbuf(s3, "over", [P, E, NT])
        r1 = sbuf(s3, "r1", [P, 8, NT])
        e1 = sbuf(s3, "e1", [P, 4, E])
        top_w = sbuf(s3, "top_w", [P, 2, NT])
        pos_i = sbuf(s3, "pos_i", [P, 2, NT], U32)
        pos_r = sbuf(s3, "pos_r", [P, 2, NT], U32)
        j_le = sbuf(s3, "j_le", [P, NSLOT, E])
        j_eq = sbuf(s3, "j_eq", [P, NSLOT, E])
        j_t = sbuf(s3, "j_t", [P, NSLOT, E])
        j_f = sbuf(s3, "j_f", [P, 6, NSLOT])
        tab = sbuf(s3, "tab", [P, 6, NSLOT], I32)
        s34 = ExitStack()
        w_hi = sbuf(s34, "w_hi", [P, 2 * WE], F32R)
        w_lo = sbuf(s34, "w_lo", [P, 2 * WE], F32R)
        s34.close()
        rows_0 = sbuf(s3, "rows_0", [P, NT, D])
        rows_1 = sbuf(s3, "rows_1", [P, NT, D])
        s3.close()

        def cf(name, width, *dims):
            a = coef[:, COEF_AT[name]:COEF_AT[name] + width]
            return a.rearrange(*dims[0:1], **dims[1]) if dims else a

        const_ld = sem("const_ld")
        c_ld = sem("c_ld")
        stage_ld = [sem(f"stage_ld{s}") for s in range(3)]
        x_ld = sem("x_ld")
        silu_c = sem("silu_c")
        mod_full = sem("mod_full")
        mod_ev = sem("mod_ev")
        mod_st = [sem("mod_st0"), sem("mod_st1")]
        modt_full = sem("modt_full")
        modc_ok = sem("modc_ok")
        wq_hi_ok = sem("wq_hi_ok")
        wq_ok = sem("wq_ok")
        dchain = sem("dve_chain")
        mh_ok = sem("minus_half_ok")
        split_hi = sem("split_hi")
        ln_chain = sem("ln_chain")
        ln_var = sem("ln_var")
        ln_seed = sem("ln_seed")
        xn_ok = sem("xn_ok")
        tx_full = sem("tx_full")
        hf_ok = sem("h_full_ok")
        hhi_ok = sem("h_hi_ok")
        hlo_ok = sem("h_lo_ok")
        q_full = sem("q_full")
        q_ev = sem("q_ev")
        q_st = [sem(f"q_st{s}") for s in range(4)]
        zero_ok = sem("zero_ok")
        zero_st = sem("zero_st")
        wk_ld = sem("wk_ld")
        wv_ld = sem("wv_ld")
        wo_ld = sem("wo_ld")
        wk_ok = sem("wk_ok")
        wv_ok = sem("wv_ok")
        wv_hi_ok = sem("wv_hi_ok")
        wo_ok = sem("wo_ok")
        acc_ok = sem("acc_ok")
        q_ld = sem("q_ld")
        q_ok = sem("q_split")
        k_full = sem("k_full")
        k_hi_ok = sem("k_hi_ok")
        k_ok = sem("k_ok")
        v_full = sem("v_full")
        v_hi_ok = sem("v_hi_ok")
        v_ok = sem("v_ok")
        s_full = sem("s_full")
        s_mask = sem("s_mask")
        s_max = sem("s_max")
        s_neg = sem("s_neg")
        s_exp = sem("s_exp")
        inv_ok = sem("inv_ok")
        p_ok = sem("p_ok")
        pt_full = sem("pt_full")
        pt_hi_ok = sem("pt_hi_ok")
        pt_ok = sem("pt_ok")
        o_full = sem("o_full")
        o_hi_ok = sem("o_hi_ok")
        o_ok = sem("o_ok")
        wo_full = sem("wo_full")
        wo_add = sem("wo_add")
        ch_ld = [sem("ch_ld0"), sem("ch_ld1")]
        ch_ok = sem("ch_ok")
        ch_st = [sem("ch_st0"), sem("ch_st1")]
        c3_ld = sem("stage3_constants")
        bo_ld = sem("bo_ld")
        mods_ld = [sem(f"mods_ld{b}") for b in range(B)]
        we_ld = [sem(f"shared_ld{k}") for k in range(3)]
        xr_ld = sem("xr_ld")
        x1_scaled = sem("x1_scaled")
        x1_ok = sem("x1_ok")
        c_var = sem("c_var")
        c_seed = sem("c_seed")
        c_xn = sem("c_xn")
        c_chain = sem("c_chain")
        c_stat = sem("c_stat")
        g_hi_ok = sem("g_hi_ok")
        h2_ok = sem("h2_ok")
        h2_st = sem("h2_st")
        g_ok = sem("g_ok")
        ones_ok = sem("ones_ok")
        w_ld = [sem("w_ld_even"), sem("w_ld_odd")]
        w_ready = sem("w_ready")
        xin_ld = [sem("xin_ld0"), sem("xin_ld1")]
        xt_full = sem("xt_full")
        xt_hi_ok = sem("xt_hi_ok")
        xt_ok = sem("xt_ok")
        gt_full = sem("gate_full")
        up_full = sem("up_full")
        silu_ok = sem("silu_ok")
        mid_ok = sem("mid_ok")
        ht_full = sem("ht_full")
        ht_hi_ok = sem("ht_hi_ok")
        ht_ok = sem("ht_ok")
        y_full = sem("y_full")
        y_gb = sem("y_gb")
        y_add = sem("y_add")
        y_ev = sem("y_ev")
        y_st = [sem("y_st0"), sem("y_st1")]
        lg_full = sem("lg_full")
        lg_ok = sem("lg_ok")
        rt_sub = sem("rt_sub")
        rt_exp = sem("rt_exp")
        rt_hot = sem("rt_hot")
        rt_cnt = sem("rt_cnt")
        pos_ok = sem("pos_ok")
        tab_ok = sem("tab_ok")
        sc_ld = [sem("sc_ld0"), sem("sc_ld1")]
        sc_st = [sem("sc_st0"), sem("sc_st1")]
        g_ld = [sem(f"g_ld{t}") for t in range(NT)]
        f_w1 = sem("f_w1")
        f_w2 = sem("f_w2")
        f_gb = sem("f_gb")
        f_ok = sem("f_ok")
        out_st = sem("out_st")

        block = ctx.enter_context(nc.Block())

        def wait_apart(eng, *waits):
            waits = [(s, v if isinstance(v, int) else eng.to_reg(v)) for s, v in waits]
            eng.wait_ge(c_ld, 16)
            for s, v in waits:
                eng.wait_ge(s, v)

        def walk_steps(eng, step):
            step(0, 0, True, False)
            with eng.Fori(0, HP - 1) as p:
                for b in range(1, B):
                    step(p, b, False, False)
                step(p + 1, 0, False, False)
            for b in range(1, B):
                step(HP - 1, b, False, b == B - 1)

        x_t = x.rearrange("(t p) d -> p t d", p=P)
        wq_v = wq.rearrange("(c p) n -> p c n", p=P)
        wk_v = wk.rearrange("(c p) n -> p c n", p=P)
        wv_v = wv.rearrange("(c p) n -> p c n", p=P)
        wo_v = wo.rearrange("(h p) n -> p h n", p=P)
        wmod_v = wmod.rearrange("(c p) n -> p c n", p=P)
        out_t = out.rearrange("(t p) d -> p t d", p=P)
        rows_t = rows_d.rearrange("(t p) d -> p t d", p=P)
        y_t = y_d.rearrange("(t p) d -> p t d", p=P)
        q_v = q_d.rearrange("b j p t -> p b j t")

        loads = [("mod", 0), ("mod", 1)] + [("wq", g) for g in range(4)] + [("mod", m) for m in range(2, 6)]
        load_at = {what: i for i, what in enumerate(loads)}

        def stage1_over(eng):
            eng.wait_ge(q_full, B * H)
            eng.wait_ge(hlo_ok, NT)
            for s in q_st:
                eng.wait_ge(s, 16 * B * H // 4)
            for s in mod_st:
                eng.wait_ge(s, 3 * 16)

        @block.sync
        def _(sp):
            sp.dma_start(c_in[:, :, :], c_t.rearrange("(c p) b -> p c b", p=P)).then_inc(c_ld, 16)
            sp.dma_start(x_in, x_t[:, 0:TT, :]).then_inc(x_ld, 16)
            for i, (kind, m) in enumerate(loads[:-1]):
                if i == 2:
                    sp.dma_start(ident[:, :], ident_in).then_inc(const_ld, 16)
                    sp.dma_start(causal[:, :], causal_in).then_inc(const_ld, 16)
                    sp.dma_start(bq_c[:, :], bq).then_inc(const_ld, 16)
                    sp.dma_start(bk_c[:, :], bk).then_inc(const_ld, 16)
                    sp.dma_start(bv_c[:, :], bv).then_inc(const_ld, 16)
                if i >= 3:
                    was, k = loads[i - 3]
                    if was == "mod":
                        sp.wait_ge(mod_full, k + 1)
                    else:
                        sp.wait_ge(wq_ok, k + 1)
                src = (wmod_v if kind == "mod" else wq_v)[:, :, m * D:(m + 1) * D]
                sp.dma_start(stage[i % 3], src).then_inc(stage_ld[i % 3], 16)
                if i == 5:
                    for r in range(2):
                        sp.wait_ge(mod_ev, r + 1)
                        sp.dma_start(mod_d[:, r * D:(r + 1) * D], mod_row[:, r, :]).then_inc(mod_st[r], 16)
            sp.dma_start(bo_b[:, :], bo.to_broadcast([P, D])).then_inc(bo_ld, 16)
            sp.dma_start(wk_raw[:, :, :], wk_v[:, :, 0:2 * P]).then_inc(wk_ld, 16)
            sp.dma_start(wv_raw[:, :, :], wv_v[:, :, 0:2 * P]).then_inc(wv_ld, 16)
            sp.dma_start(wo_raw[:, :, :], wo_v[:, 0:2, :]).then_inc(wo_ld, 16)

            def q_rows(b, more):
                if more:
                    sp.wait_ge(tx_full, b * TT + TT)
                    sp.dma_start(x_in, x_t[:, bass.ds((b + 1) * TT, TT), :]).then_inc(x_ld, 16)
                for j in range(H):
                    sp.wait_ge(q_ev, b * H + (j + 1))
                    sp.dma_start(q_v[:, bass.ds(b, 1), j, :], q_out[:, j % 4, :].unsqueeze(1))\
                      .then_inc(q_st[j % 4], 16)
                    if not more and j == 3:
                        sp.wait_ge(mod_full, 3)
                        i = len(loads) - 1
                        sp.dma_start(stage[i % 3], wmod_v[:, :, 5 * D:6 * D]).then_inc(stage_ld[i % 3], 16)
                    if not more and j in MOD_STORES:
                        store_mod(MOD_STORES[j])

            def store_mod(m):
                sp.wait_ge(mod_ev, m + 1)
                sp.dma_start(mod_d[:, m * D:(m + 1) * D], mod_row[:, m % 2, :]).then_inc(mod_st[m % 2], 16)

            with sp.Fori(0, B - 1) as b:
                q_rows(b, True)
            q_rows(B - 1, False)

            stage1_over(sp)

            def load_q(p, b):
                sp.dma_start(q_raw[:, :, :], q_v[:, b, :, bass.ds(p * 64, 64)]).then_inc(q_ld, 16)

            load_q(0, 0)
            for s in range(2):
                sp.dma_start(ch_raw[:, s, :], wexp[:, s * CH:(s + 1) * CH]).then_inc(ch_ld[s], 16)

            slots = rows_d[N:, :].rearrange("(a p) d -> p a d", p=P)
            sp.wait_ge(zero_ok, 1)

            def load_mods(b):
                sp.wait_ge(v_full, (NIT - B + b) * 2 + 2)
                sp.dma_start(mods[:, b, :, :].rearrange("p k d -> p (k d)"),
                             mod_d[b:b + 1, 2 * D:6 * D].to_broadcast([P, 4 * D])).then_inc(mods_ld[b], 16)

            def load_xr(b):
                if b:
                    sp.wait_ge(x1_ok, b)
                sp.dma_start(xr[:, :, :], x_t[:, b * TT:(b + 1) * TT, :]).then_inc(xr_ld, 16)

            def store_h2(b):
                sp.wait_ge(h2_ok, b * TT + TT)
                sp.dma_start(rows_t[:, b * TT:(b + 1) * TT, :], h2[:, :, :]).then_inc(h2_st, 16)

            def load_shared(k, at, end):
                sp.dma_start(w_hi[:, at:end].bitcast(F32), wx_hi_d[:, E * WE + at:E * WE + end]).then_inc(we_ld[k], 16)
                sp.dma_start(w_lo[:, at:end].bitcast(F32), wx_lo_d[:, E * WE + at:E * WE + end]).then_inc(we_ld[k], 16)

            def step(p, b, first, last):
                n = p * B + b
                tail = b - 1 if isinstance(p, int) and p == HP - 1 else -1
                if tail == 2:
                    sp.wait_ge(wk_ok, HP)
                    sp.dma_start(g_raw[:, :, :], gate_t.rearrange("(c p) e -> p c e", p=P)).then_inc(c3_ld, 16)
                    sp.dma_start(tri[:, :], tri_in).then_inc(c3_ld, 16)
                    sp.dma_start(coef[:, :], coef_in).then_inc(c3_ld, 16)
                if not last:
                    sp.wait_ge(q_ok, n * 2 + 2)
                    load_q(p if b < B - 1 else p + 1, (b + 1) % B)
                if b == 2:
                    sp.dma_start(slots[:, bass.ds(p * (NSLOT // HP), NSLOT // HP), :],
                                 zero[:, :].unsqueeze(1).to_broadcast([P, NSLOT // HP, D])).then_inc(zero_st, 16)
                if b == 1 and not (isinstance(p, int) and p == HP - 1):
                    nxt = (p + 1) * 2 * P
                    sp.wait_ge(wk_ok, p + 1)
                    sp.dma_start(wk_raw[:, :, :], wk_v[:, :, bass.ds(nxt, 2 * P)]).then_inc(wk_ld, 16)
                    sp.wait_ge(wv_ok, p + 1)
                    sp.dma_start(wv_raw[:, :, :], wv_v[:, :, bass.ds(nxt, 2 * P)]).then_inc(wv_ld, 16)
                    sp.wait_ge(wo_ok, p + 1)
                    sp.dma_start(wo_raw[:, :, :], wo_v[:, bass.ds((p + 1) * 2, 2), :]).then_inc(wo_ld, 16)
                for q in range(4):
                    c, s = n * 4 + q, q % 2
                    sp.wait_ge(ch_ok, c + 1)
                    sp.dma_start(wx_hi_d[:, bass.ds(c * CH, CH)], ch_hi[:, s, :].bitcast(F32)).then_inc(ch_st[s], 16)
                    sp.dma_start(wx_lo_d[:, bass.ds(c * CH, CH)], ch_lo[:, s, :].bitcast(F32)).then_inc(ch_st[s], 16)
                    if not (last and q >= 2):
                        sp.dma_start(ch_raw[:, s, :], wexp[:, bass.ds((c + 2) * CH, CH)]).then_inc(ch_ld[s], 16)
                    if tail >= 0 and q == 1:
                        load_mods(tail)
                        load_xr(tail)
                    if last and q == 2:
                        sp.wait_ge(v_full, NIT * 2)
                        for k in range(2):
                            sp.wait_ge(ch_st[k], 16 * (NCH - 4))
                        load_shared(0, WG, WU)
                if tail == 1:
                    store_h2(0)

            for s in range(2):
                sp.wait_ge(mod_st[s], 3 * 16)
            walk_steps(sp, step)

            sp.wait_ge(wo_add, NIT * TT)

            def load_w(e, s):
                sp.dma_start(w_hi[:, s * WE:(s + 1) * WE].bitcast(F32), wx_hi_d[:, e * WE:(e + 1) * WE]).then_inc(w_ld[s], 16)
                sp.dma_start(w_lo[:, s * WE:(s + 1) * WE].bitcast(F32), wx_lo_d[:, e * WE:(e + 1) * WE]).then_inc(w_ld[s], 16)

            load_shared(1, WU, WD)
            load_shared(2, WD, WE)
            store_h2(1)
            load_xr(3)
            load_mods(3)
            store_h2(2)
            store_h2(3)
            load_w(E + 1, 1)
            sp.wait_ge(y_full, NT)
            load_w(0, 0)
            for b, dst, k in ((0, xr, 0), (1, h2, 1), (2, xr, 0)):
                if b == 0:
                    sp.wait_ge(x1_ok, B)
                else:
                    sp.wait_ge(sc_st[k], 2 * TT * 16)
                sp.dma_start(dst[:, :, :], rows_t[:, b * TT:(b + 1) * TT, :]).then_inc(sc_ld[k], 16)

            sp.wait_ge(tab_ok, 1)

            def routed(j, first, last):
                for k in range(2):
                    r = j * 2 + k
                    n = r + 2 * NT
                    nxt = sp.value_load(tab[0:1, 3, bass.ds(r, 1)], min_val=1, max_val=E)
                    load = [sp.value_load(tab[0:1, 4 + s, bass.ds(r, 1)], min_val=0, max_val=1) for s in range(2)]
                    wait_apart(sp, (y_full, n))
                    for s in range(2):
                        with sp.If(load[s]):
                            sp.dma_start(w_hi[:, s * WE:(s + 1) * WE].bitcast(F32), wx_hi_d[:, bass.ds(nxt * WE, WE)])\
                              .then_inc(w_ld[s], 16)
                            sp.dma_start(w_lo[:, s * WE:(s + 1) * WE].bitcast(F32), wx_lo_d[:, bass.ds(nxt * WE, WE)])\
                              .then_inc(w_ld[s], 16)
                    if not (first and k == 0):
                        store_y(r - 1, (k + 1) % 2)

            def store_y(r, s):
                sp.wait_ge(y_ev, r + 1)
                sp.dma_start(y_t[:, bass.ds(r, 1), :], y_sb[:, s, :].unsqueeze(1)).then_inc(y_st[s], 16)

            routed(0, True, False)
            with sp.Fori(1, NSLOT // 2 - 1) as j:
                routed(j, False, False)
            routed(NSLOT // 2 - 1, False, True)
            store_y(NSLOT - 1, 1)

            for t in range(NT):
                sp.wait_ge(f_ok, t + 1)
                sp.dma_start(out_t[:, t, :], rows_1[:, t, :]).then_inc(out_st, 16)
            sp.wait_ge(out_st, 16 * NT)
            for s in range(2):
                sp.wait_ge(y_st[s], 16 * NSLOT // 2)
            sp.wait_ge(zero_st, 16 * HP)

        @block.gpsimd
        def _(pool):
            pool.memset(zero[:, :], 0.0).then_inc(zero_ok, 1)
            pool.memset(mh[:, :], -0.5).then_inc(mh_ok, 1)
            pool.wait_ge(mh_ok, 1)

            def seed(b):
                pool.wait_ge(ln_var, b + 1)
                pool.tensor_tensor(rs0[:, :], ve[:, :], mh[:, :], ALU.pow).then_inc(ln_seed, 1)

            seed(0)
            with pool.Fori(0, B - 1) as b:
                seed(b + 1)

            q_nat_hi = q_hi[:, :, :].rearrange("p h (r j) -> p h r j", j=H)
            q_nat_lo = q_lo[:, :, :].rearrange("p h (r j) -> p h r j", j=H)
            q_in = q_raw[:, :, :].rearrange("p j (h r) -> p h r j", h=2)

            def run(what, base):
                for k, (raw, hi, lo, waits, done) in enumerate(what):
                    wait_apart(pool, *waits)
                    pool.tensor_copy(hi, raw).then_inc(split_hi, 1)
                    pool.wait_ge(split_hi, base + (k + 1))
                    pool.tensor_tensor(lo, raw, hi.bitcast(F32), ALU.subtract).then_inc(done, 1)

            SPB = [7, 6, 7, 7]
            SPP = sum(SPB)

            def base_of(p, b):
                done = 3 + sum(SPB[:b])
                if isinstance(p, int) and p == HP - 1 and b == B - 1:
                    done -= 1
                return p * SPP + done

            run([(wk_raw[:, :, :], wk_hi[:, :, :], wk_lo[:, :, :], [(wk_ld, 16)], wk_ok)], 0)
            stage1_over(pool)
            run([
                (q_in[:, 0], q_nat_hi[:, 0], q_nat_lo[:, 0], [(q_ld, 16)], q_ok),
                (q_in[:, 1], q_nat_hi[:, 1], q_nat_lo[:, 1], [], q_ok)], 1)
            def c_pre(b):
                a = acc[:, b * TT:(b + 1) * TT, :]
                pool.wait_ge(wo_add, (NIT - B + b) * TT + TT)
                pool.wait_ge(mods_ld[b], 16)
                pool.tensor_tensor(a, a, mods[:, b, 0:1, :].to_broadcast([P, TT, D]), ALU.mult).then_inc(x1_scaled, 1)
                pool.wait_ge(x1_scaled, b + 1)
                pool.wait_ge(xr_ld, b * 16 + 16)
                pool.tensor_tensor(a, a, xr[:, :, :], ALU.add).then_inc(x1_ok, 1)

            def c_seed_of(b):
                pool.wait_ge(c_var, b + 1)
                pool.tensor_tensor(rs0[:, :], ve[:, :], mh[:, :], ALU.pow).then_inc(c_seed, 1)

            def step(p, b, first, last):
                n = p * B + b
                base = base_of(p, b)
                k = 0
                at_end = isinstance(p, int) and p == HP - 1
                tail = b - 1 if at_end else -1
                for h in range(2):
                    if not last:
                        run([(q_in[:, h], q_nat_hi[:, h], q_nat_lo[:, h],
                                    [(q_ld, n * 16 + 32), (s_full, n * 6 + (3 * h + 3))], q_ok)], base + k)
                        k += 1
                if b == 0:
                    waits = [(wo_ld, p * 16 + 16)]
                    if not first:
                        waits.append((wo_full, n * TT))
                    run([(wo_raw[:, :, :], wo_hi[:, :, :], wo_lo[:, :, :], waits, wo_ok)], base + k)
                    k += 1
                for q in range(4):
                    c, s = n * 4 + q, q % 2
                    waits = [(ch_ld[s], n * 32 + (q // 2 + 1) * 16)]
                    if not (first and q < 2):
                        waits.append((ch_st[s], n * 64 + (q // 2) * 32))
                    run([(ch_raw[:, s, :], ch_hi[:, s, :], ch_lo[:, s, :], waits, ch_ok)], base + k)
                    k += 1
                    if tail == 1 and q == 0:
                        c_seed_of(0)
                if tail >= 0:
                    c_pre(tail)
                if last:
                    c_seed_of(1)
                if b == 2 and not at_end:
                    run([(wk_raw[:, :, :], wk_hi[:, :, :], wk_lo[:, :, :],
                                [(wk_ld, p * 16 + 32), (k_full, n * 2 + 4)], wk_ok)], base + k)
                    k += 1
                if b == 3 and not at_end:
                    run([(wv_raw[:, :, :], wv_hi[:, :, :], wv_lo[:, :, :],
                                [(wv_ld, p * 16 + 32), (v_full, n * 2 + 2)], wv_ok)], base + k)
                    k += 1
                assert at_end or k == SPB[b]

            walk_steps(pool, step)

            pool.wait_ge(wo_add, NIT * TT)
            pool.memset(ones[:, :], 1.0).then_inc(ones_ok, 1)

            def add_y(t, n, s):
                wait_apart(pool, (y_gb, n + 1))
                pool.tensor_tensor(acc[:, bass.ds(t, 1), :], acc[:, bass.ds(t, 1), :], y_sb[:, s, :].unsqueeze(1),
                                   ALU.add).then_inc(y_add, 1)

            def quad0(b, hidden, first):
                for i in range(TT):
                    n = b * TT + i
                    if not (first and i == 0):
                        add_y(n - 1, n - 1, (i + 1) % 2)
                    if hidden and i == 1:
                        c_seed_of(b + 2)
                    if first and i == 1:
                        c_pre(B - 1)

            quad0(0, True, True)
            quad0(1, True, False)
            with pool.Fori(2, B) as b:
                quad0(b, False, False)

            def scatter(b, i):
                src = xr if b % 2 == 0 else h2
                if i == 0 and b < B - 1:
                    pool.wait_ge(sc_ld[b % 2], 16 * (b // 2 + 1))
                for c in range(2):
                    pool.indirect_dma_start(
                        out=rows_d,
                        out_offset=bass.IndirectOffsetOnAxis(ap=pos_r[:, c, b * TT + i:b * TT + i + 1], axis=0),
                        in_=src[:, i, :], in_offset=None,
                        bounds_check=N + NSLOT * P - 1, oob_is_err=True).then_inc(sc_st[b % 2], 16)

            for n in range(NT, SCATTER_AT):
                add_y((n - 1) % NT, n - 1, (n - 1) % 2)
            order = [(b, i) for b in (B - 1, 0, 1, 2) for i in range(TT)]
            pool.wait_ge(pos_ok, 2)
            pool.wait_ge(zero_st, 16 * HP)
            pool.wait_ge(h2_st, 16 * B)
            for n in range(SCATTER_AT, 2 * NT):
                add_y(n - 1 - NT, n - 1, (n - 1) % 2)
                for b, i in order[(n - SCATTER_AT) * 3:(n - SCATTER_AT) * 3 + 3]:
                    scatter(b, i)

            pool.wait_ge(tab_ok, 1)

            def weights_ready(r):
                loads = [pool.value_load(tab[0:1, 1 + s, bass.ds(r, 1)], min_val=32, max_val=32 * E)
                         for s in range(2)]
                own = [] if isinstance(r, int) else [(w_ready, r)]
                wait_apart(pool, (w_ld[0], loads[0]), (w_ld[1], loads[1]), *own)
                pool.memset(sign[:, :], 1.0).then_inc(w_ready, 1)

            weights_ready(0)
            add_y(NT - 1, 2 * NT - 1, 1)
            with pool.Fori(1, NSLOT) as r:
                weights_ready(r)

            pool.wait_ge(y_full, NJ)
            for s in range(2):
                pool.wait_ge(y_st[s], 16 * NSLOT // 2)
            for t in range(NT):
                for c, rows in enumerate((rows_0, rows_1)):
                    pool.indirect_dma_start(
                        out=rows[:, t, :], out_offset=None, in_=y_d,
                        in_offset=bass.IndirectOffsetOnAxis(ap=pos_i[:, c, t:t + 1], axis=0),
                        bounds_check=NSLOT * P - 1, oob_is_err=True).then_inc(g_ld[t], 16)

        @block.scalar
        def _(act):
            act.wait_ge(c_ld, 16)
            act.activation(c_silu[:, :, :], c_in[:, :, :], ACT.Silu).then_inc(silu_c, 1)
            for g in range(4):
                i = load_at["wq", g]
                act.wait_ge(stage_ld[i % 3], 16 * (i // 3 + 1))
                act.activation(wq_hi[:, :, g * D:(g + 1) * D], stage[i % 3], ACT.Copy).then_inc(wq_hi_ok, 1)
                if g == 0:
                    for i in range(TT):
                        act.wait_ge(hf_ok, i + 1)
                        act.activation(h_hi[:, 0:DC, i * P:(i + 1) * P], h_full[:, i % 2], ACT.Copy)\
                           .then_inc(hhi_ok, 1)

            act.wait_ge(const_ld, 5 * 16)

            def q_rows(b, more, first):
                for j in range(H):
                    act.wait_ge(q_full, b * H + (j + 1))
                    if not (first and j < 4):
                        act.wait_ge(q_st[j % 4], b * (16 * H // 4) + 16 * (j // 4))
                    act.activation(q_out[:, j % 4, :], bank[j % 4][:, :], ACT.Identity,
                                   bias=bq_c[:, j:j + 1]).then_inc(q_ev, 1)
                    if more and j >= 11 and j < 15:
                        i = j - 11
                        wait_apart(act, (hf_ok, b * TT + (TT + i + 1)))
                        act.activation(h_hi[:, bass.ds((b + 1) * DC, DC), i * P:(i + 1) * P], h_full[:, i % 2],
                                       ACT.Copy).then_inc(hhi_ok, 1)

            q_rows(0, True, True)
            with act.Fori(1, B - 1) as b:
                q_rows(b, True, False)
            q_rows(B - 1, False, False)

            stage1_over(act)

            def k_part(p, n, h):
                wait_apart(act, (k_full, n * 2 + (h + 1)))
                act.activation(k_hi[:, h, :], bank[h][:, :], ACT.Identity,
                               bias=bk_c[:, bass.ds(p * 2 + h, 1)]).then_inc(k_hi_ok, 1)

            k_part(0, 0, 0)
            k_part(0, 0, 1)
            def bias_rows(b):
                act.activation(acc[:, b * TT:(b + 1) * TT, :], bo_b[:, :].unsqueeze(1).to_broadcast([P, TT, D]),
                               ACT.Copy).then_inc(acc_ok, 1)

            def step(p, b, first, last):
                n = p * B + b

                def exps(i):
                    h, rows = i // 3, S_PARTS[i % 3]
                    if i % 3 == 0 and not first:
                        act.wait_ge(pt_full, n * 6 + (3 * h - 3))
                    act.wait_ge(s_neg, n * 6 + (i + 1))
                    for r in rows:
                        at = ROW_AT[r] - ROW_AT[rows[0]]
                        ins = act.activation(prob[:, h, ROW_AT[r]:ROW_AT[r] + (r + 1) * P],
                                             bank[2 + i % 2][:, at:at + (r + 1) * P], ACT.Exp,
                                             bias=neg_max[:, h, r:r + 1], scale=SCALE,
                                             accum_out=row_sum[:, h, r:r + 1])
                    ins.then_inc(s_exp, 1)

                def v_part(g):
                    if g == 0 and not first:
                        act.wait_ge(o_full, n * 2)
                    act.wait_ge(v_full, n * 2 + (g + 1))
                    act.activation(v_hi[:, 2 * g:2 * g + 2, :], bank[g][:, :].rearrange("p (i n) -> p i n", i=2),
                                   ACT.Copy).then_inc(v_hi_ok, 1)

                def pt_part(h, g):
                    if g == 0 and not (first and h == 0):
                        act.wait_ge(o_full, n * 2 + h)
                    act.wait_ge(pt_full, n * 6 + (3 * h + g + 1))
                    act.activation(pt_hi[:, PT_AT[g]:PT_AT[g] + PT_LEN[g]], bank[4 + g % 2][:, 0:PT_LEN[g]],
                                   ACT.Copy).then_inc(pt_hi_ok, 1)

                def o_part(h):
                    free = [(wo_full, n * TT)] if h == 0 and not first else []
                    wait_apart(act, *free, (o_full, n * 2 + (h + 1)))
                    act.activation(o_hi[:, h, :], bank[6 + h][:, :], ACT.Identity,
                                   bias=bv_c[:, bass.ds(p * 2 + h, 1)]).then_inc(o_hi_ok, 1)

                pn = p if b < B - 1 else p + 1
                if first:
                    act.wait_ge(bo_ld, 16)
                    bias_rows(0)
                    v_part(0)
                    bias_rows(1)
                    v_part(1)
                for i in range(5):
                    exps(i)
                if not first:
                    v_part(0)
                exps(5)
                if not first:
                    v_part(1)
                if first:
                    bias_rows(2)
                pt_part(0, 0)
                pt_part(0, 1)
                if not last:
                    k_part(pn, n + 1, 0)
                if first:
                    bias_rows(3)
                pt_part(0, 2)
                o_part(0)
                for g in range(3):
                    pt_part(1, g)
                o_part(1)
                if not last:
                    k_part(pn, n + 1, 1)

            walk_steps(act, step)


            def xt_part(n, s):
                act.wait_ge(xt_full, n + 1)
                act.activation(xt_hi[:, s], bank[2][:, :].rearrange("p (c n) -> p c n", c=DC), ACT.Copy)\
                   .then_inc(xt_hi_ok, 1)

            def load_xin(m, s, tile):
                act.dma_start(xin[:, s, :].unsqueeze(1), rows_t[:, bass.ds(tile, 1), :]).then_inc(xin_ld[s], 16)

            def load_hidden(m, s, batch=None):
                if batch is not None:
                    wait_apart(act, (h2_st, batch * 16 + 16))
                load_xin(m, s, m)

            def job(n, s, prev, nxt, load="again", batch=None):
                act.wait_ge(gt_full, n + 1)
                act.activation(gate_s[:, s, :], bank[0][:, 0:F], ACT.Silu).then_inc(silu_ok, 1)
                if prev:
                    ht_part(n - 1)
                if nxt:
                    if not (isinstance(n, int) and n == 0):
                        act.wait_ge(up_full, n)
                    xt_part(n + 1, 1 - s)
                if load == "first":
                    load_hidden(n + 3, 1 - s, batch)
                elif load == "again":
                    load_xin(n + 3, 1 - s, n + (3 - NT))
                if prev == "routed":
                    y_part(n - 1, 1 - s)

            def ht_part(m):
                act.wait_ge(ht_full, m + 1)
                for f in range(FC):
                    ins = act.activation(ht_hi[0:FK[f], f, :], bank[3][0:FK[f], f * P:(f + 1) * P], ACT.Copy)
                ins.then_inc(ht_hi_ok, 1)

            def y_part(m, s):
                act.wait_ge(y_full, m + 1)
                if not (isinstance(m, int) and m < 2 * NT + 2):
                    act.wait_ge(y_st[s], (m - (2 * NT + s)) * 8)
                act.activation(y_sb[:, s, :], bank[4 + s][:, :], ACT.Copy).then_inc(y_ev, 1)

            load_hidden(0, 0, 0)
            load_hidden(1, 1)
            act.wait_ge(wo_add, NIT * TT)
            xt_part(0, 0)
            load_hidden(2, 0)

            def quad0(b, first):
                for i in range(TT):
                    job(b * TT + i, i % 2, None if first and i == 0 else "shared", True,
                        "first", b + 1 if i == 1 else None)

            quad0(0, True)
            with act.Fori(1, B - 1) as b:
                quad0(b, False)
            job(NT - 4, 0, "shared", True, "first")
            for n in range(NT - 3, NT + 1):
                job(n, n % 2, "shared", True)
            act.wait_ge(rt_sub, 1)
            act.activation(sc[:, :, :], ra[:, :, :], ACT.Exp).then_inc(rt_exp, 1)
            job(NT + 1, 1, "shared", True)
            with act.Fori(NT // 2 + 1, NT - 2) as j:
                for k in range(2):
                    job(j * 2 + k, k, "shared", True)
            job(2 * NT - 4, 0, "shared", True)
            for s in range(2):
                act.wait_ge(sc_st[s], 16 * NT)
            for n in range(2 * NT - 3, 2 * NT):
                job(n, n % 2, "shared", True)
            job(2 * NT, 0, "shared", True)
            act.wait_ge(y_add, 2 * NT)
            job(2 * NT + 1, 1, "routed", True)
            with act.Fori(NT + 1, NJ // 2 - 2) as j:
                for k in range(2):
                    job(j * 2 + k, k, "routed", True)
            job(NJ - 4, 0, "routed", True)
            job(NJ - 3, 1, "routed", True, None)
            job(NJ - 2, 0, "routed", True, None)
            job(NJ - 1, 1, "routed", False, None)
            ht_part(NJ - 1)
            y_part(NJ - 1, 1)

            for t in range(NT):
                act.wait_ge(g_ld[t], 32)
                act.activation(rows_0[:, t, :], rows_0[:, t, :], ACT.Copy, scale=top_w[:, 0, t:t + 1])\
                   .then_inc(f_w1, 1)

        @block.tensor
        def _(pe):
            def mm3(dst, terms):
                k, last = 0, 3 * len(terms) - 1
                for sh, sl, mh_, ml in terms:
                    for a, m in ((sh, mh_), (sh, ml), (sl, mh_)):
                        ins = pe.matmul(dst, a, m, start=(k == 0), stop=(k == last))
                        k += 1
                return ins

            pe.wait_ge(silu_c, 1)

            def mod_piece(m):
                i = load_at["mod", m]
                pe.wait_ge(stage_ld[i % 3], 16 * (i // 3 + 1))
                if m >= 1:
                    pe.wait_ge(mod_ev, m)
                for c in range(DC):
                    ins = pe.matmul(bank[6][0:B, :], c_silu[:, c, :], stage[i % 3][:, c, :],
                                    start=(c == 0), stop=(c == DC - 1))
                ins.then_inc(mod_full, 1)

            def transposes(b, i):
                pe.wait_ge(xn_ok, b * TT + (i + 1))
                if not (isinstance(b, int) and b == 0 and i < 2):
                    pe.wait_ge(hf_ok, b * TT + (i - 1))
                for c in range(DC):
                    ins = pe.transpose(bank[4 + i % 2][:, c * P:(c + 1) * P], x_in[:, i, c * P:(c + 1) * P],
                                       ident[:, :])
                ins.then_inc(tx_full, 1)

            mod_piece(0)
            pe.wait_ge(const_ld, 5 * 16)
            transposes(0, 0)
            transposes(0, 1)
            mod_piece(1)
            for m in range(2):
                pe.wait_ge(mod_ev, m + 1)
                for c in range(DC):
                    ins = pe.transpose(bank[7][:, (m * DC + c) * B:(m * DC + c + 1) * B],
                                       mod_row[:, m, c * P:(c + 1) * P], ident[0:B, 0:B])
            ins.then_inc(modt_full, 1)

            for i in range(2, TT):
                transposes(0, i)

            def q_rows(b, more, first):
                def hidden(h, c):
                    return h[:, bass.ds(b * DC + c, 1), :].rearrange("p a t -> p (a t)")

                pe.wait_ge(hlo_ok, b * TT + TT)
                for j in range(H):
                    if first and j % 4 == 0:
                        pe.wait_ge(wq_ok, j // 4 + 1)
                    if not (first and j < 4):
                        pe.wait_ge(q_ev, b * H + (j - 3))
                    mm3(bank[j % 4][:, :],
                        [(wq_hi[:, c, j * P:(j + 1) * P], wq_lo[:, c, j * P:(j + 1) * P],
                          hidden(h_hi, c), hidden(h_lo, c)) for c in range(DC)]).then_inc(q_full, 1)
                    if more and j >= 10 and j < 14:
                        transposes(b + 1, j - 10)
                    if not more and j in MOD_PIECES:
                        mod_piece(MOD_PIECES[j])

            q_rows(0, True, True)
            with pe.Fori(1, B - 1) as b:
                q_rows(b, True, False)
            q_rows(B - 1, False, False)

            pe.wait_ge(q_ev, B * H)
            pe.wait_ge(mod_ev, 6)
            pe.wait_ge(hlo_ok, NT)

            def keys(n, pair, b, h, chunks):
                if chunks[0] == 0:
                    pe.wait_ge(wk_ok, pair + 1)
                    if not (isinstance(n, int) and n == 0):
                        pe.wait_ge(v_ok, n * 2 + (h - 1))
                for c in chunks:
                    for k, (a, m) in enumerate(((wk_hi, h_hi), (wk_hi, h_lo), (wk_lo, h_hi))):
                        ins = pe.matmul(bank[h][:, :], a[:, c, h * P:(h + 1) * P], m[:, b * DC + c, :],
                                        start=(c == 0 and k == 0), stop=(c == DC - 1 and k == 2))
                if chunks[-1] == DC - 1:
                    ins.then_inc(k_full, 1)

            for h in range(2):
                keys(0, 0, 0, h, range(DC))

            def out_tile(m, pair, i, after):
                if i == 0:
                    pe.wait_ge(wo_ok, pair + 1)
                    pe.wait_ge(o_ok, m * 2 + 2)
                if after:
                    pe.wait_ge(*after)
                mm3(bank[i % 2][:, :],
                    [(o_hi[:, h, i * P:(i + 1) * P], o_lo[:, h, i * P:(i + 1) * P],
                      wo_hi[:, h, :], wo_lo[:, h, :]) for h in range(2)]).then_inc(wo_full, 1)

            def step(p, b, first, last):
                n = p * B + b

                def scores(i):
                    h, rows = i // 3, S_PARTS[i % 3]
                    if i % 3 == 0:
                        pe.wait_ge(k_ok, n * 2 + (h + 1))
                        pe.wait_ge(q_ok, n * 2 + (h + 1))
                    if not (first and i < 2):
                        pe.wait_ge(s_exp, n * 6 + (i - 1))
                    for r in rows:
                        w = (r + 1) * P
                        at = ROW_AT[r] - ROW_AT[rows[0]]
                        dst = bank[2 + i % 2][:, at:at + w]
                        for k, (a, m) in enumerate(((q_hi, k_hi), (q_hi, k_lo), (q_lo, k_hi))):
                            ins = pe.matmul(dst, a[:, h, r * P:w], m[:, h, 0:w], start=(k == 0), stop=(k == 2))
                    ins.then_inc(s_full, 1)

                def values(t):
                    g, i = t // 2, t % 2
                    if i == 0:
                        pe.wait_ge(wv_ok, p + 1)
                        if not first:
                            pe.wait_ge(wo_add, n * TT + (g - 1))
                        else:
                            pe.wait_ge(k_ok, g + 1)
                    rows = slice(t * P, (t + 1) * P)
                    ins = mm3(bank[g][:, i * 2 * P:(i + 1) * 2 * P],
                              [(h_hi[:, b * DC + c, rows], h_lo[:, b * DC + c, rows], wv_hi[:, c, :], wv_lo[:, c, :])
                               for c in range(DC)])
                    if i == 1:
                        ins.then_inc(v_full, 1)

                def turn(h, groups):
                    if groups[0] == 0:
                        pe.wait_ge(p_ok, n * 6 + (3 * h + 3))
                    for g in groups:
                        blocks = PT_GROUPS[g]
                        if not (first and h == 0 and g < 2):
                            pe.wait_ge(pt_ok, n * 6 + (3 * h + (1 if g == 2 else 0)))
                        for k, at in blocks:
                            for r in range(k, TT):
                                ins = pe.transpose(
                                    bank[4 + g % 2][:, at + (r - k) * P:at + (r - k + 1) * P],
                                    prob[:, h, ROW_AT[r] + k * P:ROW_AT[r] + (k + 1) * P], ident[:, :])
                        ins.then_inc(pt_full, 1)

                def weigh(h):
                    if not first:
                        pe.wait_ge(o_ok, n * 2 + (h - 1))
                    for g, blocks in enumerate(PT_GROUPS):
                        pe.wait_ge(pt_ok, n * 6 + (3 * h + g + 1))
                        pe.wait_ge(v_ok, n * 2 + (1 if g == 0 else 2))
                        for k, at in blocks:
                            w = (TT - k) * P
                            cols = slice(PT_AT[g] + at, PT_AT[g] + at + w)
                            vals = slice(h * P, (h + 1) * P)
                            for q, (a, m) in enumerate(((v_hi, pt_hi), (v_hi, pt_lo), (v_lo, pt_hi))):
                                ins = pe.matmul(bank[6 + h][:, k * P:T], a[:, k, vals], m[:, cols],
                                                start=(k == 0 and q == 0), stop=(g == 2 and q == 2))
                    ins.then_inc(o_full, 1)

                def project(i):
                    if not first:
                        free = [(k_ok, n * 2 + 1), (k_ok, n * 2 + 2), (wo_add, n * TT - 3), (wo_add, n * TT - 2)][i]
                        out_tile(n - 1, p if b > 0 else p - 1, i, free)

                def next_keys(h, chunks):
                    if not last:
                        keys(n + 1, p if b < B - 1 else p + 1, (b + 1) % B, h, chunks)

                if first:
                    for t in range(TT):
                        values(t)
                scores(0)
                scores(1)
                project(0)
                project(1)
                scores(2)
                project(2)
                scores(3)
                project(3)
                if not first:
                    values(0)
                scores(4)
                if not first:
                    values(1)
                scores(5)
                if not first:
                    values(2)
                    values(3)
                turn(0, (0, 1))
                next_keys(0, range(DC))
                turn(0, (2,))
                next_keys(1, (0,))
                weigh(0)
                turn(1, (0, 1))
                next_keys(1, range(1, DC - 1))
                turn(1, (2,))
                weigh(1)
                next_keys(1, (DC - 1,))

            walk_steps(pe, step)
            out_tile(NIT - 1, HP - 1, 0, (v_ok, 2 * NIT - 1))
            out_tile(NIT - 1, HP - 1, 1, (v_ok, 2 * NIT))
            out_tile(NIT - 1, HP - 1, 2, (wo_add, NIT * TT - 3))
            out_tile(NIT - 1, HP - 1, 3, (wo_add, NIT * TT - 2))

            pe.wait_ge(wo_add, NIT * TT)
            pe.wait_ge(pt_ok, NIT * 6)
            pe.wait_ge(o_ok, NIT * 2)

            def turn_rows(n, s, count):
                pe.wait_ge(xin_ld[s], count)
                if not (isinstance(n, int) and n == 0):
                    pe.wait_ge(xt_ok, n)
                for c in range(DC):
                    ins = pe.transpose(bank[2][:, c * P:(c + 1) * P], xin[:, s, c * P:(c + 1) * P], ident[:, :])
                ins.then_inc(xt_full, 1)

            def half(n, s, wofs, which):
                if which == 0:
                    pe.wait_ge(xt_ok, n + 1)
                if not (isinstance(n, int) and n == 0):
                    pe.wait_ge((silu_ok, mid_ok)[which], n)
                at = (WG, WU)[which]
                mm3(bank[which][:, 0:F],
                    [(xt_hi[:, s, c, :], xt_lo[:, s, c, :], w_hi[:, wcol(wofs, at + c * F, F)],
                      w_lo[:, wcol(wofs, at + c * F, F)]) for c in range(DC)])\
                    .then_inc((gt_full, up_full)[which], 1)

            def wcol(wofs, at, width):
                if isinstance(wofs, int):
                    return slice(wofs + at, wofs + at + width)
                return bass.ds(wofs + at, width)

            def logits(n, s):
                if not (isinstance(n, int) and n == 0):
                    pe.wait_ge(lg_ok, n)
                mm3(bank[6][:, 0:E],
                    [(xt_hi[:, s, c, :], xt_lo[:, s, c, :], g_hi[:, c, :], g_lo[:, c, :])
                     for c in range(DC)]).then_inc(lg_full, 1)

            def turn_mid(m, s):
                pe.wait_ge(mid_ok, m + 1)
                if not (isinstance(m, int) and m == 0):
                    pe.wait_ge(ht_ok, m)
                for f in range(FC):
                    ins = pe.transpose(bank[3][0:FK[f], f * P:(f + 1) * P],
                                       h_mid[:, s, f * P:f * P + FK[f]], ident[:, :])
                ins.then_inc(ht_full, 1)

            def down(m, s, wofs, free):
                pe.wait_ge(ht_ok, m + 1)
                if free:
                    pe.wait_ge(*free)
                mm3(bank[4 + s][:, :],
                    [(ht_hi[0:FK[f], f, :], ht_lo[0:FK[f], f, :], w_hi[0:FK[f], wcol(wofs, WD + f * D, D)],
                      w_lo[0:FK[f], wcol(wofs, WD + f * D, D)]) for f in range(FC)]).then_inc(y_full, 1)

            def job(n, s, wofs, prev_ofs, route=False, prev=True, nxt=True, free=None, up_ld=None):
                half(n, s, wofs, 0)
                if up_ld:
                    pe.wait_ge(*up_ld)
                if prev:
                    turn_mid(n - 1, 1 - s)
                half(n, s, wofs, 1)
                if route:
                    logits(n, s)
                if nxt:
                    turn_rows(n + 1, 1 - s, xcount(n + 1, 1 - s))
                if prev:
                    down(n - 1, 1 - s, prev_ofs, free)

            def xcount(m, s):
                return (m - s) * 8 + 16

            pe.wait_ge(g_ok, 1)
            turn_rows(0, 0, 16)
            pe.wait_ge(we_ld[0], 32)
            job(0, 0, 0, 0, route=True, prev=False, up_ld=(we_ld[1], 32))
            pe.wait_ge(we_ld[2], 32)
            job(1, 1, 0, 0, route=True)
            job(2, 0, 0, 0, route=True)
            job(3, 1, 0, 0, route=True, free=(y_gb, 1))
            with pe.Fori(2, NT // 2) as j:
                for k in range(2):
                    job(j * 2 + k, k, 0, 0, route=True, free=(y_gb, j * 2 + (k - 2)))
            pe.wait_ge(w_ld[1], 32)
            job(NT, 0, WE, 0, free=(y_gb, NT - 2))
            job(NT + 1, 1, WE, WE, free=(y_gb, NT - 1))
            job(NT + 2, 0, WE, WE, free=(y_gb, NT))
            pe.wait_ge(rt_hot, 1)
            pe.wait_ge(ones_ok, 1)
            hot_cols = hot[:, :, :].rearrange("p t e -> p (t e)")
            pe.matmul(bank[7][:, 0:NT * E], tri[:, :], hot_cols, start=True, stop=True)
            pe.matmul(bank[7][:, NT * E:2 * NT * E], ones[:, :], hot_cols, start=True, stop=True)\
              .then_inc(rt_cnt, 1)
            job(NT + 3, 1, WE, WE, free=(y_gb, NT + 1))
            with pe.Fori(NT // 2 + 2, NT) as j:
                for k in range(2):
                    job(j * 2 + k, k, WE, WE, free=(y_gb, j * 2 + (k - 2)))

            pe.wait_ge(tab_ok, 1)

            def read(row, r, most):
                return pe.value_load(tab[0:1, row, bass.ds(r, 1)], min_val=0, max_val=most)

            def routed(j, first, last):
                for k in range(2):
                    r = j * 2 + k
                    n = r + 2 * NT
                    if k == 1:
                        was = par
                    par = read(0, r, 1)
                    if first and k == 0:
                        free, prev_ofs = (y_gb, n - 2), WE
                    else:
                        prev_ofs = (was if k == 1 else read(0, r - 1, 1)) * WE
                        if first:
                            free = (y_gb, 2 * NT - 1)
                        elif k == 0 and isinstance(j, int) and j == 1:
                            free = (y_gb, 2 * NT)
                        else:
                            free = (y_ev, r - 2)
                    pe.wait_ge(w_ready, r + 1)
                    job(n, k, par * WE, prev_ofs, nxt=not (last and k == 1), free=free)

            routed(0, True, False)
            routed(1, False, False)
            with pe.Fori(2, NSLOT // 2 - 1) as j:
                routed(j, False, False)
            routed(NSLOT // 2 - 1, False, True)
            turn_mid(NJ - 1, 1)
            down(NJ - 1, 1, read(0, NSLOT - 1, 1) * WE, (y_ev, NSLOT - 2))

        @block.vector
        def _(dve):

            dc = [0]

            def link(ins):
                dc[0] += 1
                ins.then_inc(dchain, 1)
                dve.wait_ge(dchain, dc[0])

            def mod_piece(m):
                dst = mod_row[:, m % 2, :]
                if m >= 2:
                    dve.wait_ge(mod_st[m % 2], 16 * (m // 2))
                dve.wait_ge(mod_full, m + 1)
                src = bank[6][0:B, :]
                if m in (1, 4):
                    dve.tensor_scalar(dst, src, 1.0, None, ALU.add).then_inc(mod_ev, 1)
                elif m in (0, 3):
                    dve.tensor_copy(dst, src).then_inc(mod_ev, 1)
                else:
                    link(dve.tensor_scalar(mod_a[:, :], src, -1.0, None, ALU.mult))
                    link(dve.tensor_tensor(mod_a[:, :], mod_a[:, :], src, ALU.max))
                    link(dve.tensor_scalar(mod_a[:, :], mod_a[:, :], 0.25, None, ALU.max))
                    link(dve.tensor_scalar(mod_s[:, :], src, 0.0, 2.0, ALU.is_ge, ALU.mult))
                    dve.scalar_tensor_tensor(out=dst, in0=mod_s[:, :], scalar=-1.0, in1=mod_a[:, :],
                                             op0=ALU.add, op1=ALU.mult).then_inc(mod_ev, 1)

            def norm_stats(b, base):
                wait_apart(dve, (x_ld, b * 16 + 16))
                k = [0]

                def chain(ins):
                    k[0] += 1
                    ins.then_inc(ln_chain, 1)
                    wait_apart(dve, (ln_chain, base + k[0]))

                for i in range(TT):
                    ins = dve.bn_stats(stat[:, i, :], x_in[:, i, :])
                chain(ins)
                for i in range(TT):
                    ins = dve.bn_aggr(mv[:, i, :], stat[:, i, :])
                chain(ins)
                dve.tensor_scalar(ve[:, :], mv[:, :, 1], EPS, None, ALU.add).then_inc(ln_var, 1)
                dve.wait_ge(ln_seed, b + 1)
                chain(dve.tensor_tensor(nt1[:, :], rs0[:, :], rs0[:, :], ALU.mult))
                chain(dve.tensor_tensor(nt2[:, :], nt1[:, :], ve[:, :], ALU.mult))
                chain(dve.tensor_scalar(nt1[:, :], nt2[:, :], -0.5, 1.5, ALU.mult, ALU.add))
                chain(dve.tensor_tensor(rstd[:, :], nt1[:, :], rs0[:, :], ALU.mult))
                for i in range(TT):
                    dve.tensor_scalar(x_in[:, i, :], x_in[:, i, :], mv[:, i, 0:1], rstd[:, i:i + 1],
                                      ALU.subtract, ALU.mult).then_inc(xn_ok, 1)

            LN_CHAIN = 6

            def modulate(b, i, first):
                dve.wait_ge(tx_full, b * TT + (i + 1))
                if not (first and i < 2):
                    dve.wait_ge(hlo_ok, b * TT + (i - 1))
                for c in range(DC):
                    ins = dve.tensor_scalar(h_full[:, i % 2, c, :], bank[4 + i % 2][:, c * P:(c + 1) * P],
                                            modc[:, 1, c, bass.ds(b, 1)], modc[:, 0, c, bass.ds(b, 1)],
                                            ALU.mult, ALU.add)
                ins.then_inc(hf_ok, 1)

            def h_low(b, i):
                dve.wait_ge(hhi_ok, b * TT + (i + 1))
                to = (slice(None), bass.ds(b * DC, DC), slice(i * P, (i + 1) * P))
                dve.tensor_tensor(h_lo[to], h_full[:, i % 2], h_hi[to].bitcast(F32), ALU.subtract)\
                    .then_inc(hlo_ok, 1)

            def wq_low(g):
                i = load_at["wq", g]
                dve.wait_ge(wq_hi_ok, g + 1)
                dve.tensor_tensor(wq_lo[:, :, g * D:(g + 1) * D], stage[i % 3],
                                  wq_hi[:, :, g * D:(g + 1) * D].bitcast(F32), ALU.subtract).then_inc(wq_ok, 1)

            norm_stats(0, 0)
            mod_piece(0)
            dve.wait_ge(const_ld, 5 * 16)
            mod_piece(1)
            wq_low(0)
            dve.wait_ge(modt_full, 1)
            dve.tensor_copy(modc[:, :, :, :].rearrange("p m c b -> p (m c b)"), bank[7][:, 0:2 * DC * B])\
                .then_inc(modc_ok, 1)
            dve.wait_ge(modc_ok, 1)
            for i in range(TT):
                modulate(0, i, True)
                if i:
                    h_low(0, i - 1)
            h_low(0, TT - 1)
            for g in range(1, 4):
                wq_low(g)

            def batch(b, first=False):
                norm_stats(b, b * LN_CHAIN)
                for i in range(TT):
                    modulate(b, i, False)
                    if i:
                        h_low(b, i - 1)
                h_low(b, TT - 1)

            with dve.Fori(1, B) as b:
                batch(b)
            for m in range(2, 6):
                mod_piece(m)

            stage1_over(dve)

            def low(dst, src, hi, bias, done):
                if bias is None:
                    dve.tensor_tensor(dst, src, hi.bitcast(F32), ALU.subtract).then_inc(done, 1)
                else:
                    dve.scalar_tensor_tensor(out=dst, in0=src, scalar=bias, in1=hi.bitcast(F32),
                                             op0=ALU.add, op1=ALU.subtract).then_inc(done, 1)

            def k_part(p, n, h):
                dve.wait_ge(k_hi_ok, n * 2 + (h + 1))
                low(k_lo[:, h, :], bank[h][:, :], k_hi[:, h, :], bk_c[:, bass.ds(p * 2 + h, 1)], k_ok)

            dve.wait_ge(wv_ld, 16)
            dve.tensor_copy(wv_hi[:, :, :], wv_raw[:, :, :]).then_inc(wv_hi_ok, 1)
            dve.wait_ge(wv_hi_ok, 1)
            dve.tensor_tensor(wv_lo[:, :, :], wv_raw[:, :, :], wv_hi[:, :, :].bitcast(F32), ALU.subtract)\
               .then_inc(wv_ok, 1)
            k_part(0, 0, 0)
            k_part(0, 0, 1)

            def step(p, b, first, last):
                n = p * B + b

                def maxima(i):
                    h, rows = i // 3, S_PARTS[i % 3]
                    dve.wait_ge(s_full, n * 6 + (i + 1))
                    if len(rows) == 2:
                        diag = bank[2 + i % 2][:, 0:3 * P].rearrange("p (k n) -> p k n", k=3)[:, 0:3:2, :]
                        mask = causal[:, :].unsqueeze(1).to_broadcast([P, 2, P])
                    else:
                        diag = bank[2 + i % 2][:, rows[0] * P:(rows[0] + 1) * P]
                        mask = causal[:, :]
                    dve.tensor_tensor(diag, diag, mask, ALU.add).then_inc(s_mask, 1)
                    dve.wait_ge(s_mask, n * 6 + (i + 1))
                    for r in rows:
                        at = ROW_AT[r] - ROW_AT[rows[0]]
                        ins = dve.tensor_reduce(row_max[:, h, r:r + 1], bank[2 + i % 2][:, at:at + (r + 1) * P],
                                                AX_X, ALU.max)
                    ins.then_inc(s_max, 1)
                    dve.wait_ge(s_max, n * 6 + (i + 1))
                    cols = slice(rows[0], rows[-1] + 1)
                    dve.tensor_scalar(neg_max[:, h, cols], row_max[:, h, cols], -SCALE, None,
                                      ALU.mult).then_inc(s_neg, 1)

                def normalise(i):
                    h, rows = i // 3, S_PARTS[i % 3]
                    dve.wait_ge(s_exp, n * 6 + (i + 1))
                    cols = slice(rows[0], rows[-1] + 1)
                    dve.reciprocal(row_inv[:, h, cols], row_sum[:, h, cols]).then_inc(inv_ok, 1)
                    wait_apart(dve, (inv_ok, n * 6 + (i + 1)))
                    for r in rows:
                        part = prob[:, h, ROW_AT[r]:ROW_AT[r] + (r + 1) * P]
                        ins = dve.tensor_scalar(part, part, row_inv[:, h, r:r + 1], None, ALU.mult)
                    ins.then_inc(p_ok, 1)

                def v_part(g):
                    dve.wait_ge(v_hi_ok, n * 2 + (g + 1))
                    low(v_lo[:, 2 * g:2 * g + 2, :], bank[g][:, :].rearrange("p (i n) -> p i n", i=2),
                        v_hi[:, 2 * g:2 * g + 2, :], None, v_ok)

                def pt_part(h, g):
                    dve.wait_ge(pt_hi_ok, n * 6 + (3 * h + g + 1))
                    cols = slice(PT_AT[g], PT_AT[g] + PT_LEN[g])
                    low(pt_lo[:, cols], bank[4 + g % 2][:, 0:PT_LEN[g]], pt_hi[:, cols], None, pt_ok)

                def o_part(h):
                    dve.wait_ge(o_hi_ok, n * 2 + (h + 1))
                    low(o_lo[:, h, :], bank[6 + h][:, :], o_hi[:, h, :], bv_c[:, bass.ds(p * 2 + h, 1)], o_ok)

                def add(i):
                    if not first:
                        add_out(n - 1, (b - 1) % B, i)

                norm2 = isinstance(p, int) and p == HP - 1 and b == 2
                pn = p if b < B - 1 else p + 1
                if first:
                    v_part(0)
                    v_part(1)
                maxima(0)
                maxima(1)
                add(0)
                add(1)
                maxima(2)
                normalise(0)
                add(2)
                maxima(3)
                normalise(1)
                add(3)
                normalise(2)
                maxima(4)
                normalise(3)
                if not first:
                    v_part(0)
                maxima(5)
                normalise(4)
                if not first:
                    v_part(1)
                pt_part(0, 0)
                pt_part(0, 1)
                normalise(5)
                if norm2:
                    for t in range(TT):
                        c_stats(b - 2, t)
                    c_moments(b - 2)
                if not last:
                    k_part(pn, n + 1, 0)
                pt_part(0, 2)
                if norm2:
                    c_rstd(b - 2)
                    c_rows(b - 2, 0)
                o_part(0)
                pt_part(1, 0)
                pt_part(1, 1)
                if norm2:
                    c_rows(b - 2, 1)
                pt_part(1, 2)
                if norm2:
                    c_rows(b - 2, 2)
                o_part(1)
                if not last:
                    k_part(pn, n + 1, 1)
                if norm2:
                    c_rows(b - 2, 3)
                if first:
                    dve.wait_ge(acc_ok, B)

            def add_out(m, b, i):
                dve.wait_ge(wo_full, m * TT + (i + 1))
                t = b * TT + i
                dve.tensor_tensor(acc[:, t, :], acc[:, t, :], bank[i % 2][:, :], ALU.add).then_inc(wo_add, 1)

            def c_stats(b, t):
                dve.wait_ge(x1_ok, b + 1)
                dve.bn_stats(stat[:, t, :], acc[:, b * TT + t, :]).then_inc(c_stat, 1)

            def c_moments(b):
                dve.wait_ge(c_stat, b * TT + TT)
                for t in range(TT):
                    ins = dve.bn_aggr(mv[:, t, :], stat[:, t, :])
                ins.then_inc(c_chain, 1)
                dve.wait_ge(c_chain, b * C_CHAIN + 1)
                dve.tensor_scalar(ve[:, :], mv[:, :, 1], EPS, None, ALU.add).then_inc(c_var, 1)

            def c_rstd(b):
                dve.wait_ge(c_seed, b + 1)
                dve.tensor_tensor(nt1[:, :], rs0[:, :], rs0[:, :], ALU.mult).then_inc(c_chain, 1)
                dve.wait_ge(c_chain, b * C_CHAIN + 2)
                dve.tensor_tensor(nt2[:, :], nt1[:, :], ve[:, :], ALU.mult).then_inc(c_chain, 1)
                dve.wait_ge(c_chain, b * C_CHAIN + 3)
                dve.tensor_scalar(nt1[:, :], nt2[:, :], -0.5, 1.5, ALU.mult, ALU.add).then_inc(c_chain, 1)
                dve.wait_ge(c_chain, b * C_CHAIN + 4)
                dve.tensor_tensor(rstd[:, :], nt1[:, :], rs0[:, :], ALU.mult).then_inc(c_chain, 1)
                dve.wait_ge(c_chain, b * C_CHAIN + 5)
                if b:
                    dve.wait_ge(h2_st, b * 16)

            def c_rows(b, t):
                dve.scalar_tensor_tensor(out=h2[:, t, :], in0=acc[:, b * TT + t, :], scalar=mv[:, t, 0:1],
                                         in1=mods[:, b, 2, :], op0=ALU.subtract, op1=ALU.mult).then_inc(c_xn, 1)
                dve.wait_ge(c_xn, b * TT + (t + 1))
                dve.scalar_tensor_tensor(out=h2[:, t, :], in0=h2[:, t, :], scalar=rstd[:, t:t + 1],
                                         in1=mods[:, b, 1, :], op0=ALU.mult, op1=ALU.add).then_inc(h2_ok, 1)

            C_CHAIN = 5
            walk_steps(dve, step)
            for i in range(TT):
                add_out(NIT - 1, B - 1, i)

            dve.wait_ge(wo_add, NIT * TT)
            dve.wait_ge(c3_ld, 16 * 3)
            dve.tensor_copy(g_hi[:, :, :], g_raw[:, :, :]).then_inc(g_hi_ok, 1)
            dve.wait_ge(g_hi_ok, 1)
            dve.tensor_tensor(g_lo[:, :, :], g_raw[:, :, :], g_hi[:, :, :].bitcast(F32), ALU.subtract)\
                .then_inc(g_ok, 1)

            def xt_part(n, s):
                dve.wait_ge(xt_hi_ok, n + 1)
                low(xt_lo[:, s], bank[2][:, :].rearrange("p (c n) -> p c n", c=DC), xt_hi[:, s], None, xt_ok)

            def ht_part(m):
                dve.wait_ge(ht_hi_ok, m + 1)
                for f in range(FC):
                    ins = dve.tensor_tensor(ht_lo[0:FK[f], f, :], bank[3][0:FK[f], f * P:(f + 1) * P],
                                            ht_hi[0:FK[f], f, :].bitcast(F32), ALU.subtract)
                ins.then_inc(ht_ok, 1)

            def gb_row(b):
                return mods[:, bass.ds(b, 1), 3, :]

            def y_part(m, s, b):
                dve.wait_ge(y_full, m + 1)
                if not (isinstance(m, int) and m < 2):
                    dve.wait_ge(y_add, m - 1)
                dve.tensor_tensor(y_sb[:, s, :].unsqueeze(1), bank[4 + s][:, :].unsqueeze(1),
                                  gb_row(b), ALU.mult).then_inc(y_gb, 1)

            def job(n, s, prev, nxt, b_prev=None, route=False, between=None):
                if prev:
                    ht_part(n - 1)
                dve.wait_ge(up_full, n + 1)
                dve.wait_ge(silu_ok, n + 1)
                if not (isinstance(n, int) and n < 2):
                    dve.wait_ge(ht_full, n - 1)
                dve.tensor_tensor(h_mid[:, s, :], gate_s[:, s, :], bank[1][:, 0:F], ALU.mult).then_inc(mid_ok, 1)
                if between:
                    between()
                if nxt:
                    xt_part(n + 1, 1 - s)
                if route:
                    dve.wait_ge(lg_full, n + 1)
                    dve.tensor_copy(lg[:, bass.ds(n, 1), :], bank[6][:, 0:E].unsqueeze(1)).then_inc(lg_ok, 1)
                if prev == "shared":
                    y_part(n - 1, 1 - s, b_prev)

            for t in range(TT):
                c_stats(1, t)
            xt_part(0, 0)
            c_moments(1)
            c_rstd(1)
            for t in range(TT):
                c_rows(1, t)

            def quad0(b, hidden, first):
                for i in range(TT):
                    n = b * TT + i
                    job(n, i % 2, None if first and i == 0 else "shared", True,
                        b_prev=b if i else b - 1, route=True)
                    if hidden and i == 0:
                        for t in range(TT):
                            c_stats(b + 2, t)
                    if hidden and i == 1:
                        c_moments(b + 2)
                    if hidden and i == 2:
                        c_rstd(b + 2)
                        c_rows(b + 2, 0)
                        c_rows(b + 2, 1)
                    if hidden and i == 3:
                        c_rows(b + 2, 2)
                        c_rows(b + 2, 3)

            quad0(0, True, True)
            quad0(1, True, False)
            with dve.Fori(2, B) as b:
                quad0(b, False, False)

            def bt(a):
                return a.unsqueeze(2).to_broadcast([P, NT, E])

            iota_e = cf("iota", NT * E, "p (t e) -> p t e", dict(e=E))

            def highest(scores_, top):
                link(dve.tensor_reduce(top, scores_, AX_X, ALU.max))
                link(dve.tensor_tensor(ra[:, :, :], scores_, bt(top), ALU.is_equal))
                link(dve.tensor_tensor(ra[:, :, :], ra[:, :, :], iota_e, ALU.mult))

            def lowest_of(hot_):
                link(dve.tensor_reduce(r1[:, 1, :], ra[:, :, :], AX_X, ALU.min))
                link(dve.tensor_tensor(hot_, iota_e, bt(r1[:, 1, :]), ALU.is_equal))

            def less_max():
                dve.wait_ge(lg_ok, NT)
                link(dve.tensor_reduce(r1[:, 0, :], lg[:, :, :], AX_X, ALU.max))
                dve.tensor_tensor(ra[:, :, :], lg[:, :, :], bt(r1[:, 0, :]), ALU.subtract).then_inc(rt_sub, 1)

            def softmax():
                dve.wait_ge(rt_exp, 1)
                link(dve.tensor_reduce(r1[:, 0, :], sc[:, :, :], AX_X, ALU.add))
                link(dve.reciprocal(r1[:, 2, :], r1[:, 0, :]))
                link(dve.tensor_tensor(sc[:, :, :], sc[:, :, :], bt(r1[:, 2, :]), ALU.mult))

            def first_expert():
                highest(sc[:, :, :], r1[:, 3, :])
                lowest_of(oh1[:, :, :])

            def others():
                link(dve.scalar_tensor_tensor(out=rb[:, :, :], in0=oh1[:, :, :], scalar=-4.0,
                                              in1=sc[:, :, :], op0=ALU.mult, op1=ALU.add))
                link(dve.tensor_reduce(r1[:, 4, :], rb[:, :, :], AX_X, ALU.max))

            def second_expert():
                link(dve.tensor_tensor(ra[:, :, :], rb[:, :, :], bt(r1[:, 4, :]), ALU.is_equal))
                link(dve.tensor_tensor(ra[:, :, :], ra[:, :, :], iota_e, ALU.mult))
                lowest_of(oh2[:, :, :])
                dve.tensor_tensor(hot[:, :, :], oh1[:, :, :], oh2[:, :, :], ALU.add).then_inc(rt_hot, 1)

            def weights():
                link(dve.tensor_tensor(r1[:, 5, :], r1[:, 3, :], r1[:, 4, :], ALU.add))
                link(dve.tensor_scalar(r1[:, 5, :], r1[:, 5, :], 1e-20, None, ALU.add))
                link(dve.reciprocal(r1[:, 6, :], r1[:, 5, :]))
                for c in range(2):
                    link(dve.tensor_tensor(top_w[:, c, :], r1[:, 3 + c, :], r1[:, 6, :], ALU.mult))

            before = bank[7][:, 0:NT * E].rearrange("p (t e) -> p t e", e=E)
            count = bank[7][:, NT * E:2 * NT * E].rearrange("p (t e) -> p e t", e=E)

            def totals():
                dve.wait_ge(rt_cnt, 1)
                link(dve.tensor_copy(cnt_et[:, :, :], count))
                flat = "p e t -> p (e t)"
                link(dve.tensor_tensor_scan(cum_et[:, :, :].rearrange(flat), cf("keep", NT * E),
                                            cnt_et[:, :, :].rearrange(flat), 0.0, ALU.mult, ALU.add))

            def tiles_of():
                total = cum_et[:, :, NT - 1:NT]
                link(dve.tensor_tensor(over[:, :, :], total.to_broadcast([P, E, NT]),
                                       cf("edges", NT * E, "p (e t) -> p e t", dict(t=NT)), ALU.is_gt))
                link(dve.tensor_reduce(e1[:, 0, :], over[:, :, :], AX_X, ALU.add))
                link(dve.tensor_scalar(e1[:, 1, :], e1[:, 0, :], 1.0, None, ALU.max))

            def first_tiles():
                link(dve.tensor_tensor_scan(e1[:, 2, :], cf("one_e", E), e1[:, 1, :], 0.0, ALU.mult, ALU.add))
                link(dve.tensor_tensor(e1[:, 3, :], e1[:, 2, :], e1[:, 1, :], ALU.subtract))
                link(dve.tensor_tensor(cum_et[:, :, :], cum_et[:, :, :], cnt_et[:, :, :], ALU.subtract))

            def slots_of():
                link(dve.scalar_tensor_tensor(
                    out=over[:, :, :], in0=e1[:, 3, :].unsqueeze(2).to_broadcast([P, E, NT]), scalar=float(P),
                    in1=cum_et[:, :, :], op0=ALU.mult, op1=ALU.add))
                link(dve.tensor_tensor(slot_base[:, :, :], before, over[:, :, :].rearrange("p e t -> p t e"),
                                       ALU.add))

            def position(c):
                link(dve.tensor_tensor(ra[:, :, :], slot_base[:, :, :], (oh1, oh2)[c][:, :, :], ALU.mult))
                link(dve.tensor_reduce(r1[:, 7, :], ra[:, :, :], AX_X, ALU.add))
                link(dve.tensor_copy(pos_i[:, c, :], r1[:, 7, :]))
                dve.tensor_scalar(pos_r[:, c, :], r1[:, 7, :], float(N), None, ALU.add).then_inc(pos_ok, 1)
                dve.wait_ge(pos_ok, c + 1)

            def begun():
                tiles = cf("tiles", NSLOT * E, "p (j e) -> p j e", dict(e=E))
                first_ = e1[:, 3, :].unsqueeze(1).to_broadcast([P, NSLOT, E])
                link(dve.tensor_tensor(j_le[:, :, :], first_, tiles, ALU.is_le))
                link(dve.tensor_tensor(j_eq[:, :, :], first_, tiles, ALU.is_equal))

            def table(row):
                src, name = ((j_le, "parity"), (j_le, "even"), (j_le, "odd"),
                             (j_le, "next"), (j_eq, "load_0"), (j_eq, "load_1"))[row]
                weight = cf(name, E).unsqueeze(1).to_broadcast([P, NSLOT, E])
                link(dve.tensor_tensor(j_t[:, :, :], src[:, :, :], weight, ALU.mult))
                link(dve.tensor_reduce(j_f[:, row, :], j_t[:, :, :], AX_X, ALU.add))

            def tables_done():
                dve.tensor_copy(tab[:, :, :], j_f[:, :, :]).then_inc(tab_ok, 1)

            job(NT, 0, "shared", True, b_prev=B - 1, between=less_max)
            softmax()
            job(NT + 1, 1, "shared", True, b_prev=0, between=first_expert)
            others()
            second_expert()
            job(NT + 2, 0, "shared", True, b_prev=0)
            weights()
            job(NT + 3, 1, "shared", True, b_prev=0, between=totals)
            tiles_of()
            first_tiles()
            job(NT + 4, 0, "shared", True, b_prev=0, between=slots_of)
            position(0)
            job(NT + 5, 1, "shared", True, b_prev=1, between=lambda: position(1))
            begun()
            for k in range(6):
                job(NT + 6 + k, k % 2, "shared", True, b_prev=(5 + k) // TT)
                table(k)
            tables_done()
            for n in range(2 * NT - 4, 2 * NT):
                job(n, n % 2, "shared", True, b_prev=(n - 1 - NT) // TT)
            job(2 * NT, 0, "shared", True, b_prev=B - 1)
            job(2 * NT + 1, 1, "routed", True)
            with dve.Fori(NT + 1, NJ // 2 - 1) as j:
                for k in range(2):
                    job(j * 2 + k, k, "routed", True)
            job(NJ - 2, 0, "routed", True)
            job(NJ - 1, 1, "routed", False)
            ht_part(NJ - 1)

            for t in range(NT):
                a = rows_1[:, t, :]
                dve.wait_ge(f_w1, t + 1)
                dve.scalar_tensor_tensor(out=a, in0=a, scalar=top_w[:, 1, t:t + 1],
                                         in1=rows_0[:, t, :], op0=ALU.mult, op1=ALU.add).then_inc(f_w2, 1)
                dve.wait_ge(f_w2, t + 1)
                dve.tensor_tensor(a, a, mods[:, t // TT, 3, :], ALU.mult).then_inc(f_gb, 1)
                dve.wait_ge(f_gb, t + 1)
                dve.tensor_tensor(a, a, acc[:, t, :], ALU.add).then_inc(f_ok, 1)


def _experts(w_gate, w_up, w_down, sw_gate, sw_up, sw_down):
    out = np.zeros((P, NX, WE), w_gate.dtype)
    for e in range(NX):
        if e < E:
            g, u, d = w_gate[e], w_up[e], w_down[e]
        else:
            part = slice((e - E) * F, (e - E + 1) * F)
            g, u, d = sw_gate[part], sw_up[part], sw_down[:, part]
        for at, w in ((WG, g), (WU, u)):
            out[:, e, at:at + DC * F] = w.T.reshape(DC, P, F).transpose(1, 0, 2).reshape(P, DC * F)
        rows = np.zeros((FC * P, D), d.dtype)
        rows[:F] = d.T
        out[:, e, WD:] = rows.reshape(FC, P, D).transpose(1, 0, 2).reshape(P, FC * D)
    return out.reshape(P, NX * WE)


def kernel(**inputs):
    import concourse.bacc as _bacc
    from concourse.bass_utils import run_bass_kernel_spmd as _run

    a = {k.replace("L0_", ""): np.asarray(v) for k, v in inputs.items()}
    by_head = [np.ascontiguousarray(a[f"attn_b{i}"].reshape(H, P).T) for i in "qkv"]
    arrays = {
        "x": a["attn_x"].reshape(N, D),
        "wq": a["attn_Wq"], "bq": by_head[0],
        "wk": a["attn_Wk"], "bk": by_head[1],
        "wv": a["attn_Wv"], "bv": by_head[2],
        "wo": a["attn_Wo"], "bo": a["attn_bo"].reshape(1, D),
        "gate_t": a["ffn_gate_weight"].T,
        "wexp": _experts(*(a[f"ffn_{n}"] for n in ("w_gate", "w_up", "w_down", "sw_gate", "sw_up", "sw_down"))),
        "c_t": a["c"].T, "wmod": a["wmod"],
        "ident_in": np.eye(P, dtype=np.float32),
        "causal_in": np.triu(np.full((P, P), MASKED, np.float32), 1),
        "tri_in": np.triu(np.ones((P, P), np.float32), 1),
        "coef_in": coefficients(),
    }
    arrays = {k: np.ascontiguousarray(v) for k, v in arrays.items()}
    nc = _bacc.Bacc("TRN2", target_bir_lowering=False, num_devices=1)
    args = {k: nc.dram_tensor(k, v.shape, mybir.dt.from_np(v.dtype), kind="ExternalInput").ap()
            for k, v in arrays.items()}
    out = nc.dram_tensor("out", (N, D), F32, kind="ExternalOutput").ap()
    adaln_layer(nc, out=out, **args)
    r = _run(nc, [arrays], core_ids=[0])
    return r.results[0]["out"].reshape(B, T, D)
```
